# Optimizing a Trainium2 kernel written in Bass

```python
import numpy as np
import jax
import jax.numpy as jnp

def _softmax(x, axis=-1):
    return jax.nn.softmax(x, axis=axis)

def _gelu(x):
    return jax.nn.gelu(x, approximate=True)

def _silu(x):
    return jax.nn.silu(x)

def _sigmoid(x):
    return jax.nn.sigmoid(x)

def _layernorm(x, axis=-1, eps=1e-05):
    m = jnp.mean(x, axis=axis, keepdims=True)
    v = jnp.var(x, axis=axis, keepdims=True)
    return (x - m) / jnp.sqrt(v + eps)

def _scatter_add(tgt, idx, src, axis=0):
    return tgt.at[idx].add(src)

def _segment_sum(src, seg, n):
    return jax.ops.segment_sum(src, seg, n)
kernel_name = 'mk_adaln_d1_jaxref_r4_516c7d'

def setup_inputs(seed: int=0):
    np.random.seed(seed)
    _w = jnp.asarray

    def _L0_attn_setup():
        import jax, jax.numpy as jnp
        import numpy as np
        key = jax.random.key(seed)
        ks = jax.random.split(key, 5)
        B, S, D = (1, 1024, 512)
        H, Dh = (16, 128)
        scale = 1.0 / np.sqrt(D).astype(np.float32)
        return {'x': jax.random.normal(ks[0], (B, S, D), dtype=jnp.float32), 'W_K': jax.random.normal(ks[1], (H, Dh, D), dtype=jnp.float32) * scale, 'W_Q': jax.random.normal(ks[2], (H, Dh, D), dtype=jnp.float32) * scale, 'W_V': jax.random.normal(ks[3], (H, Dh, D), dtype=jnp.float32) * scale, 'W_O': jax.random.normal(ks[4], (D, H * Dh), dtype=jnp.float32) * scale}
    _L0_attn_in = _L0_attn_setup()

    def _L0_ffn_setup():
        import jax, jax.numpy as jnp
        import numpy as np
        B, S, D = (4, 512, 512)
        E = 8
        N_SHARE = 2
        N_ROUTED = E - N_SHARE
        H = 2048 // E
        key = jax.random.key(seed)
        ks = jax.random.split(key, 12)
        s = 0.02
        return {'x': jax.random.normal(ks[0], (B, S, D), jnp.float32), 'Wg': jax.random.normal(ks[1], (D, E), jnp.float32) * s, 'bg': jnp.zeros((E,), jnp.float32), 'Wgate': jax.random.normal(ks[2], (N_ROUTED, D, H), jnp.float32) * s, 'bgate': jnp.zeros((N_ROUTED, H), jnp.float32), 'Wup': jax.random.normal(ks[3], (N_ROUTED, D, H), jnp.float32) * s, 'bup': jnp.zeros((N_ROUTED, H), jnp.float32), 'Wdown': jax.random.normal(ks[4], (N_ROUTED, H, D), jnp.float32) * s, 'bdown': jnp.zeros((N_ROUTED, D), jnp.float32), 'Ws_up': jax.random.normal(ks[5], (D, N_SHARE * H), jnp.float32) * s, 'bs_up': jnp.zeros((N_SHARE * H,), jnp.float32), 'Ws_down': jax.random.normal(ks[6], (N_SHARE * H, D), jnp.float32) * s, 'bs_down': jnp.zeros((D,), jnp.float32)}
    _L0_ffn_in = _L0_ffn_setup()
    _L0_c = _w((lambda *s: np.random.randn(*s).astype(np.float32) * 0.05)(2, 512))
    _L0_wmod = _w((lambda *s: np.random.randn(*s).astype(np.float32) * 0.05)(512, 6 * 512) * 512 ** (-0.5))
    _d = {'L0_attn_x': _L0_attn_in['x'], 'L0_attn_W_K': _L0_attn_in['W_K'], 'L0_attn_W_Q': _L0_attn_in['W_Q'], 'L0_attn_W_V': _L0_attn_in['W_V'], 'L0_attn_W_O': _L0_attn_in['W_O'], 'L0_ffn_Wg': _L0_ffn_in['Wg'], 'L0_ffn_bg': _L0_ffn_in['bg'], 'L0_ffn_Wgate': _L0_ffn_in['Wgate'], 'L0_ffn_bgate': _L0_ffn_in['bgate'], 'L0_ffn_Wup': _L0_ffn_in['Wup'], 'L0_ffn_bup': _L0_ffn_in['bup'], 'L0_ffn_Wdown': _L0_ffn_in['Wdown'], 'L0_ffn_bdown': _L0_ffn_in['bdown'], 'L0_ffn_Ws_up': _L0_ffn_in['Ws_up'], 'L0_ffn_bs_up': _L0_ffn_in['bs_up'], 'L0_ffn_Ws_down': _L0_ffn_in['Ws_down'], 'L0_ffn_bs_down': _L0_ffn_in['bs_down'], 'L0_c': _L0_c, 'L0_wmod': _L0_wmod}
    _x0 = _d['L0_attn_x']
    _d['L0_attn_x'] = jax.random.normal(jax.random.fold_in(jax.random.key(seed), 1), (2, 1024, 512), dtype=_x0.dtype)
    del _x0
    return _d

def reference(L0_attn_x, L0_attn_W_K, L0_attn_W_Q, L0_attn_W_V, L0_attn_W_O, L0_ffn_Wg, L0_ffn_bg, L0_ffn_Wgate, L0_ffn_bgate, L0_ffn_Wup, L0_ffn_bup, L0_ffn_Wdown, L0_ffn_bdown, L0_ffn_Ws_up, L0_ffn_bs_up, L0_ffn_Ws_down, L0_ffn_bs_down, L0_c, L0_wmod):

    def _L0_attn_ref(x, W_K, W_Q, W_V, W_O):
        import jax, jax.numpy as jnp
        import numpy as np
        b, pos, d_model = x.shape
        d_head = W_K.shape[1]
        k = jnp.einsum('ihd,bpd->biph', W_K, x)
        q = jnp.einsum('ihd,bpd->biph', W_Q, x)
        v = jnp.einsum('ihd,bpd->biph', W_V, x)
        scores = jnp.einsum('biph,biqh->biqp', k, q)
        mask = jnp.tril(jnp.ones((pos, pos), dtype=x.dtype))
        masked = scores * mask - jnp.float32(10000000000.0) * (1.0 - mask)
        attn = jax.nn.softmax(masked / jnp.sqrt(jnp.float32(d_head)), axis=-1)
        z = jnp.einsum('biqp,biph->biqh', attn, v)
        z_flat = jnp.transpose(z, (0, 2, 1, 3)).reshape(b, pos, -1)
        out = jnp.einsum('df,bqf->bqd', W_O, z_flat)
        return out

    def _L0_ffn_ref(x, Wg, bg, Wgate, bgate, Wup, bup, Wdown, bdown, Ws_up, bs_up, Ws_down, bs_down):
        import jax, jax.numpy as jnp
        import numpy as np
        B, S, D = (4, 512, 512)
        E = 8
        N_SHARE = 2
        N_ROUTED = E - N_SHARE
        H = 2048 // E
        b, s, d = x.shape
        T = b * s
        n = Wgate.shape[0]
        xf = x.reshape(T, d)
        gate = xf @ Wg + bg
        vals, ids = jax.lax.top_k(gate, n)
        rows = jnp.arange(T)[:, None]
        masked = jnp.full_like(gate, -jnp.inf).at[rows, ids].set(vals)
        probs = jax.nn.softmax(masked, axis=-1)
        routed_mask = (ids[:, :, None] == jnp.arange(n)).any(axis=1)
        w = probs[:, :n] * routed_mask
        g = jnp.einsum('td,ndh->tnh', xf, Wgate) + bgate
        u = jnp.einsum('td,ndh->tnh', xf, Wup) + bup
        h = jax.nn.silu(g) * u
        eo = jnp.einsum('tnh,nhd->tnd', h, Wdown) + bdown
        routed_out = jnp.einsum('tnd,tn->td', eo, w)
        share = jax.nn.silu(xf @ Ws_up + bs_up) @ Ws_down + bs_down
        return (routed_out + share).reshape(b, s, d)
    x = L0_attn_x
    mod = (_silu(L0_c) @ L0_wmod).reshape(L0_c.shape[0], 6, 1, -1)
    sa, ca, ga, sb, cb, gb = (mod[:, 0], mod[:, 1], mod[:, 2], mod[:, 3], mod[:, 4], mod[:, 5])
    ga = (2 * (ga >= 0) - 1) * jnp.maximum(jnp.abs(ga), 0.25)
    gb = (2 * (gb >= 0) - 1) * jnp.maximum(jnp.abs(gb), 0.25)
    h = _layernorm(x, axis=-1) * (1 + ca) + sa
    x = x + ga * _L0_attn_ref(h, L0_attn_W_K, L0_attn_W_Q, L0_attn_W_V, L0_attn_W_O)
    h = _layernorm(x, axis=-1) * (1 + cb) + sb
    x = x + gb * _L0_ffn_ref(h, L0_ffn_Wg, L0_ffn_bg, L0_ffn_Wgate, L0_ffn_bgate, L0_ffn_Wup, L0_ffn_bup, L0_ffn_Wdown, L0_ffn_bdown, L0_ffn_Ws_up, L0_ffn_bs_up, L0_ffn_Ws_down, L0_ffn_bs_down)
    return x

_drawn_inputs = setup_inputs


def setup_inputs(seed=0):
    import zlib

    import numpy as np

    out = dict(_drawn_inputs(seed))
    spreads = {'L0_ffn_bg': (0.0, 0.8),
     'L0_ffn_bgate': (0.0, 0.8),
     'L0_ffn_bup': (0.0, 0.8),
     'L0_ffn_bdown': (0.0, 0.8),
     'L0_ffn_bs_up': (0.0, 2.0),
     'L0_ffn_bs_down': (0.0, 1.382)}
    factors = {'L0_ffn_Wg': 8.0,
     'L0_ffn_Wgate': 8.0,
     'L0_ffn_Wup': 8.0,
     'L0_ffn_Wdown': 8.0,
     'L0_ffn_Ws_up': 7.893,
     'L0_ffn_Ws_down': 3.669}
    for name, (base, spread) in spreads.items():
        noise = np.random.default_rng([zlib.crc32(name.encode()), seed]).standard_normal(out[name].shape)
        drawn = base * np.exp(spread * noise) if base else spread * noise
        out[name] = jnp.asarray(drawn.astype(out[name].dtype))
    for name, factor in factors.items():
        out[name] = (out[name] * factor).astype(out[name].dtype)
    return out
```

```python
from contextlib import ExitStack

import concourse.bass as bass
from concourse import mybir

F32 = mybir.dt.float32
F32R = mybir.dt.float32r
ACT = mybir.ActivationFunctionType
ALU = mybir.AluOpType
AX = mybir.AxisListType

P = 128
EPS = 1e-5
MASKED = -1e10


def block_kernel(nc, x_in, w_attn, w_mod, c_T, w_router, b_router, w_routed, w_shared_up, w_shared_down,
                 b_shared_up, b_down, out):
    B, S, D = x_in.shape
    H = w_attn.shape[0]
    DC = D // P
    QT = S // P
    NT = B * QT
    W = 512
    NG = S // W
    TG = B * NG
    TPG = W // P
    E = b_router.shape[0]
    NR = w_routed.shape[0]
    NSH = w_shared_down.shape[0]
    NM = NSH + NR
    HC = w_shared_down.shape[2] // D
    HID = HC * P
    SCALE = float(P) ** -0.5
    TOPK = NR

    y_dram = nc.dram_tensor("y_scratch", (B, S, D), F32, kind="Internal").ap()
    x2_dram = nc.dram_tensor("x2_scratch", (B, S, D), F32, kind="Internal").ap()

    def tiles(dram, group):
        b, g = divmod(group, NG)
        return dram[b, g * W:(g + 1) * W, :].rearrange("(t p) d -> p t d", p=P)

    P_GROUPS = [(i, j, min(4, i + 1 - j)) for i in range(QT) for j in range(0, i + 1, 4)]
    NPG = len(P_GROUPS)
    FIRST_PG = [next(k for k, g in enumerate(P_GROUPS) if g[0] == i) for i in range(QT)] + [NPG]

    with ExitStack() as ctx:
        def sb(name, shape, dt, c=ctx):
            return c.enter_context(nc.sbuf_tensor(name, shape, dt))

        def sem(name):
            return ctx.enter_context(nc.semaphore(name))

        ident = sb("ident", [P, P], F32)
        causal = sb("causal", [P, P], F32)
        ones = sb("ones", [P, 1, 1], F32)[:, :, :]
        tril = sb("tril", [P, E, E], F32)
        mod_cols = sb("mod_cols", [P, 4 * DC, B], F32)
        cT = sb("cT", [P, DC, B], F32)
        sc = sb("sc", [P, DC, B], F32)
        sc_wide = sb("sc_wide", [P, DC * B, P], F32)
        NLN = 2 * TG
        st = sb("st", [P, NLN, TPG, 6], F32)
        mv = sb("mv", [P, NLN, TPG, 2], F32)
        sd = sb("sd", [P, NLN, TPG], F32)
        rstd = sb("rstd", [P, NLN, TPG], F32)

        attn = ExitStack()
        hT_hi = sb("hT_hi", [P, DC, S], F32R, attn)
        hT_lo = sb("hT_lo", [P, DC, S], F32R, attn)
        q_hi, q_lo, k_hi, k_lo = [], [], [], []
        for par in range(2):
            if par == 1:
                with ExitStack() as ln:
                    x_sb = sb("x_sb", [P, NG, TPG, D], F32, ln)
            q_hi.append(sb(f"q_hi{par}", [P, S], F32R, attn))
            q_lo.append(sb(f"q_lo{par}", [P, S], F32R, attn))
            k_hi.append(sb(f"k_hi{par}", [P, S], F32R, attn))
            k_lo.append(sb(f"k_lo{par}", [P, S], F32R, attn))
        v_hi = [sb(f"v_hi{par}", [P, QT, P], F32R, attn) for par in range(2)]
        v_lo = [sb(f"v_lo{par}", [P, QT, P], F32R, attn) for par in range(2)]
        vT = sb("vT", [P, NG, W], F32, attn)
        wqkv_raw = sb("wqkv_raw", [P, 2, 3, DC, P], F32, attn)
        wo_raw = sb("wo_raw", [P, 2, D], F32, attn)
        wqkv_hi = sb("wqkv_hi", [P, 3, DC, P], F32R, attn)
        wqkv_lo = sb("wqkv_lo", [P, 3, DC, P], F32R, attn)
        wo_hi = sb("wo_hi", [P, D], F32R, attn)
        wo_lo = sb("wo_lo", [P, D], F32R, attn)
        probs = sb("probs", [P, 2, S], F32, attn)
        z_hi = sb("z_hi", [P, S], F32R, attn)
        z_lo = sb("z_lo", [P, S], F32R, attn)
        acc = sb("acc", [P, QT, D], F32, attn)
        ga_row = sb("ga_row", [P, B, D], F32, attn)
        nmax = sb("nmax", [P, QT], F32, attn)
        rsum = sb("rsum", [P, 2, QT], F32, attn)
        rinv = sb("rinv", [P, 2, QT], F32, attn)
        with ExitStack() as mod:
            wmod = sb("wmod", [P, 3, DC, D], F32, mod)
        pT_hi = [sb(f"pT_hi{g}", [P, 4 * (g + 1), W], F32R, attn) for g in range(NG)]
        pT_lo = [sb(f"pT_lo{g}", [P, 4 * (g + 1), W], F32R, attn) for g in range(NG)]
        attn.close()

        h2_hi = sb("h2_hi", [P, DC, B * S], F32R)
        h2_lo = sb("h2_lo", [P, DC, B * S], F32R)
        F = sb("F", [P, NT, D], F32)
        wmod2 = F[:, 0:3 * DC].rearrange("p (v k) d -> p v k d", k=DC)
        route_tmp = F[:, 2 * TPG:3 * TPG].rearrange("p t d -> p (t d)")
        yb = F[:, 3 * TPG:4 * TPG]
        wf_land = sb("wf_land", [P, 3 * HC * D + 2 * HC], F32)
        wf_raw = wf_land[:, 0:3 * HC * D].rearrange("p (a f) -> p a f", a=3)
        bgu_raw = wf_land[:, 3 * HC * D:].rearrange("p (a c) -> p a c", a=2)
        with ExitStack() as end:
            x2b = sb("x2b", [P, 2, TPG, D], F32, end)
        wf_hi, wf_lo = [], []
        for par in range(2):
            wf_hi.append(sb(f"wf_hi{par}", [P, 3, HC * D], F32R))
            wf_lo.append(sb(f"wf_lo{par}", [P, 3, HC * D], F32R))
        with ExitStack() as ln:
            xb = sb("xb", [P, 2, TPG, D], F32, ln)
        hid_hi = [sb(f"hid_hi{par}", [P, HC, W], F32R) for par in range(2)]
        hid_lo = [sb(f"hid_lo{par}", [P, HC, W], F32R) for par in range(2)]
        hid = sb("hid", [P, HC, W], F32)
        gb_row = sb("gb_row", [P, B, D], F32)
        wr_raw = sb("wr_raw", [P, DC, E], F32)
        wr_hi = sb("wr_hi", [P, DC, E], F32R)
        wr_lo = sb("wr_lo", [P, DC, E], F32R)
        br = sb("br", [E, 1], F32)
        bgu = [sb(f"bgu{par}", [P, 2, HC], F32) for par in range(2)]
        bsu = sb("bsu", [P, NSH, HC], F32)
        gateT = sb("gateT", [E, TG, W], F32)
        wT = gateT
        bd = sb("bd", [1 + NR, D], F32)
        mix = sb("mix", [P, NT, 1 + NR], F32)
        rank = sb("rank", [P, NT, E], F32)
        gs = sb("gs", [P, NT, E], F32)
        sel = sb("sel", [P, NT, E], F32)
        gm = sb("gm", [P, NT], F32)
        gsum = sb("gsum", [P, NT], F32)
        ginv = sb("ginv", [P, NT], F32)

        def ps(name, shape):
            return ctx.enter_context(nc.psum_tensor(name, shape, F32))

        ps_s = [ps(f"ps_s{k}", [P, 2, W]) for k in range(2)]
        ps_t = [ps(f"ps_t{k}", [P, W]) for k in range(2)]
        ps_g = [ps(f"ps_g{k}", [P, W]) for k in range(2)]
        LN_BANKS = [ps_s[k // 2][:, k % 2, :] for k in range(4)]
        PROJ_BANK = [0, 0, 1, 0, 1, 1]
        PV_BANK = [0, 1]
        WO_BANK = [0, 1, 0, 1, 1, 0, 0, 1]
        P_BANK = [0, 1, 0, 1, 0, 1, 0, 1, 1, 0, 0, 1]

        def score_pieces(i):
            return (1, P * (i + 1)) if P * (i + 1) <= W else (2, P * (i + 1) // 2)

        def p_block(pT, i, j, n):
            return pT[i // 4][:, j:j + n, (i % 4) * P:(i % 4 + 1) * P]

        def p_bank(k, n):
            return ps_t[P_BANK[k]][:, 0:n * P].rearrange("p (j q) -> p j q", q=P)

        ps_gu = [[ps_s[c][:, k, :] for k in range(2)] for c in range(2)]
        ps_d = [ps_t[0], ps_t[1], ps_g[0], ps_g[1]]

        const_done = sem("const_done")
        ident_0 = sem("ident_0")
        cT_loaded = sem("cT_loaded")
        wmod_loaded = [sem(f"wmod_loaded{v}") for v in range(6)]
        acc_zeroed = sem("acc_zeroed")
        silu_step = sem("silu_step")
        silu_exp = sem("silu_exp")
        sc_ready = sem("sc_ready")
        mod_done = sem("mod_done")
        mod_read = sem("mod_read")
        gate_step = sem("gate_step")
        x_loaded = [sem(f"x_loaded{g}") for g in range(NG)]
        ln_stat = sem("ln_stat")
        ln_agg = sem("ln_agg")
        ln_var = sem("ln_var")
        ln_sd = sem("ln_sd")
        ln_rstd = sem("ln_rstd")
        xn_ready = sem("xn_ready")
        lnT_done = sem("lnT_done")
        ln_affine = sem("ln_affine")
        ln_hi = sem("ln_hi")
        ln_lo = sem("ln_lo")
        wqkv_loaded = [sem(f"wqkv_loaded{k}") for k in range(2)]
        wo_loaded = [sem(f"wo_loaded{k}") for k in range(2)]
        wqkv_rounded = sem("wqkv_rounded")
        wqkv_split = sem("wqkv_split")
        wo_rounded = sem("wo_rounded")
        wo_split = sem("wo_split")
        proj_done = sem("proj_done")
        qk_hi_done = sem("qk_hi_done")
        qk_lo_done = sem("qk_lo_done")
        vT_copied = sem("vT_copied")
        vtr_done = sem("vtr_done")
        v_hi_done = sem("v_hi_done")
        v_lo_done = sem("v_lo_done")
        score_done = sem("score_done")
        masked = sem("masked")
        rowmax = sem("rowmax")
        exp_done = sem("exp_done")
        pT_done = sem("pT_done")
        p_hi_done = sem("p_hi_done")
        p_lo_done = sem("p_lo_done")
        pv_done = sem("pv_done")
        z_hi_done = sem("z_hi_done")
        z_lo_done = sem("z_lo_done")
        rinv_ready = sem("rinv_ready")
        wo_done = sem("wo_done")
        acc_done = sem("acc_done")
        y_ready = sem("y_ready")
        y_stored = sem("y_stored")
        xb_loaded = [sem(f"xb_loaded{k}") for k in range(2)]
        yb_loaded = sem("yb_loaded")
        small_loaded = sem("small_loaded")
        x2b_loaded = [sem(f"x2b_loaded{k}") for k in range(2)]
        x2_ready = sem("x2_ready")
        x2_stored = sem("x2_stored")
        wr_rounded = sem("wr_rounded")
        wr_split = sem("wr_split")
        wf_loaded = sem("wf_loaded")
        wf_rounded = sem("wf_rounded")
        wf_split = sem("wf_split")
        bgu_ready = sem("bgu_ready")
        router_done = sem("router_done")
        gateT_ready = sem("gateT_ready")
        gateT_back = sem("gateT_back")
        route_step = sem("route_step")
        route_shift = sem("route_shift")
        route_exp = sem("route_exp")
        mix_ready = sem("mix_ready")
        mixT_done = sem("mixT_done")
        mixT_read = sem("mixT_read")
        bias_done = sem("bias_done")
        bias_added = sem("bias_added")
        gate_done = sem("gate_done")
        up_done = sem("up_done")
        silu_done = sem("silu_done")
        hidden_ready = sem("hidden_ready")
        hid_hi_done = sem("hid_hi_done")
        hid_lo_done = sem("hid_lo_done")
        down_done = sem("down_done")
        F_added = sem("F_added")
        F_scaled = sem("F_scaled")
        out_ready = sem("out_ready")
        out_stored = sem("out_stored")

        block = ctx.enter_context(nc.Block())

        UNITS = H
        ATT = B * UNITS

        @block.sync
        def _(sp):
            sp.dma_start(cT[:, :, :], c_T).then_inc(cT_loaded, 16)
            mod_v = w_mod.rearrange("(k p) n -> p k n", p=P)

            def load_mod(v, dst):
                sp.dma_start(dst, mod_v[:, :, v * D:(v + 1) * D]).then_inc(wmod_loaded[v], 16)

            def load_x(b):
                for g in range(NG):
                    sp.dma_start(x_sb[:, g], tiles(x_in, NG * b + g)).then_inc(x_loaded[g], 16)

            def load_qkv(head, par):
                sp.dma_start(wqkv_raw[:, par].rearrange("p k c n -> p (k c n)"),
                             w_attn[bass.ds(head, 1), :, 0:3 * D].rearrange("o p n -> p (o n)")) \
                  .then_inc(wqkv_loaded[par], 16)

            def load_wo(head, par):
                sp.dma_start(wo_raw[:, par], w_attn[bass.ds(head, 1), :, 3 * D:4 * D].rearrange("o p n -> p (o n)")) \
                  .then_inc(wo_loaded[par], 16)

            def stream(U, head_qkv, head_wo, par):
                if head_qkv is not None:
                    sp.wait_ge(wqkv_split, 3 * U + 6)
                    load_qkv(head_qkv, 1 - par)
                if head_wo is not None:
                    sp.wait_ge(wo_split, U + 1)
                    load_wo(head_wo, par)

            for v in range(2):
                load_mod(v, wmod[:, v])
            load_x(0)
            for head in range(2):
                load_qkv(head, head)
                load_wo(head, head)
            load_mod(2, wmod[:, 2])
            sp.wait_ge(wqkv_split, 3)
            load_qkv(2, 0)
            for b in range(B):
                u0 = b * UNITS
                with sp.Fori(0, UNITS // 2 - 2) as it:
                    for par in range(2):
                        stream(u0 + 2 * it + par, 2 * it + par + 3, 2 * it + par + 2, par)
                more = b + 1 < B
                stream(u0 + UNITS - 4, UNITS - 1, UNITS - 2, 0)
                stream(u0 + UNITS - 3, 0 if more else None, UNITS - 1, 1)
                if more:
                    stream(u0 + UNITS - 2, 1, 0, 0)
                    stream(u0 + UNITS - 1, 2, 1, 1)
                    sp.wait_ge(score_done, QT * (u0 + UNITS))
                    load_x(b + 1)
                for g in range(NG):
                    sp.wait_ge(y_ready, QT * b + TPG * (g + 1))
                    sp.dma_start(tiles(y_dram, NG * b + g), acc[:, TPG * g:TPG * (g + 1), :]).then_inc(y_stored, 16)

            sp.wait_ge(y_stored, 16 * TG)
            sp.dma_start(xb[:, 0], tiles(x_in, 0)).then_inc(xb_loaded[0], 16)
            sp.dma_start(yb, tiles(y_dram, 0)).then_inc(yb_loaded, 16)
            load_mod(3, wmod2[:, 0])
            load_mod(4, wmod2[:, 1])
            sp.dma_start(xb[:, 1], tiles(x_in, 1)).then_inc(xb_loaded[1], 16)
            sp.dma_start(wr_raw[:, :, :], w_router).then_inc(small_loaded, 16)
            sp.dma_start(br[:, :], b_router).then_inc(small_loaded, 16)
            sp.dma_start(bsu[:, :, :], b_shared_up).then_inc(small_loaded, 16)
            sp.dma_start(bd[:, :], b_down).then_inc(small_loaded, 16)

            def load_shared(m):
                sp.dma_start(wf_raw[:, 0, :], w_shared_up[m]).then_inc(wf_loaded, 16)
                sp.dma_start(wf_raw[:, 2, :], w_shared_down[m]).then_inc(wf_loaded, 16)

            load_shared(0)
            load_mod(5, wmod2[:, 2])
            for tg in range(TG):
                sp.wait_ge(x2_ready, tg + 1)
                sp.dma_start(tiles(x2_dram, tg), yb).then_inc(x2_stored, 16)
                if tg + 1 < TG:
                    sp.wait_ge(x2_stored, 16 * (tg + 1))
                    sp.wait_ge(xn_ready, TPG * (TG + tg + 1))
                    sp.dma_start(yb, tiles(y_dram, tg + 1)).then_inc(yb_loaded, 16)
                if tg + 2 < TG:
                    sp.wait_ge(lnT_done, DC * (TG + tg + 1))
                    sp.dma_start(xb[:, tg % 2], tiles(x_in, tg + 2)).then_inc(xb_loaded[tg % 2], 16)
            sp.wait_ge(wf_split, 1)
            load_shared(1)
            with sp.Fori(0, NR) as n:
                sp.wait_ge(wf_split, n + NSH)
                sp.dma_start(wf_land[:, :], w_routed[bass.ds(n, 1)].rearrange("o p f -> p (o f)")) \
                  .then_inc(wf_loaded, 32)
            sp.wait_ge(x2_stored, 16 * TG)
            sp.wait_ge(down_done, NT * (NM - 1))
            for tg in range(2):
                sp.dma_start(x2b[:, tg % 2], tiles(x2_dram, tg)).then_inc(x2b_loaded[tg % 2], 16)
            for tg in range(TG):
                sp.wait_ge(out_ready, tg + 1)
                sp.dma_start(tiles(out, tg), F[:, TPG * tg:TPG * (tg + 1), :]).then_inc(out_stored, 16)
                if tg + 2 < TG:
                    sp.dma_start(x2b[:, tg % 2], tiles(x2_dram, tg + 2)).then_inc(x2b_loaded[tg % 2], 16)
            sp.wait_ge(out_stored, 16 * TG)

        @block.gpsimd
        def _(pool):
            nc.gpsimd.memset(ident[:, :], 0.0).then_inc(ident_0, 1)
            nc.gpsimd.memset(causal[:, :], 0.0).then_inc(ident_0, 1)
            nc.gpsimd.memset(tril[:, :, :], 1.0).then_inc(ident_0, 1)
            nc.gpsimd.memset(ones, 1.0).then_inc(ident_0, 1)
            pool.wait_ge(ident_0, 4)
            nc.gpsimd.affine_select(out=ident[:, :], in_=ident[:, :], compare_op=ALU.not_equal, fill=1.0, base=0,
                                    pattern=[[-1, P]], channel_multiplier=1).then_inc(const_done, 1)
            nc.gpsimd.affine_select(out=causal[:, :], in_=causal[:, :], compare_op=ALU.is_ge, fill=MASKED, base=0,
                                    pattern=[[-1, P]], channel_multiplier=1).then_inc(const_done, 1)
            nc.gpsimd.affine_select(out=tril[:, :, :], in_=tril[:, :, :], compare_op=ALU.is_gt, fill=0.0, base=0,
                                    pattern=[[1, E], [-1, E]], channel_multiplier=0).then_inc(const_done, 1)

            def round_to(hi, raw):
                return nc.gpsimd.tensor_tensor(hi, raw, ones.to_broadcast(list(raw.shape)), ALU.mult)

            def split_qkv(unit, par, loads, first=False):
                for k in range(3):
                    if k == 0:
                        pool.wait_ge(wqkv_loaded[par], 16 * loads)
                    if not first:
                        pool.wait_ge(proj_done, 6 * unit - 6 + 2 * k + 2)
                    round_to(wqkv_hi[:, k], wqkv_raw[:, par, k]).then_inc(wqkv_rounded, 1)
                    pool.wait_ge(wqkv_rounded, 3 * unit + k + 1)
                    nc.gpsimd.tensor_tensor(wqkv_lo[:, k], wqkv_raw[:, par, k], wqkv_hi[:, k].bitcast(F32),
                                            ALU.subtract).then_inc(wqkv_split, 1)

            def split_wo(unit, par, loads, first=False):
                pool.wait_ge(wo_loaded[par], 16 * loads)
                if not first:
                    pool.wait_ge(wo_done, QT * unit)
                round_to(wo_hi[:, None, :], wo_raw[:, par:par + 1]).then_inc(wo_rounded, 1)
                pool.wait_ge(wo_rounded, unit + 1)
                nc.gpsimd.tensor_tensor(wo_lo[:, :], wo_raw[:, par], wo_hi[:, :].bitcast(F32),
                                        ALU.subtract).then_inc(wo_split, 1)

            half = UNITS // 2
            for b in range(B):
                u0 = b * UNITS
                if b == 0:
                    split_qkv(0, 0, 1, first=True)
                split_qkv(u0 + 1, 1, b * half + 1)
                split_wo(u0, 0, b * half + 1, first=(b == 0))
                with pool.Fori(0, half - 1) as it:
                    split_qkv(u0 + 2 + 2 * it, 0, b * half + it + 2)
                    split_wo(u0 + 1 + 2 * it, 1, b * half + it + 1)
                    split_qkv(u0 + 3 + 2 * it, 1, b * half + it + 2)
                    split_wo(u0 + 2 + 2 * it, 0, b * half + it + 2)
                if b + 1 < B:
                    split_qkv(u0 + UNITS, 0, (b + 1) * half + 1)
                split_wo(u0 + UNITS - 1, 1, (b + 1) * half)

            pool.wait_ge(small_loaded, 16 * 4)
            round_to(wr_hi[:, :, :], wr_raw[:, :, :]).then_inc(wr_rounded, 1)
            pool.wait_ge(wr_rounded, 1)
            nc.gpsimd.tensor_tensor(wr_lo[:, :, :], wr_raw[:, :, :], wr_hi[:, :, :].bitcast(F32),
                                    ALU.subtract).then_inc(wr_split, 1)

            def split_slice(m, par, parts, bias=True):
                pool.wait_ge(wf_loaded, 32 * m + 32)
                round_to(wf_hi[par][:, parts], wf_raw[:, parts]).then_inc(wf_rounded, 1)
                pool.wait_ge(wf_rounded, m + 1)
                if bias:
                    round_to(bgu[par][:, :, :], bgu_raw).then_inc(bgu_ready, 1)
                nc.gpsimd.tensor_tensor(wf_lo[par][:, parts], wf_raw[:, parts], wf_hi[par][:, parts].bitcast(F32),
                                        ALU.subtract).then_inc(wf_split, 1)

            for m in range(NSH):
                split_slice(m, m % 2, slice(0, 3, 2), bias=False)
            with pool.Fori(0, NR // 2) as it:
                for par in range(2):
                    m = 2 * it + par + NSH
                    pool.wait_ge(down_done, NT * (m - 1))
                    split_slice(m, par, slice(0, 3))

        @block.scalar
        def _(act):
            nc_act = nc.scalar
            act.wait_ge(cT_loaded, 16)
            nc_act.activation(sc[:, :, :], cT[:, :, :], ACT.Exp, scale=-1.0).then_inc(silu_exp, 1)

            def layer_norm_sd(G):
                act.wait_ge(ln_var, G + 1)
                nc_act.activation(sd[:, G], sd[:, G], ACT.Sqrt).then_inc(ln_sd, 1)

            def layer_norm_out(G, dst_hi, col, banks, vec, b):
                for dc in range(DC):
                    act.wait_ge(lnT_done, DC * G + dc + 1)
                    bank = banks[dc % len(banks)]
                    nc_act.activation(bank, bank, ACT.Identity, bias=mod_cols[:, vec * DC + dc, b:b + 1],
                                      scale=mod_cols[:, (vec + 1) * DC + dc, b:b + 1]).then_inc(ln_affine, 1)
                    act.wait_ge(ln_affine, DC * G + dc + 1)
                    nc_act.activation(dst_hi[:, dc, col:col + W], bank, ACT.Copy).then_inc(ln_hi, 1)

            def proj_hi(unit, par, k):
                act.wait_ge(proj_done, 6 * unit + k + 1)
                g = k % NG
                bank = ps_g[PROJ_BANK[k]]
                if k < 4:
                    dst = (q_hi, k_hi)[k // 2][par]
                    nc_act.activation(dst[:, g * W:(g + 1) * W], bank[:, :], ACT.Copy,
                                      scale=SCALE if k < 2 else 1.0).then_inc(qk_hi_done, 1)
                else:
                    nc_act.activation(vT[:, g, :], bank[:, :], ACT.Copy).then_inc(vT_copied, 1)

            def v_round(unit, par, g, bank):
                act.wait_ge(vtr_done, 2 * unit + g + 1)
                nc_act.activation(v_hi[par][:, 4 * g:4 * g + 4, :], bank.rearrange("p (j h) -> p j h", h=P),
                                  ACT.Copy).then_inc(v_hi_done, 1)

            def softmax_exp(unit, par, i):
                act.wait_ge(rowmax, QT * unit + i + 1)
                pieces, n = score_pieces(i)
                nc_act.activation(probs[:, i % 2, 0:pieces * n].rearrange("p (a n) -> p a n", n=n),
                                  ps_s[i % 2][:, 0:pieces, 0:n], ACT.Exp, bias=nmax[:, i:i + 1],
                                  accum_out=rsum[:, par, i:i + 1]).then_inc(exp_done, 1)

            def p_round(unit, i):
                for k in range(FIRST_PG[i], FIRST_PG[i + 1]):
                    _, j, n = P_GROUPS[k]
                    act.wait_ge(pT_done, NPG * unit + k + 1)
                    nc_act.activation(p_block(pT_hi, i, j, n), p_bank(k, n), ACT.Copy).then_inc(p_hi_done, 1)

            def z_round(unit, g):
                act.wait_ge(pv_done, 2 * unit + g + 1)
                nc_act.activation(z_hi[:, g * W:(g + 1) * W], ps_g[PV_BANK[g]][:, :], ACT.Copy) \
                      .then_inc(z_hi_done, 1)

            def slot(U, par, has_prev=True, has_next=True):
                nxt = lambda k: proj_hi(U + 1, 1 - par, k) if has_next else None
                softmax_exp(U, par, 0)
                softmax_exp(U, par, 1)
                nxt(0)
                p_round(U, 0)
                softmax_exp(U, par, 2)
                if has_prev:
                    z_round(U - 1, 1)
                nxt(1)
                p_round(U, 1)
                softmax_exp(U, par, 3)
                nxt(2)
                p_round(U, 2)
                softmax_exp(U, par, 4)
                nxt(3)
                p_round(U, 3)
                softmax_exp(U, par, 5)
                nxt(4)
                p_round(U, 4)
                softmax_exp(U, par, 6)
                z_round(U, 0)
                p_round(U, 5)
                nxt(5)
                if has_next:
                    v_round(U + 1, 1 - par, 0, ps_t[0])
                softmax_exp(U, par, 7)
                p_round(U, 6)
                if has_next:
                    v_round(U + 1, 1 - par, 1, ps_t[1])
                p_round(U, 7)

            for b in range(B):
                u0 = b * UNITS
                for g in range(NG):
                    layer_norm_sd(NG * b + g)
                if b == 0:
                    act.wait_ge(mod_read, 1)
                for g in range(NG):
                    layer_norm_out(NG * b + g, hT_hi, g * W, LN_BANKS, 0, b)
                for k in range(6):
                    proj_hi(u0, 0, k)
                for g in range(NG):
                    v_round(u0, 0, g, ps_t[g])
                slot(u0, 0, has_prev=False)
                with act.Fori(0, UNITS // 2 - 1) as it:
                    slot(u0 + 1 + 2 * it, 1)
                    slot(u0 + 2 + 2 * it, 0)
                slot(u0 + UNITS - 1, 1, has_next=False)
                z_round(u0 + UNITS - 1, 1)

            for tg in range(TG):
                layer_norm_sd(TG + tg)
                if tg == 0:
                    act.wait_ge(mod_read, 2 + B)
                layer_norm_out(TG + tg, h2_hi, tg * W, LN_BANKS, 2, tg // NG)
            for tg in range(TG):
                act.wait_ge(router_done, tg + 1)
                if tg == 0:
                    act.wait_ge(small_loaded, 16 * 4)
                nc_act.activation(gateT[:, tg, :], ps_d[tg][0:E, :], ACT.Identity, bias=br[:, 0:1]) \
                      .then_inc(gateT_ready, 1)

            def hidden(step, tg, bias, shared=False, first=False):
                for c in range(HC):
                    act.wait_ge(gate_done, HC * step + c + 1)
                    if not first:
                        act.wait_ge(hid_lo_done, HC * step - HC + c + 1)
                    nc_act.activation(hid[:, c, :], ps_gu[c][0], ACT.Silu, bias=bias(c)).then_inc(silu_done, 1)
                for c in range(HC):
                    if shared:
                        act.wait_ge(silu_done, HC * step + c + 1)
                    else:
                        act.wait_ge(hidden_ready, HC * step - HC * TG * NSH + c + 1)
                    nc_act.activation(hid_hi[tg % 2][:, c, :], hid[:, c, :], ACT.Copy).then_inc(hid_hi_done, 1)

            for m in range(NSH):
                for tg in range(TG):
                    if m == 0 and tg == 2:
                        act.wait_ge(route_shift, 1)
                        nc_act.activation(sel[:, :, :], gs[:, :, :], ACT.Exp).then_inc(route_exp, 1)
                    hidden(TG * m + tg, tg, lambda c: bsu[:, m, c:c + 1], shared=True, first=(m + tg == 0))
            with act.Fori(0, NR // 2) as it:
                for par in range(2):
                    n = 2 * it + par
                    act.wait_ge(bgu_ready, n + 1)
                    for tg in range(TG):
                        hidden(TG * NSH + TG * n + tg, tg,
                               lambda c: bgu[par][:, 0, c:c + 1])

        @block.vector
        def _(dve):
            v = nc.vector
            dve.wait_ge(silu_exp, 1)
            v.tensor_scalar_add(sc[:, :, :], sc[:, :, :], 1.0).then_inc(silu_step, 1)
            dve.wait_ge(silu_step, 1)
            v.reciprocal(sc[:, :, :], sc[:, :, :]).then_inc(silu_step, 1)
            dve.wait_ge(silu_step, 2)
            v.tensor_tensor(sc[:, :, :], sc[:, :, :], cT[:, :, :], ALU.mult).then_inc(silu_step, 1)
            dve.wait_ge(silu_step, 3)
            for k in range(DC):
                for b in range(B):
                    v.tensor_copy(sc_wide[:, k * B + b, :], sc[:, k, b:b + 1].to_broadcast([P, P])) \
                     .then_inc(sc_ready, 1)

            def layer_norm_stats(G, src):
                for t in range(TPG):
                    v.bn_stats(st[:, G, t], src[:, t]).then_inc(ln_stat, 1)
                for t in range(TPG):
                    dve.wait_ge(ln_stat, TPG * G + t + 1)
                    v.bn_aggr(mv[:, G, t], st[:, G, t]).then_inc(ln_agg, 1)
                dve.wait_ge(ln_agg, TPG * (G + 1))
                v.tensor_scalar_add(sd[:, G], mv[:, G, :, 1], EPS).then_inc(ln_var, 1)

            def layer_norm_apply(G, src, dst):
                dve.wait_ge(ln_sd, G + 1)
                v.reciprocal(rstd[:, G], sd[:, G]).then_inc(ln_rstd, 1)
                dve.wait_ge(ln_rstd, G + 1)
                for t in range(TPG):
                    v.tensor_scalar(dst[:, t], src[:, t], mv[:, G, t, 0:1], rstd[:, G, t:t + 1],
                                    ALU.subtract, ALU.mult).then_inc(xn_ready, 1)

            def layer_norm_rest(G, dst_hi, dst_lo, col, banks):
                for dc in range(DC):
                    dve.wait_ge(ln_hi, DC * G + dc + 1)
                    v.tensor_tensor(dst_lo[:, dc, col:col + W], banks[dc % len(banks)],
                                    dst_hi[:, dc, col:col + W].bitcast(F32), ALU.subtract).then_inc(ln_lo, 1)

            def modulation_columns(vecs, count):
                dve.wait_ge(mod_done, count)
                mod_ps = ps_t[0][:, 0:4 * DC * B].rearrange("p (v b) -> p v b", b=B)
                for vec in vecs:
                    rows = slice(vec * DC, (vec + 1) * DC)
                    last = v.tensor_scalar_add(mod_cols[:, rows], mod_ps[:, rows], float(vec % 2))
                last.then_inc(mod_read, 1)

            def gate_row(n, dst, bank, count):
                dve.wait_ge(mod_done, count)
                v.tensor_scalar(dst, bank, 0.0, 2.0, ALU.is_ge, ALU.mult).then_inc(gate_step, 1)
                dve.wait_ge(gate_step, 3 * n + 1)
                v.tensor_scalar_add(dst, dst, -1.0).then_inc(gate_step, 1)
                dve.wait_ge(gate_step, 3 * n + 2)
                v.tensor_tensor(bank, bank, dst, ALU.mult).then_inc(gate_step, 1)
                dve.wait_ge(gate_step, 3 * n + 3)
                v.scalar_tensor_tensor(out=dst, in0=bank, scalar=0.25, in1=dst, op0=ALU.max, op1=ALU.mult) \
                 .then_inc(mod_read, 1)

            def proj_lo(unit, par, k):
                if k >= 4:
                    return
                dve.wait_ge(qk_hi_done, 4 * unit + k + 1)
                cols = slice((k % NG) * W, (k % NG + 1) * W)
                hi, lo = ((q_hi, q_lo), (k_hi, k_lo))[k // 2]
                v.scalar_tensor_tensor(out=lo[par][:, cols], in0=ps_g[PROJ_BANK[k]][:, :],
                                       scalar=SCALE if k < 2 else 1.0, in1=hi[par][:, cols].bitcast(F32),
                                       op0=ALU.mult, op1=ALU.subtract).then_inc(qk_lo_done, 1)

            def v_rest(unit, par, g, bank):
                dve.wait_ge(v_hi_done, 2 * unit + g + 1)
                rows = slice(4 * g, 4 * g + 4)
                v.tensor_tensor(v_lo[par][:, rows, :], bank.rearrange("p (j h) -> p j h", h=P),
                                v_hi[par][:, rows, :].bitcast(F32), ALU.subtract).then_inc(v_lo_done, 1)

            def row_max(unit, i):
                pieces, n = score_pieces(i)
                bank = ps_s[i % 2]
                at = P * i - (pieces - 1) * n
                dve.wait_ge(score_done, QT * unit + i + 1)
                diag = bank[:, pieces - 1, at:at + P]
                v.tensor_tensor(diag, diag, causal[:, :], ALU.add).then_inc(masked, 1)
                dve.wait_ge(masked, QT * unit + i + 1)
                v.tensor_reduce(nmax[:, i:i + 1], bank[:, 0:pieces, 0:n], AX.XY, ALU.max, negate=True) \
                 .then_inc(rowmax, 1)

            def p_rest(unit, i):
                for k in range(FIRST_PG[i], FIRST_PG[i + 1]):
                    _, j, n = P_GROUPS[k]
                    dve.wait_ge(p_hi_done, NPG * unit + k + 1)
                    v.tensor_tensor(p_block(pT_lo, i, j, n), p_bank(k, n), p_block(pT_hi, i, j, n).bitcast(F32),
                                    ALU.subtract).then_inc(p_lo_done, 1)

            def z_rest(unit, par, g):
                dve.wait_ge(z_hi_done, 2 * unit + g + 1)
                cols = slice(g * W, (g + 1) * W)
                v.tensor_tensor(z_lo[:, cols], ps_g[PV_BANK[g]][:, :], z_hi[:, cols].bitcast(F32),
                                ALU.subtract).then_inc(z_lo_done, 1)
                dve.wait_ge(exp_done, QT * unit + TPG * (g + 1))
                v.reciprocal(rinv[:, par, TPG * g:TPG * (g + 1)], rsum[:, par, TPG * g:TPG * (g + 1)]) \
                 .then_inc(rinv_ready, 1)

            def add_out(unit, par, t):
                dve.wait_ge(wo_done, QT * unit + t + 1)
                dve.wait_ge(rinv_ready, 2 * unit + t // TPG + 1)
                v.scalar_tensor_tensor(out=acc[:, t], in0=ps_g[WO_BANK[t]][:, :], scalar=rinv[:, par, t:t + 1],
                                       in1=acc[:, t], op0=ALU.mult, op1=ALU.add).then_inc(acc_done, 1)

            def slot(U, par, has_prev=True, has_next=True):
                nxt = lambda k: proj_lo(U + 1, 1 - par, k) if has_next else None
                prev = lambda t: add_out(U - 1, 1 - par, t) if has_prev else None
                row_max(U, 1)
                nxt(0)
                p_rest(U, 0)
                row_max(U, 2)
                if has_prev:
                    z_rest(U - 1, 1 - par, 1)
                nxt(1)
                prev(4)
                p_rest(U, 1)
                row_max(U, 3)
                prev(5)
                nxt(2)
                prev(6)
                p_rest(U, 2)
                row_max(U, 4)
                prev(7)
                nxt(3)
                p_rest(U, 3)
                row_max(U, 5)
                p_rest(U, 4)
                row_max(U, 6)
                z_rest(U, par, 0)
                p_rest(U, 5)
                row_max(U, 7)
                if has_next:
                    v_rest(U + 1, 1 - par, 0, ps_t[0])
                add_out(U, par, 0)
                add_out(U, par, 1)
                p_rest(U, 6)
                add_out(U, par, 2)
                if has_next:
                    v_rest(U + 1, 1 - par, 1, ps_t[1])
                    row_max(U + 1, 0)
                add_out(U, par, 3)
                p_rest(U, 7)

            for b in range(B):
                u0 = b * UNITS
                for g in range(NG):
                    dve.wait_ge(x_loaded[g], 16 * (b + 1))
                    layer_norm_stats(NG * b + g, x_sb[:, g])
                for g in range(NG):
                    layer_norm_apply(NG * b + g, x_sb[:, g], x_sb[:, g])
                if b == 0:
                    modulation_columns((0, 1), 1)
                for g in range(NG):
                    layer_norm_rest(NG * b + g, hT_hi, hT_lo, g * W, LN_BANKS)
                if b > 0:
                    dve.wait_ge(y_stored, 16 * NG * b)
                v.memset(acc[:, :, :], 0.0).then_inc(acc_zeroed, 1)
                for k in range(4):
                    proj_lo(u0, 0, k)
                for g in range(NG):
                    v_rest(u0, 0, g, ps_t[g])
                if b == 0:
                    for n in range(B):
                        gate_row(n, ga_row[:, n], ps_g[n % 2][:, :], 2 + n)
                row_max(u0, 0)
                slot(u0, 0, has_prev=False)
                with dve.Fori(0, UNITS // 2 - 1) as it:
                    slot(u0 + 1 + 2 * it, 1)
                    slot(u0 + 2 + 2 * it, 0)
                slot(u0 + UNITS - 1, 1, has_next=False)
                z_rest(u0 + UNITS - 1, 1, 1)
                for t in range(TPG, QT):
                    add_out(u0 + UNITS - 1, 1, t)
                for t in range(QT):
                    dve.wait_ge(acc_done, QT * (u0 + UNITS - 1) + t + 1)
                    v.tensor_tensor(acc[:, t], acc[:, t], ga_row[:, b], ALU.mult).then_inc(y_ready, 1)

            for tg in range(TG):
                dve.wait_ge(xb_loaded[tg % 2], 16 * (tg // 2 + 1))
                dve.wait_ge(yb_loaded, 16 * (tg + 1))
                v.tensor_tensor(yb, yb, xb[:, tg % 2], ALU.add).then_inc(x2_ready, 1)
                dve.wait_ge(x2_ready, tg + 1)
                layer_norm_stats(TG + tg, yb)
                layer_norm_apply(TG + tg, yb, xb[:, tg % 2])
                if tg == 0:
                    modulation_columns((2, 3), 2 + B)
                layer_norm_rest(TG + tg, h2_hi, h2_lo, tg * W, LN_BANKS)

            def hidden(step, tg, par=None):
                if par is not None:
                    for c in range(HC):
                        dve.wait_ge(up_done, HC * step - HC * TG * NSH + c + 1)
                        dve.wait_ge(silu_done, HC * step + c + 1)
                        v.scalar_tensor_tensor(out=hid[:, c, :], in0=ps_gu[c][1],
                                               scalar=bgu[par][:, 1, c:c + 1],
                                               in1=hid[:, c, :], op0=ALU.add, op1=ALU.mult) \
                         .then_inc(hidden_ready, 1)
                for c in range(HC):
                    dve.wait_ge(hid_hi_done, HC * step + c + 1)
                    v.tensor_tensor(hid_lo[tg % 2][:, c, :], hid[:, c, :], hid_hi[tg % 2][:, c, :].bitcast(F32),
                                    ALU.subtract).then_inc(hid_lo_done, 1)

            def add_down(m, tg, col=None):
                for k in range(TPG):
                    t = TPG * tg + k
                    dve.wait_ge(down_done, NT * m + t + 1)
                    if col is None:
                        if m == 0:
                            v.tensor_copy(F[:, t], ps_d[k][:, :]).then_inc(F_added, 1)
                        else:
                            dve.wait_ge(F_added, NT * (m - 1) + t + 1)
                            v.tensor_tensor(F[:, t], F[:, t], ps_d[k][:, :], ALU.add).then_inc(F_added, 1)
                    else:
                        dve.wait_ge(F_added, NT * m - NT + t + 1)
                        v.scalar_tensor_tensor(out=F[:, t], in0=ps_d[k][:, :],
                                               scalar=mix[:, t, bass.ds(col, 1)], in1=F[:, t],
                                               op0=ALU.mult, op1=ALU.add).then_inc(F_added, 1)

            def route():
                done = 1

                def after():
                    nonlocal done
                    dve.wait_ge(route_step, done)
                    done += 1

                gt, eq = (route_tmp[:, k * NT * E * E:(k + 1) * NT * E * E].rearrange("p (t i j) -> p t i j", i=E, j=E)
                          for k in range(2))
                g_j = gs[:, :, None, :].to_broadcast([P, NT, E, E])
                g_i = gs[:, :, :, None].to_broadcast([P, NT, E, E])
                after()
                v.tensor_tensor(eq, g_j, g_i, ALU.is_equal).then_inc(route_step, 1)
                after()
                v.tensor_tensor(eq, eq, tril[:, None, :, :].to_broadcast([P, NT, E, E]), ALU.mult) \
                 .then_inc(route_step, 1)
                after()
                v.tensor_tensor(gt, g_j, g_i, ALU.is_gt).then_inc(route_step, 1)
                after()
                v.tensor_tensor(gt, gt, eq, ALU.add).then_inc(route_step, 1)
                after()
                v.tensor_reduce(rank[:, :, :], gt, AX.X, ALU.add).then_inc(route_step, 1)
                after()
                v.tensor_reduce(gm[:, :], gs[:, :, :], AX.X, ALU.max).then_inc(route_step, 1)
                after()
                v.tensor_tensor(gs[:, :, :], gs[:, :, :], gm[:, :, None].to_broadcast([P, NT, E]), ALU.subtract) \
                 .then_inc(route_shift, 1)
                v.tensor_scalar(rank[:, :, :], rank[:, :, :], float(TOPK), None, ALU.is_lt).then_inc(route_step, 1)
                after()
                dve.wait_ge(route_exp, 1)
                v.tensor_tensor(rank[:, :, :], rank[:, :, :], sel[:, :, :], ALU.mult).then_inc(route_step, 1)
                after()
                v.tensor_reduce(gsum[:, :], rank[:, :, :], AX.X, ALU.add).then_inc(route_step, 1)
                after()
                v.reciprocal(ginv[:, :], gsum[:, :]).then_inc(route_step, 1)
                after()
                v.memset(mix[:, :, 0:1], 1.0).then_inc(mix_ready, 1)
                v.tensor_tensor(mix[:, :, 1:1 + NR], rank[:, :, 0:NR], ginv[:, :, None].to_broadcast([P, NT, NR]),
                                ALU.mult).then_inc(mix_ready, 1)

            dve.wait_ge(gateT_back, 1)
            v.tensor_copy(gs[:, :, :], ps_d[0][:, 0:NT * E].rearrange("p (t e) -> p t e", e=E)) \
             .then_inc(route_step, 1)
            for n in range(B):
                gate_row(B + n, gb_row[:, n], ps_d[1 + n][:, :], 3 + B + n)
            dve.wait_ge(x2_stored, 16 * TG)
            for step in range(NSH * TG):
                hidden(step, step % TG)
                if step == NSH * TG - 1:
                    for tg in range(TG):
                        dve.wait_ge(mixT_done, tg + 1)
                        v.tensor_copy(wT[0:1 + NR, tg, :], ps_gu[tg % 2][1][0:1 + NR, :]).then_inc(mixT_read, 1)
                if step > 0:
                    add_down((step - 1) // TG, (step - 1) % TG)
                if step == 1:
                    route()
            for t in range(NT):
                dve.wait_ge(bias_done, t + 1)
                dve.wait_ge(F_added, NT * (NSH - 1) - TPG + t + 1 if t >= NT - TPG else NT * (NSH - 1) + t + 1)
                v.tensor_tensor(F[:, t], F[:, t], ps_d[t % TPG][:, :], ALU.add).then_inc(bias_added, 1)

            def expert(n, m, par):
                for tg in range(TG):
                    hidden(TG * m + tg, tg, par)
                    if tg == 0:
                        add_down(m - 1, TG - 1, n)
                    else:
                        add_down(m, tg - 1, n + 1)

            with dve.Fori(0, NR // 2) as it:
                for par in range(2):
                    n = 2 * it + par
                    dve.wait_ge(bgu_ready, n + 1)
                    expert(n, NSH + n, par)
            add_down(NM - 1, TG - 1, NR)
            for tg in range(TG):
                for t in range(TPG * tg, TPG * (tg + 1)):
                    dve.wait_ge(F_added, NT * (NM - 1) + t + 1)
                    v.tensor_tensor(F[:, t], F[:, t], gb_row[:, tg // NG], ALU.mult).then_inc(F_scaled, 1)
                dve.wait_ge(x2b_loaded[tg % 2], 16 * (tg // 2 + 1))
                dve.wait_ge(F_scaled, TPG * (tg + 1))
                mine = slice(TPG * tg, TPG * (tg + 1))
                v.tensor_tensor(F[:, mine], F[:, mine], x2b[:, tg % 2], ALU.add).then_inc(out_ready, 1)

        @block.tensor
        def _(pe):
            mm = nc.tensor.matmul

            def product(out, stat, mov, first, last):
                mm(out, stat[0], mov[0], start=first, stop=False)
                mm(out, stat[0], mov[1], start=False, stop=False)
                return mm(out, stat[1], mov[0], start=False, stop=last)

            pe.wait_ge(sc_ready, DC * B)
            pe.wait_ge(const_done, 3)
            order = [0, 1, 3, 4]
            mod_ps = ps_t[0][:, 0:4 * DC * B].rearrange("p (v b) -> p v b", b=B)

            def mod_columns(n, w):
                pe.wait_ge(wmod_loaded[order[n]], 16)
                for dc in range(DC):
                    for k in range(DC):
                        last = mm(mod_ps[:, n * DC + dc, :], w[:, k, dc * P:(dc + 1) * P],
                                  sc[:, k, :], start=(k == 0), stop=(k == DC - 1))
                return last

            def mod_row(vec, b, w, bank):
                pe.wait_ge(wmod_loaded[vec], 16)
                for k in range(DC):
                    last = mm(bank, sc_wide[:, k * B + b, :], w[:, k, :], start=(k == 0), stop=(k == DC - 1))
                last.then_inc(mod_done, 1)

            def layer_norm_transpose(G, src, banks, used):
                for dc in range(DC):
                    used(dc)
                    for t in range(TPG):
                        if dc == 0:
                            pe.wait_ge(xn_ready, TPG * G + t + 1)
                        last = nc.tensor.transpose(banks[dc % len(banks)][:, t * P:(t + 1) * P],
                                                   src[:, t, dc * P:(dc + 1) * P], ident[:, :])
                    last.then_inc(lnT_done, 1)

            def project(unit, par, k):
                g = k % NG
                pe.wait_ge(wqkv_split, 3 * unit + k // 2 + 1)
                for dc in range(DC):
                    last = product(ps_g[PROJ_BANK[k]][:, :], (wqkv_hi[:, k // 2, dc], wqkv_lo[:, k // 2, dc]),
                                   [h[:, dc, g * W:(g + 1) * W] for h in (hT_hi, hT_lo)], dc == 0, dc == DC - 1)
                last.then_inc(proj_done, 1)

            def v_transpose(unit, g, bank):
                pe.wait_ge(vT_copied, 2 * unit + g + 1)
                for j in range(4):
                    last = nc.tensor.transpose(bank[:, j * P:(j + 1) * P], vT[:, g, j * P:(j + 1) * P], ident[:, :])
                last.then_inc(vtr_done, 1)

            def scores(unit, par, i):
                if i == 0:
                    pe.wait_ge(qk_lo_done, 4 * unit + 4)
                pieces, n = score_pieces(i)
                cols = slice(i * P, (i + 1) * P)
                for piece, (s, m) in enumerate(((q_hi, k_hi), (q_hi, k_lo), (q_lo, k_hi))):
                    for a in range(pieces):
                        last = mm(ps_s[i % 2][:, a, 0:n], s[par][:, cols], m[par][:, a * n:(a + 1) * n],
                                  start=(piece == 0), stop=(piece == 2))
                last.then_inc(score_done, 1)

            def p_transpose(unit, i, used):
                pe.wait_ge(exp_done, QT * unit + i + 1)
                for k in range(FIRST_PG[i], FIRST_PG[i + 1]):
                    _, j0, n = P_GROUPS[k]
                    used(k)
                    for j in range(n):
                        last = nc.tensor.transpose(ps_t[P_BANK[k]][:, j * P:(j + 1) * P],
                                                   probs[:, i % 2, (j0 + j) * P:(j0 + j + 1) * P], ident[:, :])
                    last.then_inc(pT_done, 1)

            def values(unit, par, g):
                pe.wait_ge(p_lo_done, NPG * unit + FIRST_PG[4 * (g + 1)])
                if g == 0:
                    pe.wait_ge(v_lo_done, 2 * unit + 2)
                nj = 4 * (g + 1)
                for j in range(nj):
                    c0 = max(0, j - 4 * g) * P
                    last = product(ps_g[PV_BANK[g]][:, c0:W], (v_hi[par][:, j], v_lo[par][:, j]),
                                   (pT_hi[g][:, j, c0:W], pT_lo[g][:, j, c0:W]), j == 0, j == nj - 1)
                last.then_inc(pv_done, 1)

            def out_proj(unit, t):
                if t == 0:
                    pe.wait_ge(wo_split, unit + 1)
                if t % TPG == 0:
                    pe.wait_ge(z_lo_done, 2 * unit + t // TPG + 1)
                cols = slice(t * P, (t + 1) * P)
                product(ps_g[WO_BANK[t]][:, :], (z_hi[:, cols], z_lo[:, cols]), (wo_hi[:, :], wo_lo[:, :]),
                        True, True).then_inc(wo_done, 1)

            def proj_read(unit, k):
                if k < 4:
                    pe.wait_ge(qk_lo_done, 4 * unit + k + 1)
                else:
                    pe.wait_ge(vT_copied, 2 * unit + k - 3)

            def z_read(unit, g):
                pe.wait_ge(z_lo_done, 2 * unit + g + 1)

            def out_read(unit, t):
                pe.wait_ge(acc_done, QT * unit + t + 1)

            def p_read(unit, k):
                pe.wait_ge(p_lo_done, NPG * unit + k + 1)

            def v_read(unit, g):
                pe.wait_ge(v_lo_done, 2 * unit + g + 1)

            def score_read(unit, i):
                pe.wait_ge(exp_done, QT * unit + i + 1)

            def slot(U, par, has_prev=True, has_next=True):
                N, Q = U + 1, 1 - par

                def p_used(k):
                    if k == 0:
                        if has_prev:
                            p_read(U - 1, NPG - 2)
                        else:
                            v_read(U, 0)
                    elif k == 1:
                        if has_prev:
                            p_read(U - 1, NPG - 1)
                        else:
                            v_read(U, 1)
                    elif k == 8:
                        p_read(U, 7)
                    elif k == 9:
                        v_read(N, 0) if has_next else p_read(U, 6)
                    elif k == 10:
                        p_read(U, 9)
                    elif k == 11:
                        v_read(N, 1) if has_next else p_read(U, 8)
                    else:
                        p_read(U, k - 2)

                if has_next:
                    if has_prev:
                        out_read(U - 1, 2)
                    else:
                        proj_read(U, 3)
                    project(N, Q, 0)
                p_transpose(U, 0, p_used)
                score_read(U, 0)
                scores(U, par, 2)
                if has_prev:
                    out_read(U - 1, 3)
                    values(U - 1, Q, 1)
                if has_next:
                    proj_read(N, 0)
                    project(N, Q, 1)
                if has_prev:
                    z_read(U - 1, 1)
                    out_proj(U - 1, 4)
                p_transpose(U, 1, p_used)
                score_read(U, 1)
                scores(U, par, 3)
                if has_prev:
                    if has_next:
                        proj_read(N, 1)
                    else:
                        out_read(U - 1, 2)
                    out_proj(U - 1, 5)
                if has_next:
                    if has_prev:
                        out_read(U - 1, 4)
                    else:
                        proj_read(U, 5)
                    project(N, Q, 2)
                if has_prev:
                    out_read(U - 1, 5)
                    out_proj(U - 1, 6)
                p_transpose(U, 2, p_used)
                score_read(U, 2)
                scores(U, par, 4)
                if has_prev:
                    if has_next:
                        proj_read(N, 2)
                    else:
                        out_read(U - 1, 4)
                    out_proj(U - 1, 7)
                if has_next:
                    if has_prev:
                        out_read(U - 1, 6)
                    else:
                        proj_read(N, 1)
                    project(N, Q, 3)
                p_transpose(U, 3, p_used)
                score_read(U, 3)
                scores(U, par, 5)
                if has_next:
                    if has_prev:
                        out_read(U - 1, 7)
                    else:
                        proj_read(N, 2)
                    project(N, Q, 4)
                p_transpose(U, 4, p_used)
                score_read(U, 4)
                scores(U, par, 6)
                if has_next:
                    proj_read(N, 3)
                else:
                    out_read(U - 1, 6)
                values(U, par, 0)
                p_transpose(U, 5, p_used)
                score_read(U, 5)
                scores(U, par, 7)
                if has_next:
                    proj_read(N, 4)
                    project(N, Q, 5)
                    p_read(U, 6)
                    v_transpose(N, 0, ps_t[0])
                z_read(U, 0)
                out_proj(U, 0)
                if has_next:
                    proj_read(N, 5)
                else:
                    out_read(U - 1, 7)
                out_proj(U, 1)
                p_transpose(U, 6, p_used)
                out_read(U, 0)
                out_proj(U, 2)
                if has_next:
                    score_read(U, 6)
                    scores(N, Q, 0)
                    p_read(U, 8)
                    v_transpose(N, 1, ps_t[1])
                out_read(U, 1)
                out_proj(U, 3)
                p_transpose(U, 7, p_used)
                if has_next:
                    score_read(U, 7)
                    scores(N, Q, 1)

            for n in range(2):
                last = mod_columns(n, wmod[:, n])
            last.then_inc(mod_done, 1)
            for b in range(B):
                u0 = b * UNITS
                for g in range(NG):
                    G = NG * b + g

                    def used(dc):
                        if g > 0:
                            pe.wait_ge(ln_lo, DC * (G - 1) + dc + 1)
                        elif b > 0 and dc == 0:
                            score_read(u0 - 1, QT - 1)
                    layer_norm_transpose(G, x_sb[:, g], LN_BANKS, used)
                for k in range(6):
                    if k == 0 and b > 0:
                        out_read(u0 - 1, QT - 1)
                    if k == 1:
                        proj_read(u0, 0)
                    if k == 3:
                        proj_read(u0, 1)
                    if k == 4:
                        proj_read(u0, 2)
                    if k == 5:
                        proj_read(u0, 4)
                    if k < NG:
                        pe.wait_ge(ln_lo, DC * (NG * b + k + 1))
                    project(u0, 0, k)
                if b > 0:
                    p_read(u0 - 1, NPG - 1)
                else:
                    pe.wait_ge(mod_read, 1)
                for g in range(NG):
                    v_transpose(u0, g, ps_t[g])
                if b == 0:
                    proj_read(u0, 3)
                    mod_row(2, 0, wmod[:, 2], ps_g[0][:, :])
                    proj_read(u0, 5)
                    mod_row(2, 1, wmod[:, 2], ps_g[1][:, :])
                for i in range(2):
                    scores(u0, 0, i)
                if b == 0:
                    pe.wait_ge(mod_read, 1 + B)
                slot(u0, 0, has_prev=False)
                with pe.Fori(0, UNITS // 2 - 1) as it:
                    slot(u0 + 1 + 2 * it, 1)
                    slot(u0 + 2 + 2 * it, 0)
                slot(u0 + UNITS - 1, 1, has_next=False)
                last = u0 + UNITS - 1
                out_read(last, 3)
                values(last, 1, 1)
                z_read(last, 1)
                out_proj(last, 4)
                out_proj(last, 5)
                out_read(last, 5)
                out_proj(last, 6)
                out_read(last, 4)
                out_proj(last, 7)

            def gates_up(step, m, par, tg, shared=False, first=False):
                if tg == 0:
                    pe.wait_ge(wf_split, m + 1)
                for c in range(HC):
                    for k in range(1 if shared else 2):
                        if not first:
                            pe.wait_ge((silu_done, hid_lo_done)[k], HC * step - HC + c + 1)
                        for dc in range(DC):
                            at = dc * HID + c * P
                            last = product(ps_gu[c][k], (wf_hi[par][:, k, at:at + P], wf_lo[par][:, k, at:at + P]),
                                           [h[:, dc, tg * W:(tg + 1) * W] for h in (h2_hi, h2_lo)],
                                           dc == 0, dc == DC - 1)
                        last.then_inc((gate_done, up_done)[k], 1)

            def down(step, m, par, tg):
                pe.wait_ge(hid_lo_done, HC * step + HC)
                for k in range(TPG):
                    if isinstance(m, int) and m == 0 and tg == 0:
                        if k == 0:
                            pe.wait_ge(route_step, 1)
                            pe.wait_ge(mod_read, 2 + 2 * B)
                    else:
                        pe.wait_ge(F_added, NT * m + TPG * (tg - 1) + k + 1)
                    for c in range(HC):
                        last = product(ps_d[k][:, :], [h[tg % 2][:, c, k * P:(k + 1) * P] for h in (hid_hi, hid_lo)],
                                       [w[par][:, 2, c * D:(c + 1) * D] for w in (wf_hi, wf_lo)],
                                       c == 0, c == HC - 1)
                    last.then_inc(down_done, 1)

            for tg in range(TG):
                def used(dc):
                    if tg > 0:
                        pe.wait_ge(ln_lo, DC * (TG + tg - 1) + dc + 1)
                    elif dc == 0:
                        score_read(ATT - 1, QT - 1)
                layer_norm_transpose(TG + tg, xb[:, tg % 2], LN_BANKS, used)
                if tg == 0:
                    for n in range(2, 4):
                        last = mod_columns(n, wmod2[:, n - 2])
                    last.then_inc(mod_done, 1)
            pe.wait_ge(wr_split, 1)
            pe.wait_ge(mod_read, 2 + B)
            for tg in range(TG):
                pe.wait_ge(ln_lo, DC * (TG + tg + 1))
                for dc in range(DC):
                    last = product(ps_d[tg][0:E, :], (wr_hi[:, dc], wr_lo[:, dc]),
                                   [h[:, dc, tg * W:(tg + 1) * W] for h in (h2_hi, h2_lo)], dc == 0, dc == DC - 1)
                last.then_inc(router_done, 1)
            pe.wait_ge(gateT_ready, TG)
            gate_T = gateT[:, :, :].rearrange("e g w -> e (g w)")
            for t in range(NT):
                last = nc.tensor.transpose(ps_d[0][:, t * E:(t + 1) * E], gate_T[:, t * P:(t + 1) * P],
                                           ident[0:E, 0:E])
            last.then_inc(gateT_back, 1)
            gates_up(0, 0, 0, 0, shared=True, first=True)
            for b in range(B):
                mod_row(5, b, wmod2[:, 2], ps_d[1 + b][:, :])
            for step in range(1, NSH * TG):
                gates_up(step, step // TG, step // TG % 2, step % TG, shared=True)
                if step == NSH * TG - 1:
                    pe.wait_ge(mix_ready, 2)
                    for tg in range(TG):
                        if tg >= 2:
                            pe.wait_ge(mixT_read, tg - 1)
                        for t in range(TPG):
                            last = nc.tensor.transpose(ps_gu[tg % 2][1][0:1 + NR, t * P:(t + 1) * P],
                                                       mix[:, TPG * tg + t, :], ident[:, :])
                        last.then_inc(mixT_done, 1)
                down(step - 1, (step - 1) // TG, (step - 1) // TG % 2, (step - 1) % TG)
            w_T = wT[0:1 + NR, :, :].rearrange("e g w -> e (g w)")
            pe.wait_ge(mixT_read, TG)
            for t in range(NT):
                if t < TPG:
                    pe.wait_ge(F_added, NT * (NSH - 1) + NT - 2 * TPG + t + 1)
                else:
                    pe.wait_ge(bias_added, t - TPG + 1)
                mm(ps_d[t % TPG][:, :], w_T[:, t * P:(t + 1) * P], bd[:, :], start=True, stop=True) \
                  .then_inc(bias_done, 1)
            pe.wait_ge(bias_added, NT)
            with pe.Fori(0, NR // 2) as it:
                for par in range(2):
                    m = NSH + 2 * it + par
                    for tg in range(TG):
                        gates_up(TG * m + tg, m, par, tg)
                        if tg == 0:
                            down(TG * m - 1, m - 1, 1 - par, TG - 1)
                        else:
                            down(TG * m + tg - 1, m, par, tg - 1)
            down(TG * NM - 1, NM - 1, (NM - 1) % 2, TG - 1)


def kernel(**inputs):
    import numpy as np
    import concourse.bacc as bacc
    from concourse.bass_utils import run_bass_kernel_spmd as run

    a = {k.replace("L0_", ""): np.asarray(v) for k, v in inputs.items()}
    H, Dh, D = a["attn_W_Q"].shape
    DC = D // P
    NR, _, HID = a["ffn_Wgate"].shape
    HC = HID // P
    NSH = a["ffn_Ws_up"].shape[1] // HID
    E = a["ffn_Wg"].shape[1]

    def head_major(w):
        return w.transpose(0, 2, 1).reshape(H, DC, P, Dh).transpose(0, 2, 1, 3).reshape(H, P, DC * Dh)

    def chunked(w):
        n, rows, cols = w.shape
        return w.reshape(n, rows // P, P, cols).transpose(0, 2, 1, 3).reshape(n, P, -1)

    arrays = {
        "x_in": a["attn_x"],
        "w_attn": np.concatenate([head_major(a["attn_W_Q"]), head_major(a["attn_W_K"]), head_major(a["attn_W_V"]),
                                  a["attn_W_O"].T.reshape(H, P, D)], axis=2),
        "w_mod": a["wmod"],
        "c_T": a["c"].T.reshape(DC, P, -1).transpose(1, 0, 2),
        "w_router": a["ffn_Wg"].reshape(DC, P, E).transpose(1, 0, 2),
        "b_router": a["ffn_bg"].reshape(E, 1),
        "w_routed": np.concatenate([chunked(a["ffn_Wgate"]), chunked(a["ffn_Wup"]), chunked(a["ffn_Wdown"]),
                                    np.stack([a["ffn_bgate"], a["ffn_bup"]], 1).reshape(NR, 2 * HC, P)
                                    .transpose(0, 2, 1)], axis=2),
        "w_shared_up": chunked(a["ffn_Ws_up"].reshape(D, NSH, HID).transpose(1, 0, 2)),
        "w_shared_down": chunked(a["ffn_Ws_down"].reshape(NSH, HID, D)),
        "b_shared_up": a["ffn_bs_up"].reshape(NSH, HC, P).transpose(2, 0, 1),
        "b_down": np.concatenate([a["ffn_bs_down"][None], a["ffn_bdown"]]),
    }
    arrays = {k: np.ascontiguousarray(v) for k, v in arrays.items()}
    nc = bacc.Bacc("TRN2", target_bir_lowering=False, num_devices=1)
    args = [nc.dram_tensor(k, v.shape, mybir.dt.from_np(v.dtype), kind="ExternalInput").ap()
            for k, v in arrays.items()]
    out = nc.dram_tensor("out", arrays["x_in"].shape, F32, kind="ExternalOutput").ap()
    block_kernel(nc, *args, out)
    return run(nc, [arrays], core_ids=[0]).results[0]["out"]
```

```python
from contextlib import ExitStack

import concourse.bass as bass
from concourse import mybir

F32 = mybir.dt.float32
F32R = mybir.dt.float32r
ACT = mybir.ActivationFunctionType
ALU = mybir.AluOpType
AX = mybir.AxisListType

P = 128
EPS = 1e-5
MASKED = -1e10


def block_kernel(nc, x_in, w_attn, w_mod, c_T, w_router, b_router, w_routed, w_shared_up, w_shared_down,
                 b_shared_up, b_down, out):
    B, S, D = x_in.shape
    H = w_attn.shape[0]
    DC = D // P
    QT = S // P
    NT = B * QT
    W = 512
    NG = S // W
    TG = B * NG
    TPG = W // P
    E = b_router.shape[0]
    NR = w_routed.shape[0]
    NSH = w_shared_down.shape[0]
    NM = NSH + NR
    HC = w_shared_down.shape[2] // D
    HID = HC * P
    SCALE = float(P) ** -0.5
    TOPK = NR

    y_dram = nc.dram_tensor("y_scratch", (B, S, D), F32, kind="Internal").ap()
    x2_dram = nc.dram_tensor("x2_scratch", (B, S, D), F32, kind="Internal").ap()

    def tiles(dram, group):
        b, g = divmod(group, NG)
        return dram[b, g * W:(g + 1) * W, :].rearrange("(t p) d -> p t d", p=P)

    P_GROUPS = [(i, j, min(4, i + 1 - j)) for i in range(QT) for j in range(0, i + 1, 4)]
    NPG = len(P_GROUPS)
    FIRST_PG = [next(k for k, g in enumerate(P_GROUPS) if g[0] == i) for i in range(QT)] + [NPG]

    with ExitStack() as ctx:
        def sb(name, shape, dt, c=ctx):
            return c.enter_context(nc.sbuf_tensor(name, shape, dt))

        def sem(name):
            return ctx.enter_context(nc.semaphore(name))

        ident = sb("ident", [P, P], F32)
        causal = sb("causal", [P, P], F32)
        ones = sb("ones", [P, 1, 1], F32)[:, :, :]
        tril = sb("tril", [P, E, E], F32)
        mod_cols = sb("mod_cols", [P, 4 * DC, B], F32)
        rest_rows = sb("rest_rows", [P, 1], F32)
        cT = sb("cT", [P, DC, B], F32)
        sc = sb("sc", [P, DC, B], F32)
        sc_wide = sb("sc_wide", [P, DC * B, P], F32)
        NLN = 2 * TG
        st = sb("st", [P, NLN, TPG, 6], F32)
        mv = sb("mv", [P, NLN, TPG, 2], F32)
        sd = sb("sd", [P, NLN, TPG], F32)
        rstd = sb("rstd", [P, NLN, TPG], F32)

        attn = ExitStack()
        hT_hi = sb("hT_hi", [P, DC, S], F32R, attn)
        hT_lo = sb("hT_lo", [P, DC, S], F32R, attn)
        q_hi, q_lo, k_hi, k_lo = [], [], [], []
        for par in range(2):
            if par == 0:
                with ExitStack() as ln:
                    x_sb = sb("x_sb", [P, NG, TPG, D], F32, ln)
            q_hi.append(sb(f"q_hi{par}", [P, S], F32R, attn))
            q_lo.append(sb(f"q_lo{par}", [P, S], F32R, attn))
            k_hi.append(sb(f"k_hi{par}", [P, S], F32R, attn))
            k_lo.append(sb(f"k_lo{par}", [P, S], F32R, attn))
        v_hi = [sb(f"v_hi{par}", [P, QT, P], F32R, attn) for par in range(2)]
        v_lo = [sb(f"v_lo{par}", [P, QT, P], F32R, attn) for par in range(2)]
        vT = sb("vT", [P, NG, W], F32, attn)
        wqkv_raw = sb("wqkv_raw", [P, 2, 3, DC, P], F32, attn)
        wo_raw = sb("wo_raw", [P, 2, D], F32, attn)
        wqkv_hi = sb("wqkv_hi", [P, 3, DC, P], F32R, attn)
        wqkv_lo = sb("wqkv_lo", [P, 3, DC, P], F32R, attn)
        wo_hi = sb("wo_hi", [P, D], F32R, attn)
        wo_lo = sb("wo_lo", [P, D], F32R, attn)
        probs = sb("probs", [P, 2, S], F32, attn)
        z_hi = sb("z_hi", [P, S], F32R, attn)
        z_lo = sb("z_lo", [P, S], F32R, attn)
        acc = sb("acc", [P, QT, D], F32, attn)
        ga_row = sb("ga_row", [P, B, D], F32, attn)
        nmax = sb("nmax", [P, QT], F32, attn)
        rsum = sb("rsum", [P, 2, QT], F32, attn)
        rinv = sb("rinv", [P, 2, QT], F32, attn)
        with ExitStack() as mod:
            wmod = sb("wmod", [P, 3, DC, D], F32, mod)
        pT_hi = [sb(f"pT_hi{g}", [P, 4 * (g + 1), W], F32R, attn) for g in range(NG)]
        pT_lo = [sb(f"pT_lo{g}", [P, 4 * (g + 1), W], F32R, attn) for g in range(NG)]
        attn.close()

        F = sb("F", [P, NT, D], F32)
        wmod2 = F[:, 0:3 * DC].rearrange("p (v k) d -> p v k d", k=DC)
        with ExitStack() as ln:
            xb = sb("xb", [P, 2, TPG, D], F32, ln)
        w_up = [[sb(f"w_up_{part}{par}", [P, 1, HC * D], F32R) for part in ("hi", "lo")] for par in range(2)]
        route_tmp = xb[:, 0].rearrange("p t d -> p (t d)")
        h2_hi = sb("h2_hi", [P, DC, B * S], F32R)
        with ExitStack() as ln:
            early = sb("early", [P, DC, B * S], F32, ln)
        h2_lo = sb("h2_lo", [P, DC, B * S], F32R)
        yb = [F[:, 3 * TPG:4 * TPG], early[:, :, (TG - 1) * W:TG * W]]
        wf_land = sb("wf_land", [P, 3 * HC * D + 2 * HC], F32)
        wf_raw = wf_land[:, 0:3 * HC * D].rearrange("p (a f) -> p a f", a=3)
        bgu_raw = wf_land[:, 3 * HC * D:].rearrange("p (a c) -> p a c", a=2)
        with ExitStack() as end:
            x2b = sb("x2b", [P, 2, TPG, D], F32, end)
        w_gd = [[sb(f"w_gd_{part}{par}", [P, 2, HC * D], F32R) for part in ("hi", "lo")] for par in range(2)]
        hid_hi = [sb(f"hid_hi{par}", [P, HC, W], F32R) for par in range(2)]
        hid_lo = [sb(f"hid_lo{par}", [P, HC, W], F32R) for par in range(2)]
        hid = sb("hid", [P, HC, W], F32)
        gb_row = sb("gb_row", [P, B, D], F32)
        wr_raw = sb("wr_raw", [P, DC, E], F32)
        wr_hi = sb("wr_hi", [P, DC, E], F32R)
        wr_lo = sb("wr_lo", [P, DC, E], F32R)
        br = sb("br", [E, 1], F32)
        bgu = [sb(f"bgu{par}", [P, 2, HC], F32) for par in range(2)]
        bsu = sb("bsu", [P, NSH, HC], F32)
        NB = 1 + NR
        with ExitStack() as gates:
            gateT = sb("gateT", [E, TG, W], F32, gates)
        wT = sb("wT", [3 * NB, TG, W], F32R)
        bd_raw = sb("bd_raw", [3 * NB, D], F32)
        bd = sb("bd", [3 * NB, D], F32R)
        mix3 = sb("mix3", [P, NT, 3 * NB], F32R)
        mix = sb("mix", [P, NT, 1 + NR], F32)
        rank = sb("rank", [P, NT, E], F32)
        gs = sb("gs", [P, NT, E], F32)
        sel = sb("sel", [P, NT, E], F32)
        gm = sb("gm", [P, NT], F32)
        gsum = sb("gsum", [P, NT], F32)
        ginv = sb("ginv", [P, NT], F32)

        def ps(name, shape):
            return ctx.enter_context(nc.psum_tensor(name, shape, F32))

        ps_s = [ps(f"ps_s{k}", [P, 2, W]) for k in range(2)]
        ps_t = [ps(f"ps_t{k}", [P, W]) for k in range(2)]
        ps_g = [ps(f"ps_g{k}", [P, W]) for k in range(2)]
        S_BANKS = [ps_s[k // 2][:, k % 2, :] for k in range(4)]
        LN_BANKS = [S_BANKS, [ps_t[0][:, :], ps_t[1][:, :]] + S_BANKS[:2]]
        FIRST_PROJ = [ps_g[0][:, :], ps_g[1][:, :]] + S_BANKS
        PROJ_BANK = [0, 0, 1, 0, 1, 1]
        PV_BANK = [0, 1]
        WO_BANK = [0, 1, 0, 1, 1, 0, 0, 1]
        P_BANK = [0, 1, 0, 1, 0, 1, 0, 1, 1, 0, 0, 1]

        def score_pieces(i):
            return (1, P * (i + 1)) if P * (i + 1) <= W else (2, P * (i + 1) // 2)

        def p_block(pT, i, j, n):
            return pT[i // 4][:, j:j + n, (i % 4) * P:(i % 4 + 1) * P]

        def p_bank(k, n):
            return ps_t[P_BANK[k]][:, 0:n * P].rearrange("p (j q) -> p j q", q=P)

        ps_gu = [[ps_s[c][:, k, :] for k in range(2)] for c in range(2)]
        ps_d = [ps_t[0], ps_t[1], ps_g[0], ps_g[1]]
        LN2_BANKS = [S_BANKS, [S_BANKS[1], S_BANKS[3]]]

        const_done = sem("const_done")
        ident_0 = sem("ident_0")
        cT_loaded = sem("cT_loaded")
        wmod_loaded = [sem(f"wmod_loaded{v}") for v in range(6)]
        acc_zeroed = sem("acc_zeroed")
        silu_step = sem("silu_step")
        silu_exp = sem("silu_exp")
        sc_ready = sem("sc_ready")
        mod_done = sem("mod_done")
        mod_read = sem("mod_read")
        gate_step = sem("gate_step")
        x_loaded = [sem(f"x_loaded{g}") for g in range(NG)]
        ln_stat = sem("ln_stat")
        ln_agg = sem("ln_agg")
        ln_var = sem("ln_var")
        ln_sd = sem("ln_sd")
        ln_rstd = sem("ln_rstd")
        xn_ready = sem("xn_ready")
        lnT_done = sem("lnT_done")
        ln_affine = sem("ln_affine")
        ln_hi = sem("ln_hi")
        ln_lo = sem("ln_lo")
        wqkv_loaded = [sem(f"wqkv_loaded{k}") for k in range(2)]
        wo_loaded = [sem(f"wo_loaded{k}") for k in range(2)]
        wqkv_rounded = sem("wqkv_rounded")
        wqkv_split = sem("wqkv_split")
        wo_rounded = sem("wo_rounded")
        wo_split = sem("wo_split")
        proj_done = sem("proj_done")
        qk_hi_done = sem("qk_hi_done")
        qk_lo_done = sem("qk_lo_done")
        vT_copied = sem("vT_copied")
        vtr_done = sem("vtr_done")
        v_hi_done = sem("v_hi_done")
        v_lo_done = sem("v_lo_done")
        score_done = sem("score_done")
        masked = sem("masked")
        rowmax = sem("rowmax")
        exp_done = sem("exp_done")
        pT_done = sem("pT_done")
        p_hi_done = sem("p_hi_done")
        p_lo_done = sem("p_lo_done")
        pv_done = sem("pv_done")
        z_hi_done = sem("z_hi_done")
        z_lo_done = sem("z_lo_done")
        rinv_ready = sem("rinv_ready")
        wo_done = sem("wo_done")
        acc_done = sem("acc_done")
        y_ready = sem("y_ready")
        y_stored = sem("y_stored")
        xb_loaded = [sem(f"xb_loaded{k}") for k in range(2)]
        yb_loaded = [sem(f"yb_loaded{k}") for k in range(2)]
        small_loaded = sem("small_loaded")
        x2b_loaded = [sem(f"x2b_loaded{k}") for k in range(2)]
        x2_ready = sem("x2_ready")
        x2_stored = sem("x2_stored")
        wr_rounded = sem("wr_rounded")
        wr_split = sem("wr_split")
        wf_loaded = sem("wf_loaded")
        gd_rounded = sem("gd_rounded")
        gd_split = sem("gd_split")
        up_rounded = sem("up_rounded")
        up_split = sem("up_split")
        bd_step = sem("bd_step")
        mix3_step = sem("mix3_step")
        bgu_ready = sem("bgu_ready")
        router_done = sem("router_done")
        gateT_ready = sem("gateT_ready")
        gateT_back = sem("gateT_back")
        route_step = sem("route_step")
        route_shift = sem("route_shift")
        route_exp = sem("route_exp")
        mix_ready = sem("mix_ready")
        mixT_done = sem("mixT_done")
        mixT_read = sem("mixT_read")
        bias_done = sem("bias_done")
        bias_added = sem("bias_added")
        gate_done = sem("gate_done")
        up_done = sem("up_done")
        silu_done = sem("silu_done")
        hidden_ready = sem("hidden_ready")
        hid_hi_done = sem("hid_hi_done")
        hid_lo_done = sem("hid_lo_done")
        down_done = sem("down_done")
        F_added = sem("F_added")
        F_scaled = sem("F_scaled")
        out_ready = sem("out_ready")
        out_stored = sem("out_stored")

        block = ctx.enter_context(nc.Block())

        UNITS = H
        ATT = B * UNITS

        @block.sync
        def _(sp):
            sp.dma_start(cT[:, :, :], c_T).then_inc(cT_loaded, 16)
            mod_v = w_mod.rearrange("(k p) n -> p k n", p=P)

            def load_mod(v, dst):
                sp.dma_start(dst, mod_v[:, :, v * D:(v + 1) * D]).then_inc(wmod_loaded[v], 16)

            def load_x(b):
                for g in range(NG):
                    sp.dma_start(x_sb[:, g], tiles(x_in, NG * b + g)).then_inc(x_loaded[g], 16)

            def load_qkv(head, par):
                sp.dma_start(wqkv_raw[:, par].rearrange("p k c n -> p (k c n)"),
                             w_attn[bass.ds(head, 1), :, 0:3 * D].rearrange("o p n -> p (o n)")) \
                  .then_inc(wqkv_loaded[par], 16)

            def load_wo(head, par):
                sp.dma_start(wo_raw[:, par], w_attn[bass.ds(head, 1), :, 3 * D:4 * D].rearrange("o p n -> p (o n)")) \
                  .then_inc(wo_loaded[par], 16)

            def stream(U, head_qkv, head_wo, par):
                if head_qkv is not None:
                    sp.wait_ge(wqkv_split, 3 * U + 6)
                    load_qkv(head_qkv, 1 - par)
                if head_wo is not None:
                    sp.wait_ge(wo_split, U + 1)
                    load_wo(head_wo, par)

            for v in range(2):
                load_mod(v, wmod[:, v])
            load_x(0)
            for head in range(2):
                load_qkv(head, head)
                load_wo(head, head)
            load_mod(2, wmod[:, 2])
            sp.wait_ge(wqkv_split, 3)
            load_qkv(2, 0)
            for b in range(B):
                u0 = b * UNITS
                with sp.Fori(0, UNITS // 2 - 2) as it:
                    for par in range(2):
                        stream(u0 + 2 * it + par, 2 * it + par + 3, 2 * it + par + 2, par)
                more = b + 1 < B
                stream(u0 + UNITS - 4, UNITS - 1, UNITS - 2, 0)
                stream(u0 + UNITS - 3, 0 if more else None, UNITS - 1, 1)
                if more:
                    stream(u0 + UNITS - 2, 1, 0, 0)
                    sp.wait_ge(score_done, QT * (u0 + UNITS - 1))
                    load_x(b + 1)
                    stream(u0 + UNITS - 1, 2, 1, 1)
                else:
                    sp.wait_ge(proj_done, 6 * ATT)
                    sp.wait_ge(score_done, QT * (ATT - 1))
                    sp.dma_start(xb[:, 0], tiles(x_in, 0)).then_inc(xb_loaded[0], 16)
                    sp.dma_start(yb[0], tiles(y_dram, 0)).then_inc(yb_loaded[0], 16)
                    load_mod(3, wmod2[:, 0])
                    load_mod(4, wmod2[:, 1])
                    sp.dma_start(xb[:, 1], tiles(x_in, 1)).then_inc(xb_loaded[1], 16)
                    load_mod(5, wmod2[:, 2])
                for g in range(NG):
                    sp.wait_ge(y_ready, QT * b + TPG * (g + 1))
                    sp.dma_start(tiles(y_dram, NG * b + g), acc[:, TPG * g:TPG * (g + 1), :]).then_inc(y_stored, 16)

            sp.wait_ge(y_stored, 16 * TG)
            sp.dma_start(yb[1], tiles(y_dram, 1)).then_inc(yb_loaded[1], 16)

            def load_shared(m):
                sp.dma_start(wf_raw[:, 0, :], w_shared_up[m]).then_inc(wf_loaded, 16)
                sp.dma_start(wf_raw[:, 1, :], w_shared_down[m]).then_inc(wf_loaded, 16)

            load_shared(0)
            sp.dma_start(wr_raw[:, :, :], w_router).then_inc(small_loaded, 16)
            sp.dma_start(br[:, :], b_router).then_inc(small_loaded, 16)
            sp.dma_start(bsu[:, :, :], b_shared_up).then_inc(small_loaded, 16)
            for part in range(3):
                sp.dma_start(bd_raw[part * NB:(part + 1) * NB, :], b_down).then_inc(small_loaded, 16)
            for tg in range(TG):
                sp.wait_ge(x2_ready, tg + 1)
                sp.dma_start(tiles(x2_dram, tg), yb[tg % 2]).then_inc(x2_stored, 16)
                if tg + 2 < TG:
                    sp.wait_ge(lnT_done, DC * (TG + tg + 1))
                    sp.dma_start(xb[:, tg % 2], tiles(x_in, tg + 2)).then_inc(xb_loaded[tg % 2], 16)
                    sp.wait_ge(x2_stored, 16 * (tg + 1))
                    sp.wait_ge(xn_ready, TPG * (TG + tg + 1))
                    sp.dma_start(yb[tg % 2], tiles(y_dram, tg + 2)).then_inc(yb_loaded[tg % 2], 16)
                if tg == 1:
                    sp.wait_ge(gd_split, 1)
                    load_shared(1)
            sp.wait_ge(gd_split, NSH)
            with sp.Fori(0, NR) as n:
                sp.wait_ge(up_split, n + 1)
                sp.dma_start(wf_land[:, :], w_routed[bass.ds(n, 1)].rearrange("o p f -> p (o f)")) \
                  .then_inc(wf_loaded, 32)
            sp.wait_ge(x2_stored, 16 * TG)
            sp.wait_ge(down_done, NT * (NM - 1))
            for tg in range(2):
                sp.dma_start(x2b[:, tg % 2], tiles(x2_dram, tg)).then_inc(x2b_loaded[tg % 2], 16)
            for tg in range(TG):
                halves = 2 if tg == TG - 1 else 1
                for half in range(halves):
                    n = TPG // halves
                    t = TPG * tg + n * half
                    sp.wait_ge(out_ready, t + n)
                    sp.dma_start(tiles(out, tg)[:, n * half:n * (half + 1), :], F[:, t:t + n, :]) \
                      .then_inc(out_stored, 16)
                if tg + 2 < TG:
                    sp.dma_start(x2b[:, tg % 2], tiles(x2_dram, tg + 2)).then_inc(x2b_loaded[tg % 2], 16)
            sp.wait_ge(out_stored, 16 * (TG + 1))

        @block.gpsimd
        def _(pool):
            nc.gpsimd.memset(ident[:, :], 0.0).then_inc(ident_0, 1)
            nc.gpsimd.memset(causal[:, :], 0.0).then_inc(ident_0, 1)
            nc.gpsimd.memset(tril[:, :, :], 1.0).then_inc(ident_0, 1)
            nc.gpsimd.memset(ones, 1.0).then_inc(ident_0, 1)
            pool.wait_ge(ident_0, 4)
            nc.gpsimd.affine_select(out=ident[:, :], in_=ident[:, :], compare_op=ALU.not_equal, fill=1.0, base=0,
                                    pattern=[[-1, P]], channel_multiplier=1).then_inc(const_done, 1)
            nc.gpsimd.affine_select(out=causal[:, :], in_=causal[:, :], compare_op=ALU.is_ge, fill=MASKED, base=0,
                                    pattern=[[-1, P]], channel_multiplier=1).then_inc(const_done, 1)
            nc.gpsimd.affine_select(out=tril[:, :, :], in_=tril[:, :, :], compare_op=ALU.is_gt, fill=0.0, base=0,
                                    pattern=[[1, E], [-1, E]], channel_multiplier=0).then_inc(const_done, 1)
            nc.gpsimd.memset(rest_rows[:, :], -1.0).then_inc(ident_0, 1)
            pool.wait_ge(ident_0, 5)
            nc.gpsimd.affine_select(out=rest_rows[:, :], in_=rest_rows[:, :], compare_op=ALU.is_ge, fill=0.0,
                                    base=-NB, pattern=[[-1, 1]], channel_multiplier=1).then_inc(const_done, 1)
            pool.wait_ge(const_done, 4)
            nc.gpsimd.affine_select(out=rest_rows[:, :], in_=rest_rows[:, :], compare_op=ALU.is_ge, fill=0.0,
                                    base=2 * NB - 1, pattern=[[-1, 1]], channel_multiplier=-1) \
              .then_inc(const_done, 1)

            def round_to(hi, raw):
                return nc.gpsimd.tensor_tensor(hi, raw, ones.to_broadcast(list(raw.shape)), ALU.mult)

            def split_qkv(unit, par, loads, first=False):
                for k in range(3):
                    if k == 0:
                        pool.wait_ge(wqkv_loaded[par], 16 * loads)
                    if not first:
                        pool.wait_ge(proj_done, 6 * unit - 6 + 2 * k + 2)
                    round_to(wqkv_hi[:, k], wqkv_raw[:, par, k]).then_inc(wqkv_rounded, 1)
                    pool.wait_ge(wqkv_rounded, 3 * unit + k + 1)
                    nc.gpsimd.tensor_tensor(wqkv_lo[:, k], wqkv_raw[:, par, k], wqkv_hi[:, k].bitcast(F32),
                                            ALU.subtract).then_inc(wqkv_split, 1)

            def split_wo(unit, par, loads, first=False):
                pool.wait_ge(wo_loaded[par], 16 * loads)
                if not first:
                    pool.wait_ge(wo_done, QT * unit)
                round_to(wo_hi[:, None, :], wo_raw[:, par:par + 1]).then_inc(wo_rounded, 1)
                pool.wait_ge(wo_rounded, unit + 1)
                nc.gpsimd.tensor_tensor(wo_lo[:, :], wo_raw[:, par], wo_hi[:, :].bitcast(F32),
                                        ALU.subtract).then_inc(wo_split, 1)

            half = UNITS // 2
            for b in range(B):
                u0 = b * UNITS
                if b == 0:
                    split_qkv(0, 0, 1, first=True)
                else:
                    pool.wait_ge(y_stored, 16 * NG * b)
                nc.gpsimd.memset(acc[:, :, :], 0.0).then_inc(acc_zeroed, 1)
                split_qkv(u0 + 1, 1, b * half + 1)
                split_wo(u0, 0, b * half + 1, first=(b == 0))
                with pool.Fori(0, half - 1) as it:
                    split_qkv(u0 + 2 + 2 * it, 0, b * half + it + 2)
                    split_wo(u0 + 1 + 2 * it, 1, b * half + it + 1)
                    split_qkv(u0 + 3 + 2 * it, 1, b * half + it + 2)
                    split_wo(u0 + 2 + 2 * it, 0, b * half + it + 2)
                if b + 1 < B:
                    split_qkv(u0 + UNITS, 0, (b + 1) * half + 1)
                split_wo(u0 + UNITS - 1, 1, (b + 1) * half)

            pool.wait_ge(small_loaded, 16 * 6)
            round_to(wr_hi[:, :, :], wr_raw[:, :, :]).then_inc(wr_rounded, 1)
            pool.wait_ge(wr_rounded, 1)
            nc.gpsimd.tensor_tensor(wr_lo[:, :, :], wr_raw[:, :, :], wr_hi[:, :, :].bitcast(F32),
                                    ALU.subtract).then_inc(wr_split, 1)

            def split_slice(m, par):
                pool.wait_ge(wf_loaded, 32 * m + 32)
                hi, lo = w_gd[par]
                round_to(hi[:, :, :], wf_raw[:, 0:2]).then_inc(gd_rounded, 1)
                pool.wait_ge(gd_rounded, m + 1)
                nc.gpsimd.tensor_tensor(lo[:, :, :], wf_raw[:, 0:2], hi[:, :, :].bitcast(F32), ALU.subtract) \
                  .then_inc(gd_split, 1)

            def split_up(n, par):
                hi, lo = w_up[par]
                round_to(hi[:, :, :], wf_raw[:, 2:3]).then_inc(up_rounded, 1)
                round_to(bgu[par][:, :, :], bgu_raw).then_inc(bgu_ready, 1)
                pool.wait_ge(up_rounded, n + 1)
                pool.wait_ge(gd_split, n + NSH + 1)
                nc.gpsimd.tensor_tensor(lo[:, :, :], wf_raw[:, 2:3], hi[:, :, :].bitcast(F32), ALU.subtract) \
                  .then_inc(up_split, 1)

            for m in range(NSH):
                split_slice(m, m % 2)
            nc.gpsimd.memset(ones, 1.0).then_inc(up_split, 1)
            pool.wait_ge(mix_ready, 2)
            with pool.Fori(0, NR // 2) as it:
                for par in range(2):
                    m = 2 * it + par + NSH
                    pool.wait_ge(down_done, NT * (m - 1))
                    split_slice(m, par)
                    split_up(2 * it + par, par)

        @block.scalar
        def _(act):
            nc_act = nc.scalar
            act.wait_ge(cT_loaded, 16)
            nc_act.activation(sc[:, :, :], cT[:, :, :], ACT.Exp, scale=-1.0).then_inc(silu_exp, 1)

            def layer_norm_sd(G):
                act.wait_ge(ln_var, G + 1)
                nc_act.activation(sd[:, G], sd[:, G], ACT.Sqrt).then_inc(ln_sd, 1)

            def layer_norm_out(G, dst_hi, col, banks, vec, b, chunks=range(DC)):
                for dc in chunks:
                    act.wait_ge(lnT_done, DC * G + dc + 1)
                    bank = banks[dc % len(banks)]
                    nc_act.activation(bank, bank, ACT.Identity, bias=mod_cols[:, vec * DC + dc, b:b + 1],
                                      scale=mod_cols[:, (vec + 1) * DC + dc, b:b + 1]).then_inc(ln_affine, 1)
                    act.wait_ge(ln_affine, DC * G + dc + 1)
                    nc_act.activation(dst_hi[:, dc, col:col + W], bank, ACT.Copy).then_inc(ln_hi, 1)

            def proj_hi(unit, par, k, banks=[ps_g[n][:, :] for n in PROJ_BANK]):
                act.wait_ge(proj_done, 6 * unit + k + 1)
                g = k % NG
                bank = banks[k]
                if k < 4:
                    dst = (q_hi, k_hi)[k // 2][par]
                    nc_act.activation(dst[:, g * W:(g + 1) * W], bank, ACT.Copy,
                                      scale=SCALE if k < 2 else 1.0).then_inc(qk_hi_done, 1)
                else:
                    nc_act.activation(vT[:, g, :], bank, ACT.Copy).then_inc(vT_copied, 1)

            def v_round(unit, par, g, bank):
                act.wait_ge(vtr_done, 2 * unit + g + 1)
                nc_act.activation(v_hi[par][:, 4 * g:4 * g + 4, :], bank.rearrange("p (j h) -> p j h", h=P),
                                  ACT.Copy).then_inc(v_hi_done, 1)

            def softmax_exp(unit, par, i):
                act.wait_ge(rowmax, QT * unit + i + 1)
                pieces, n = score_pieces(i)
                nc_act.activation(probs[:, i % 2, 0:pieces * n].rearrange("p (a n) -> p a n", n=n),
                                  ps_s[i % 2][:, 0:pieces, 0:n], ACT.Exp, bias=nmax[:, i:i + 1],
                                  accum_out=rsum[:, par, i:i + 1]).then_inc(exp_done, 1)

            def p_round(unit, i):
                for k in range(FIRST_PG[i], FIRST_PG[i + 1]):
                    _, j, n = P_GROUPS[k]
                    act.wait_ge(pT_done, NPG * unit + k + 1)
                    nc_act.activation(p_block(pT_hi, i, j, n), p_bank(k, n), ACT.Copy).then_inc(p_hi_done, 1)

            def z_round(unit, g):
                act.wait_ge(pv_done, 2 * unit + g + 1)
                nc_act.activation(z_hi[:, g * W:(g + 1) * W], ps_g[PV_BANK[g]][:, :], ACT.Copy) \
                      .then_inc(z_hi_done, 1)

            def slot(U, par, has_prev=True, has_next=True, also=lambda i: None):
                nxt = lambda k: proj_hi(U + 1, 1 - par, k) if has_next else None
                softmax_exp(U, par, 0)
                softmax_exp(U, par, 1)
                nxt(0)
                p_round(U, 0)
                softmax_exp(U, par, 2)
                if has_prev:
                    z_round(U - 1, 1)
                nxt(1)
                p_round(U, 1)
                softmax_exp(U, par, 3)
                nxt(2)
                p_round(U, 2)
                softmax_exp(U, par, 4)
                nxt(3)
                p_round(U, 3)
                also(3)
                softmax_exp(U, par, 5)
                nxt(4)
                p_round(U, 4)
                also(4)
                softmax_exp(U, par, 6)
                z_round(U, 0)
                p_round(U, 5)
                nxt(5)
                if has_next:
                    v_round(U + 1, 1 - par, 0, ps_t[0])
                softmax_exp(U, par, 7)
                p_round(U, 6)
                if has_next:
                    v_round(U + 1, 1 - par, 1, ps_t[1])
                p_round(U, 7)

            def next_sd(b):
                def also(i):
                    if b + 1 < B and i in (3, 4):
                        layer_norm_sd(NG * (b + 1) + i - 3)
                    elif b + 1 == B and i == 4:
                        layer_norm_sd(TG)
                return also

            for b in range(B):
                u0 = b * UNITS
                if b == 0:
                    for g in range(NG):
                        layer_norm_sd(g)
                    act.wait_ge(mod_read, 1)
                    layer_norm_out(0, hT_hi, 0, LN_BANKS[0], 0, 0)
                for g in range(1, NG):
                    layer_norm_out(NG * b + g, hT_hi, g * W, LN_BANKS[g], 0, b)
                for k in range(6):
                    proj_hi(u0, 0, k, FIRST_PROJ)
                for g in range(NG):
                    v_round(u0, 0, g, ps_t[g])
                slot(u0, 0, has_prev=False)
                with act.Fori(0, UNITS // 2 - 1) as it:
                    slot(u0 + 1 + 2 * it, 1)
                    slot(u0 + 2 + 2 * it, 0)
                slot(u0 + UNITS - 1, 1, has_next=False, also=next_sd(b))
                if b + 1 < B:
                    layer_norm_out(NG * (b + 1), hT_hi, 0, LN_BANKS[0], 0, b + 1)
                z_round(u0 + UNITS - 1, 1)

            def normalise(tg, chunks):
                layer_norm_out(TG + tg, h2_hi, tg * W, LN2_BANKS[min(tg, 1)], 2, tg // NG, chunks)

            def silu(step, c, bias, first=False):
                act.wait_ge(gate_done, HC * step + c + 1)
                if not first:
                    act.wait_ge(hid_lo_done, HC * step - HC + c + 1)
                nc_act.activation(hid[:, c, :], ps_gu[c][0], ACT.Silu, bias=bias(c)).then_inc(silu_done, 1)

            def hidden_hi(step, tg, shared=False):
                for c in range(HC):
                    if shared:
                        act.wait_ge(silu_done, HC * step + c + 1)
                    else:
                        act.wait_ge(hidden_ready, HC * step - HC * TG * NSH + c + 1)
                    nc_act.activation(hid_hi[tg % 2][:, c, :], hid[:, c, :], ACT.Copy).then_inc(hid_hi_done, 1)

            act.wait_ge(mod_read, 2 + B)
            act.wait_ge(y_stored, 16 * TG)
            normalise(0, range(DC))
            layer_norm_sd(TG + 1)
            act.wait_ge(small_loaded, 16 * 6)
            for tg in range(TG):
                for c in range(HC):
                    if tg + 1 < TG:
                        normalise(tg + 1, range(DC // HC * c, DC // HC * (c + 1)))
                    silu(tg, c, lambda c: bsu[:, 0, c:c + 1], first=(tg == 0))
                hidden_hi(tg, tg, shared=True)
                if tg + 2 < TG:
                    layer_norm_sd(TG + tg + 2)
                act.wait_ge(router_done, tg + 1)
                nc_act.activation(gateT[:, tg, :], ps_d[tg][0:E, :], ACT.Identity, bias=br[:, 0:1]) \
                      .then_inc(gateT_ready, 1)
            for m in range(1, NSH):
                for tg in range(TG):
                    if m == 1 and tg == 2:
                        act.wait_ge(route_shift, 1)
                        nc_act.activation(sel[:, :, :], gs[:, :, :], ACT.Exp).then_inc(route_exp, 1)
                    for c in range(HC):
                        silu(TG * m + tg, c, lambda c: bsu[:, m, c:c + 1])
                    hidden_hi(TG * m + tg, tg, shared=True)
            with act.Fori(0, NR // 2) as it:
                for par in range(2):
                    n = 2 * it + par
                    act.wait_ge(bgu_ready, n + 1)
                    for tg in range(TG):
                        for c in range(HC):
                            silu(TG * NSH + TG * n + tg, c, lambda c: bgu[par][:, 0, c:c + 1])
                        hidden_hi(TG * NSH + TG * n + tg, tg)

        @block.vector
        def _(dve):
            v = nc.vector
            dve.wait_ge(silu_exp, 1)
            v.tensor_scalar_add(sc[:, :, :], sc[:, :, :], 1.0).then_inc(silu_step, 1)
            dve.wait_ge(silu_step, 1)
            v.reciprocal(sc[:, :, :], sc[:, :, :]).then_inc(silu_step, 1)
            dve.wait_ge(silu_step, 2)
            v.tensor_tensor(sc[:, :, :], sc[:, :, :], cT[:, :, :], ALU.mult).then_inc(silu_step, 1)
            dve.wait_ge(silu_step, 3)
            for k in range(DC):
                for b in range(B):
                    v.tensor_copy(sc_wide[:, k * B + b, :], sc[:, k, b:b + 1].to_broadcast([P, P])) \
                     .then_inc(sc_ready, 1)

            def layer_norm_stats(G, src):
                for t in range(TPG):
                    v.bn_stats(st[:, G, t], src[:, t]).then_inc(ln_stat, 1)
                for t in range(TPG):
                    dve.wait_ge(ln_stat, TPG * G + t + 1)
                    v.bn_aggr(mv[:, G, t], st[:, G, t]).then_inc(ln_agg, 1)
                dve.wait_ge(ln_agg, TPG * (G + 1))
                v.tensor_scalar_add(sd[:, G], mv[:, G, :, 1], EPS).then_inc(ln_var, 1)

            def layer_norm_apply(G, src, dst):
                dve.wait_ge(ln_sd, G + 1)
                v.reciprocal(rstd[:, G], sd[:, G]).then_inc(ln_rstd, 1)
                dve.wait_ge(ln_rstd, G + 1)
                for t in range(TPG):
                    v.tensor_scalar(dst[:, t], src[:, t], mv[:, G, t, 0:1], rstd[:, G, t:t + 1],
                                    ALU.subtract, ALU.mult).then_inc(xn_ready, 1)

            def layer_norm_rest(G, dst_hi, dst_lo, col, banks, chunks=range(DC)):
                for dc in chunks:
                    dve.wait_ge(ln_hi, DC * G + dc + 1)
                    v.tensor_tensor(dst_lo[:, dc, col:col + W], banks[dc % len(banks)],
                                    dst_hi[:, dc, col:col + W].bitcast(F32), ALU.subtract).then_inc(ln_lo, 1)

            def modulation_columns(vecs, count, bank):
                dve.wait_ge(mod_done, count)
                mod_ps = bank[:, 0:4 * DC * B].rearrange("p (v b) -> p v b", b=B)
                for vec in vecs:
                    rows = slice(vec * DC, (vec + 1) * DC)
                    last = v.tensor_scalar_add(mod_cols[:, rows], mod_ps[:, rows], float(vec % 2))
                last.then_inc(mod_read, 1)

            def gate_row(n, dst, bank, count):
                dve.wait_ge(mod_done, count)
                v.tensor_scalar(dst, bank, 0.0, 2.0, ALU.is_ge, ALU.mult).then_inc(gate_step, 1)
                dve.wait_ge(gate_step, 3 * n + 1)
                v.tensor_scalar_add(dst, dst, -1.0).then_inc(gate_step, 1)
                dve.wait_ge(gate_step, 3 * n + 2)
                v.tensor_tensor(bank, bank, dst, ALU.mult).then_inc(gate_step, 1)
                dve.wait_ge(gate_step, 3 * n + 3)
                v.scalar_tensor_tensor(out=dst, in0=bank, scalar=0.25, in1=dst, op0=ALU.max, op1=ALU.mult) \
                 .then_inc(mod_read, 1)

            def proj_lo(unit, par, k, banks=[ps_g[n][:, :] for n in PROJ_BANK]):
                if k >= 4:
                    return
                dve.wait_ge(qk_hi_done, 4 * unit + k + 1)
                cols = slice((k % NG) * W, (k % NG + 1) * W)
                hi, lo = ((q_hi, q_lo), (k_hi, k_lo))[k // 2]
                v.scalar_tensor_tensor(out=lo[par][:, cols], in0=banks[k],
                                       scalar=SCALE if k < 2 else 1.0, in1=hi[par][:, cols].bitcast(F32),
                                       op0=ALU.mult, op1=ALU.subtract).then_inc(qk_lo_done, 1)

            def v_rest(unit, par, g, bank):
                dve.wait_ge(v_hi_done, 2 * unit + g + 1)
                rows = slice(4 * g, 4 * g + 4)
                v.tensor_tensor(v_lo[par][:, rows, :], bank.rearrange("p (j h) -> p j h", h=P),
                                v_hi[par][:, rows, :].bitcast(F32), ALU.subtract).then_inc(v_lo_done, 1)

            def row_max(unit, i):
                pieces, n = score_pieces(i)
                bank = ps_s[i % 2]
                at = P * i - (pieces - 1) * n
                dve.wait_ge(score_done, QT * unit + i + 1)
                diag = bank[:, pieces - 1, at:at + P]
                v.tensor_tensor(diag, diag, causal[:, :], ALU.add).then_inc(masked, 1)
                dve.wait_ge(masked, QT * unit + i + 1)
                v.tensor_reduce(nmax[:, i:i + 1], bank[:, 0:pieces, 0:n], AX.XY, ALU.max, negate=True) \
                 .then_inc(rowmax, 1)

            def p_rest(unit, i):
                for k in range(FIRST_PG[i], FIRST_PG[i + 1]):
                    _, j, n = P_GROUPS[k]
                    dve.wait_ge(p_hi_done, NPG * unit + k + 1)
                    v.tensor_tensor(p_block(pT_lo, i, j, n), p_bank(k, n), p_block(pT_hi, i, j, n).bitcast(F32),
                                    ALU.subtract).then_inc(p_lo_done, 1)

            def z_rest(unit, par, g):
                dve.wait_ge(z_hi_done, 2 * unit + g + 1)
                cols = slice(g * W, (g + 1) * W)
                v.tensor_tensor(z_lo[:, cols], ps_g[PV_BANK[g]][:, :], z_hi[:, cols].bitcast(F32),
                                ALU.subtract).then_inc(z_lo_done, 1)
                dve.wait_ge(exp_done, QT * unit + TPG * (g + 1))
                v.reciprocal(rinv[:, par, TPG * g:TPG * (g + 1)], rsum[:, par, TPG * g:TPG * (g + 1)]) \
                 .then_inc(rinv_ready, 1)

            def add_out(unit, par, t):
                dve.wait_ge(wo_done, QT * unit + t + 1)
                dve.wait_ge(rinv_ready, 2 * unit + t // TPG + 1)
                v.scalar_tensor_tensor(out=acc[:, t], in0=ps_g[WO_BANK[t]][:, :], scalar=rinv[:, par, t:t + 1],
                                       in1=acc[:, t], op0=ALU.mult, op1=ALU.add).then_inc(acc_done, 1)

            def slot(U, par, has_prev=True, has_next=True, also=lambda i: None):
                nxt = lambda k: proj_lo(U + 1, 1 - par, k) if has_next else None
                prev = lambda t: add_out(U - 1, 1 - par, t) if has_prev else None
                row_max(U, 1)
                nxt(0)
                p_rest(U, 0)
                also(0)
                row_max(U, 2)
                if has_prev:
                    z_rest(U - 1, 1 - par, 1)
                nxt(1)
                prev(4)
                p_rest(U, 1)
                also(1)
                row_max(U, 3)
                prev(5)
                nxt(2)
                prev(6)
                p_rest(U, 2)
                also(2)
                row_max(U, 4)
                prev(7)
                nxt(3)
                p_rest(U, 3)
                also(3)
                row_max(U, 5)
                p_rest(U, 4)
                also(4)
                row_max(U, 6)
                z_rest(U, par, 0)
                p_rest(U, 5)
                also(5)
                row_max(U, 7)
                if has_next:
                    v_rest(U + 1, 1 - par, 0, ps_t[0])
                add_out(U, par, 0)
                add_out(U, par, 1)
                p_rest(U, 6)
                also(6)
                add_out(U, par, 2)
                if has_next:
                    v_rest(U + 1, 1 - par, 1, ps_t[1])
                    row_max(U + 1, 0)
                add_out(U, par, 3)
                p_rest(U, 7)
                also(7)

            def add_x(tg):
                dve.wait_ge(xb_loaded[tg % 2], 16 * (tg // 2 + 1))
                dve.wait_ge(yb_loaded[tg % 2], 16 * (tg // 2 + 1))
                v.tensor_tensor(yb[tg % 2], yb[tg % 2], xb[:, tg % 2], ALU.add).then_inc(x2_ready, 1)
                dve.wait_ge(x2_ready, tg + 1)
                layer_norm_stats(TG + tg, yb[tg % 2])

            def ahead(b):
                def also(i):
                    if b + 1 < B:
                        if i in (1, 2):
                            dve.wait_ge(x_loaded[i - 1], 16 * (b + 2))
                            layer_norm_stats(NG * (b + 1) + i - 1, x_sb[:, i - 1])
                        if i in (4, 5):
                            layer_norm_apply(NG * (b + 1) + i - 4, x_sb[:, i - 4], x_sb[:, i - 4])
                    else:
                        if i == 2:
                            add_x(0)
                        if i == 4:
                            modulation_columns((2, 3), 2 + B, ps_g[0][:, :])
                        if i == 5:
                            layer_norm_apply(TG, yb[0], xb[:, 0])
                return also

            for b in range(B):
                u0 = b * UNITS
                if b == 0:
                    for g in range(NG):
                        dve.wait_ge(x_loaded[g], 16)
                        layer_norm_stats(g, x_sb[:, g])
                    for g in range(NG):
                        layer_norm_apply(g, x_sb[:, g], x_sb[:, g])
                    modulation_columns((0, 1), 1, ps_t[0][:, :])
                    layer_norm_rest(0, hT_hi, hT_lo, 0, LN_BANKS[0])
                for g in range(1, NG):
                    layer_norm_rest(NG * b + g, hT_hi, hT_lo, g * W, LN_BANKS[g])
                if b > 0:
                    last = QT * u0 - QT
                    for t in range(QT):
                        dve.wait_ge(acc_done, last + t + 1)
                        v.tensor_tensor(acc[:, t], acc[:, t], ga_row[:, b - 1], ALU.mult).then_inc(y_ready, 1)
                for k in range(4):
                    proj_lo(u0, 0, k, FIRST_PROJ)
                for g in range(NG):
                    v_rest(u0, 0, g, ps_t[g])
                if b == 0:
                    for n in range(B):
                        gate_row(n, ga_row[:, n], ps_g[n % 2][:, :], 2 + n)
                row_max(u0, 0)
                dve.wait_ge(acc_zeroed, b + 1)
                slot(u0, 0, has_prev=False)
                with dve.Fori(0, UNITS // 2 - 1) as it:
                    slot(u0 + 1 + 2 * it, 1)
                    slot(u0 + 2 + 2 * it, 0)
                slot(u0 + UNITS - 1, 1, has_next=False, also=ahead(b))
                if b + 1 < B:
                    layer_norm_rest(NG * (b + 1), hT_hi, hT_lo, 0, LN_BANKS[0])
                z_rest(u0 + UNITS - 1, 1, 1)
                for t in range(TPG, QT):
                    add_out(u0 + UNITS - 1, 1, t)
            for t in range(QT):
                dve.wait_ge(acc_done, QT * (ATT - 1) + t + 1)
                v.tensor_tensor(acc[:, t], acc[:, t], ga_row[:, B - 1], ALU.mult).then_inc(y_ready, 1)

            def normalise_rest(tg):
                if tg == TG - 1:
                    dve.wait_ge(x2_stored, 16 * TG)
                layer_norm_rest(TG + tg, h2_hi, h2_lo, tg * W, LN2_BANKS[min(tg, 1)])

            def hidden(step, tg, par=None):
                if par is not None:
                    for c in range(HC):
                        dve.wait_ge(up_done, HC * step - HC * TG * NSH + c + 1)
                        dve.wait_ge(silu_done, HC * step + c + 1)
                        v.scalar_tensor_tensor(out=hid[:, c, :], in0=ps_gu[c][1],
                                               scalar=bgu[par][:, 1, c:c + 1],
                                               in1=hid[:, c, :], op0=ALU.add, op1=ALU.mult) \
                         .then_inc(hidden_ready, 1)
                for c in range(HC):
                    dve.wait_ge(hid_hi_done, HC * step + c + 1)
                    v.tensor_tensor(hid_lo[tg % 2][:, c, :], hid[:, c, :], hid_hi[tg % 2][:, c, :].bitcast(F32),
                                    ALU.subtract).then_inc(hid_lo_done, 1)

            def add_down(m, tg, col=None):
                for k in range(TPG):
                    t = TPG * tg + k
                    dve.wait_ge(down_done, NT * m + t + 1)
                    if col is None:
                        if m == 0:
                            v.tensor_copy(F[:, t], ps_d[k][:, :]).then_inc(F_added, 1)
                        else:
                            dve.wait_ge(F_added, NT * (m - 1) + t + 1)
                            v.tensor_tensor(F[:, t], F[:, t], ps_d[k][:, :], ALU.add).then_inc(F_added, 1)
                    else:
                        dve.wait_ge(F_added, NT * m - NT + t + 1)
                        v.scalar_tensor_tensor(out=F[:, t], in0=ps_d[k][:, :],
                                               scalar=mix[:, t, bass.ds(col, 1)], in1=F[:, t],
                                               op0=ALU.mult, op1=ALU.add).then_inc(F_added, 1)

            def split_biases():
                dve.wait_ge(small_loaded, 16 * 6)
                v.tensor_copy(bd[:, :], bd_raw[:, :]).then_inc(bd_step, 1)
                dve.wait_ge(bd_step, 1)
                dve.wait_ge(const_done, 5)
                v.scalar_tensor_tensor(out=bd_raw[:, :], in0=bd[:, :].bitcast(F32), scalar=rest_rows[0:3 * NB, :],
                                       in1=bd_raw[:, :], op0=ALU.mult, op1=ALU.add).then_inc(bd_step, 1)
                dve.wait_ge(bd_step, 2)
                v.tensor_copy(bd[:, :], bd_raw[:, :]).then_inc(bd_step, 1)

            def route():
                done = 1

                def after():
                    nonlocal done
                    dve.wait_ge(route_step, done)
                    done += 1

                gt, eq = (route_tmp[:, k * NT * E * E:(k + 1) * NT * E * E].rearrange("p (t i j) -> p t i j", i=E, j=E)
                          for k in range(2))
                g_j = gs[:, :, None, :].to_broadcast([P, NT, E, E])
                g_i = gs[:, :, :, None].to_broadcast([P, NT, E, E])
                after()
                v.tensor_tensor(eq, g_j, g_i, ALU.is_equal).then_inc(route_step, 1)
                after()
                v.tensor_tensor(eq, eq, tril[:, None, :, :].to_broadcast([P, NT, E, E]), ALU.mult) \
                 .then_inc(route_step, 1)
                after()
                v.tensor_tensor(gt, g_j, g_i, ALU.is_gt).then_inc(route_step, 1)
                after()
                v.tensor_tensor(gt, gt, eq, ALU.add).then_inc(route_step, 1)
                after()
                v.tensor_reduce(rank[:, :, :], gt, AX.X, ALU.add).then_inc(route_step, 1)
                after()
                v.tensor_reduce(gm[:, :], gs[:, :, :], AX.X, ALU.max).then_inc(route_step, 1)
                after()
                v.tensor_tensor(gs[:, :, :], gs[:, :, :], gm[:, :, None].to_broadcast([P, NT, E]), ALU.subtract) \
                 .then_inc(route_shift, 1)
                v.tensor_scalar(rank[:, :, :], rank[:, :, :], float(TOPK), None, ALU.is_lt).then_inc(route_step, 1)
                after()
                dve.wait_ge(route_exp, 1)
                v.tensor_tensor(rank[:, :, :], rank[:, :, :], sel[:, :, :], ALU.mult).then_inc(route_step, 1)
                after()
                v.tensor_reduce(gsum[:, :], rank[:, :, :], AX.X, ALU.add).then_inc(route_step, 1)
                after()
                v.reciprocal(ginv[:, :], gsum[:, :]).then_inc(route_step, 1)
                after()
                v.memset(mix[:, :, 0:1], 1.0).then_inc(mix_ready, 1)
                v.tensor_tensor(mix[:, :, 1:1 + NR], rank[:, :, 0:NR], ginv[:, :, None].to_broadcast([P, NT, NR]),
                                ALU.mult).then_inc(mix_ready, 1)
                dve.wait_ge(mix_ready, 2)
                for part in range(2):
                    v.tensor_copy(mix3[:, :, part * NB:(part + 1) * NB], mix[:, :, :]).then_inc(mix3_step, 1)
                dve.wait_ge(mix3_step, 2)
                v.tensor_tensor(mix3[:, :, 2 * NB:3 * NB], mix[:, :, :], mix3[:, :, 0:NB].bitcast(F32),
                                ALU.subtract).then_inc(mix3_step, 1)

            dve.wait_ge(y_stored, 16 * TG)
            add_x(1)
            normalise_rest(0)
            layer_norm_apply(TG + 1, yb[1], xb[:, 1])
            for tg in range(TG):
                if tg + 1 < TG:
                    normalise_rest(tg + 1)
                if tg + 2 < TG:
                    add_x(tg + 2)
                hidden(tg, tg)
                if tg + 2 < TG:
                    layer_norm_apply(TG + tg + 2, yb[tg % 2], xb[:, tg % 2])
                if tg == 0:
                    for n in range(B):
                        gate_row(B + n, gb_row[:, n], ps_g[n][:, :], 3 + B + n)
                else:
                    add_down(0, tg - 1)
            split_biases()
            dve.wait_ge(gateT_back, 1)
            v.tensor_copy(gs[:, :, :], ps_d[0][:, 0:NT * E].rearrange("p (t e) -> p t e", e=E)) \
             .then_inc(route_step, 1)
            for step in range(TG, NSH * TG):
                hidden(step, step % TG)
                if step == NSH * TG - 1:
                    for tg in range(TG):
                        dve.wait_ge(mixT_done, tg + 1)
                        v.tensor_copy(wT[:, tg, :], ps_gu[tg % 2][1][0:3 * NB, :]).then_inc(mixT_read, 1)
                add_down((step - 1) // TG, (step - 1) % TG)
                if step == TG + 1:
                    route()
            for t in range(NT):
                dve.wait_ge(bias_done, t + 1)
                dve.wait_ge(F_added, NT * (NSH - 1) - TPG + t + 1 if t >= NT - TPG else NT * (NSH - 1) + t + 1)
                v.tensor_tensor(F[:, t], F[:, t], ps_d[t % TPG][:, :], ALU.add).then_inc(bias_added, 1)

            def finish(tg):
                dve.wait_ge(x2b_loaded[tg % 2], 16 * (tg // 2 + 1))
                for t in range(TPG * tg, TPG * (tg + 1)):
                    dve.wait_ge(F_added, NT * (NM - 1) + t + 1)
                    v.tensor_tensor(F[:, t], F[:, t], gb_row[:, tg // NG], ALU.mult).then_inc(F_scaled, 1)
                for t in range(TPG * tg, TPG * (tg + 1)):
                    dve.wait_ge(F_scaled, t + 1)
                    v.tensor_tensor(F[:, t], F[:, t], x2b[:, tg % 2, t % TPG], ALU.add).then_inc(out_ready, 1)

            def expert(n, m, par, last=False):
                for tg in range(TG):
                    hidden(TG * m + tg, tg, par)
                    if tg == 0:
                        add_down(m - 1, TG - 1, n)
                    else:
                        add_down(m, tg - 1, n + 1)
                        if last:
                            finish(tg - 1)

            with dve.Fori(0, NR // 2 - 1) as it:
                for par in range(2):
                    n = 2 * it + par
                    dve.wait_ge(bgu_ready, n + 1)
                    expert(n, NSH + n, par)
            for par in range(2):
                n = NR - 2 + par
                dve.wait_ge(bgu_ready, n + 1)
                expert(n, NSH + n, par, last=(n == NR - 1))
            add_down(NM - 1, TG - 1, NR)
            finish(TG - 1)

        @block.tensor
        def _(pe):
            mm = nc.tensor.matmul

            def product(out, stat, mov, first, last):
                mm(out, stat[0], mov[0], start=first, stop=False)
                mm(out, stat[0], mov[1], start=False, stop=False)
                return mm(out, stat[1], mov[0], start=False, stop=last)

            pe.wait_ge(sc_ready, DC * B)
            pe.wait_ge(const_done, 3)
            order = [0, 1, 3, 4]

            def mod_columns(n, w, bank):
                mod_ps = bank[:, 0:4 * DC * B].rearrange("p (v b) -> p v b", b=B)
                pe.wait_ge(wmod_loaded[order[n]], 16)
                for dc in range(DC):
                    for k in range(DC):
                        last = mm(mod_ps[:, n * DC + dc, :], w[:, k, dc * P:(dc + 1) * P],
                                  sc[:, k, :], start=(k == 0), stop=(k == DC - 1))
                return last

            def mod_row(vec, b, w, bank):
                pe.wait_ge(wmod_loaded[vec], 16)
                for k in range(DC):
                    last = mm(bank, sc_wide[:, k * B + b, :], w[:, k, :], start=(k == 0), stop=(k == DC - 1))
                last.then_inc(mod_done, 1)

            def layer_norm_transpose(G, src, banks, used, chunks=range(DC)):
                for dc in chunks:
                    used(dc)
                    for t in range(TPG):
                        if dc == 0:
                            pe.wait_ge(xn_ready, TPG * G + t + 1)
                        last = nc.tensor.transpose(banks[dc % len(banks)][:, t * P:(t + 1) * P],
                                                   src[:, t, dc * P:(dc + 1) * P], ident[:, :])
                    last.then_inc(lnT_done, 1)

            def project(unit, par, k, banks=[ps_g[n][:, :] for n in PROJ_BANK]):
                g = k % NG
                pe.wait_ge(wqkv_split, 3 * unit + k // 2 + 1)
                for dc in range(DC):
                    last = product(banks[k], (wqkv_hi[:, k // 2, dc], wqkv_lo[:, k // 2, dc]),
                                   [h[:, dc, g * W:(g + 1) * W] for h in (hT_hi, hT_lo)], dc == 0, dc == DC - 1)
                last.then_inc(proj_done, 1)

            def v_transpose(unit, g, bank):
                pe.wait_ge(vT_copied, 2 * unit + g + 1)
                for j in range(4):
                    last = nc.tensor.transpose(bank[:, j * P:(j + 1) * P], vT[:, g, j * P:(j + 1) * P], ident[:, :])
                last.then_inc(vtr_done, 1)

            def scores(unit, par, i):
                if i == 0:
                    pe.wait_ge(qk_lo_done, 4 * unit + 4)
                pieces, n = score_pieces(i)
                cols = slice(i * P, (i + 1) * P)
                for piece, (s, m) in enumerate(((q_hi, k_hi), (q_hi, k_lo), (q_lo, k_hi))):
                    for a in range(pieces):
                        last = mm(ps_s[i % 2][:, a, 0:n], s[par][:, cols], m[par][:, a * n:(a + 1) * n],
                                  start=(piece == 0), stop=(piece == 2))
                last.then_inc(score_done, 1)

            def p_transpose(unit, i, used):
                pe.wait_ge(exp_done, QT * unit + i + 1)
                for k in range(FIRST_PG[i], FIRST_PG[i + 1]):
                    _, j0, n = P_GROUPS[k]
                    used(k)
                    for j in range(n):
                        last = nc.tensor.transpose(ps_t[P_BANK[k]][:, j * P:(j + 1) * P],
                                                   probs[:, i % 2, (j0 + j) * P:(j0 + j + 1) * P], ident[:, :])
                    last.then_inc(pT_done, 1)

            def values(unit, par, g):
                pe.wait_ge(p_lo_done, NPG * unit + FIRST_PG[4 * (g + 1)])
                if g == 0:
                    pe.wait_ge(v_lo_done, 2 * unit + 2)
                nj = 4 * (g + 1)
                for j in range(nj):
                    c0 = max(0, j - 4 * g) * P
                    last = product(ps_g[PV_BANK[g]][:, c0:W], (v_hi[par][:, j], v_lo[par][:, j]),
                                   (pT_hi[g][:, j, c0:W], pT_lo[g][:, j, c0:W]), j == 0, j == nj - 1)
                last.then_inc(pv_done, 1)

            def out_proj(unit, t):
                if t == 0:
                    pe.wait_ge(wo_split, unit + 1)
                if t % TPG == 0:
                    pe.wait_ge(z_lo_done, 2 * unit + t // TPG + 1)
                cols = slice(t * P, (t + 1) * P)
                product(ps_g[WO_BANK[t]][:, :], (z_hi[:, cols], z_lo[:, cols]), (wo_hi[:, :], wo_lo[:, :]),
                        True, True).then_inc(wo_done, 1)

            def proj_read(unit, k):
                if k < 4:
                    pe.wait_ge(qk_lo_done, 4 * unit + k + 1)
                else:
                    pe.wait_ge(vT_copied, 2 * unit + k - 3)

            def z_read(unit, g):
                pe.wait_ge(z_lo_done, 2 * unit + g + 1)

            def out_read(unit, t):
                pe.wait_ge(acc_done, QT * unit + t + 1)

            def p_read(unit, k):
                pe.wait_ge(p_lo_done, NPG * unit + k + 1)

            def v_read(unit, g):
                pe.wait_ge(v_lo_done, 2 * unit + g + 1)

            def score_read(unit, i):
                pe.wait_ge(exp_done, QT * unit + i + 1)

            def slot(U, par, has_prev=True, has_next=True, also=None):
                N, Q = U + 1, 1 - par

                def p_used(k):
                    if k == 0:
                        if has_prev:
                            p_read(U - 1, NPG - 2)
                        else:
                            v_read(U, 0)
                    elif k == 1:
                        if has_prev:
                            p_read(U - 1, NPG - 1)
                        else:
                            v_read(U, 1)
                    elif k == 8:
                        p_read(U, 7)
                    elif k == 9:
                        v_read(N, 0) if has_next else p_read(U, 6)
                    elif k == 10:
                        p_read(U, 9)
                    elif k == 11:
                        v_read(N, 1) if has_next else p_read(U, 8)
                    else:
                        p_read(U, k - 2)

                if has_next:
                    if has_prev:
                        out_read(U - 1, 2)
                    else:
                        proj_read(U, 3)
                    project(N, Q, 0)
                p_transpose(U, 0, p_used)
                score_read(U, 0)
                scores(U, par, 2)
                if has_prev:
                    out_read(U - 1, 3)
                    values(U - 1, Q, 1)
                if has_next:
                    proj_read(N, 0)
                    project(N, Q, 1)
                if has_prev:
                    z_read(U - 1, 1)
                    out_proj(U - 1, 4)
                p_transpose(U, 1, p_used)
                score_read(U, 1)
                scores(U, par, 3)
                if has_prev:
                    if has_next:
                        proj_read(N, 1)
                    else:
                        out_read(U - 1, 2)
                    out_proj(U - 1, 5)
                if has_next:
                    if has_prev:
                        out_read(U - 1, 4)
                    else:
                        proj_read(U, 5)
                    project(N, Q, 2)
                if has_prev:
                    out_read(U - 1, 5)
                    out_proj(U - 1, 6)
                p_transpose(U, 2, p_used)
                score_read(U, 2)
                scores(U, par, 4)
                if has_prev:
                    if has_next:
                        proj_read(N, 2)
                    else:
                        out_read(U - 1, 4)
                    out_proj(U - 1, 7)
                if has_next:
                    if has_prev:
                        out_read(U - 1, 6)
                    else:
                        proj_read(N, 1)
                    project(N, Q, 3)
                elif also:
                    out_read(U - 1, 6)
                    also()
                p_transpose(U, 3, p_used)
                score_read(U, 3)
                scores(U, par, 5)
                if has_next:
                    if has_prev:
                        out_read(U - 1, 7)
                    else:
                        proj_read(N, 2)
                    project(N, Q, 4)
                p_transpose(U, 4, p_used)
                score_read(U, 4)
                scores(U, par, 6)
                if has_next:
                    proj_read(N, 3)
                elif also:
                    pe.wait_ge(mod_read, 2 + B)
                else:
                    out_read(U - 1, 6)
                values(U, par, 0)
                p_transpose(U, 5, p_used)
                score_read(U, 5)
                scores(U, par, 7)
                if has_next:
                    proj_read(N, 4)
                    project(N, Q, 5)
                    p_read(U, 6)
                    v_transpose(N, 0, ps_t[0])
                z_read(U, 0)
                out_proj(U, 0)
                if has_next:
                    proj_read(N, 5)
                else:
                    out_read(U - 1, 7)
                out_proj(U, 1)
                p_transpose(U, 6, p_used)
                out_read(U, 0)
                out_proj(U, 2)
                if has_next:
                    score_read(U, 6)
                    scores(N, Q, 0)
                    p_read(U, 8)
                    v_transpose(N, 1, ps_t[1])
                out_read(U, 1)
                out_proj(U, 3)
                p_transpose(U, 7, p_used)
                if has_next:
                    score_read(U, 7)
                    scores(N, Q, 1)

            for n in range(2):
                last = mod_columns(n, wmod[:, n], ps_t[0][:, :])
            last.then_inc(mod_done, 1)

            def normalised_T(b, g):
                G = NG * b + g

                def used(dc):
                    if g == 0:
                        if b > 0 and dc == 0:
                            score_read(UNITS * b - 1, QT - 1)
                    elif dc == 0:
                        if b == 0:
                            pe.wait_ge(mod_read, 1)
                        else:
                            p_read(UNITS * b - 1, NPG - 1)
                    elif dc >= 2:
                        pe.wait_ge(ln_lo, DC * (G - 1) + dc - 1)
                layer_norm_transpose(G, x_sb[:, g], LN_BANKS[g], used)

            def experts_mod():
                for n in range(2, 4):
                    last = mod_columns(n, wmod2[:, n - 2], ps_g[0][:, :])
                last.then_inc(mod_done, 1)

            for b in range(B):
                u0 = b * UNITS
                if b == 0:
                    normalised_T(0, 0)
                    normalised_T(0, 1)
                else:
                    out_read(u0 - 1, QT - 1)
                for k in range(6):
                    if k < NG:
                        pe.wait_ge(ln_lo, DC * (NG * b + k + 1))
                    project(u0, 0, k, FIRST_PROJ)
                for g in range(NG):
                    v_transpose(u0, g, ps_t[g])
                scores(u0, 0, 0)
                scores(u0, 0, 1)
                if b == 0:
                    proj_read(u0, 3)
                    for n in range(B):
                        mod_row(2, n, wmod[:, 2], ps_g[n][:, :])
                    pe.wait_ge(mod_read, 1 + B)
                slot(u0, 0, has_prev=False)
                with pe.Fori(0, UNITS // 2 - 1) as it:
                    slot(u0 + 1 + 2 * it, 1)
                    slot(u0 + 2 + 2 * it, 0)
                last = u0 + UNITS - 1
                slot(last, 1, has_next=False, also=None if b + 1 < B else experts_mod)
                if b + 1 < B:
                    normalised_T(b + 1, 0)
                out_read(last, 3)
                values(last, 1, 1)
                if b + 1 < B:
                    normalised_T(b + 1, 1)
                z_read(last, 1)
                out_proj(last, 4)
                out_proj(last, 5)
                out_read(last, 5)
                out_proj(last, 6)
                out_read(last, 4)
                out_proj(last, 7)

            def gate_chunk(step, par, tg, c, shared=False, first=False):
                for k in range(1 if shared else 2):
                    if not first:
                        pe.wait_ge((silu_done, hid_lo_done)[k], HC * step - HC + c + 1)
                    hi, lo = (w_gd, w_up)[k][par]
                    for dc in range(DC):
                        at = dc * HID + c * P
                        last = product(ps_gu[c][k], (hi[:, 0, at:at + P], lo[:, 0, at:at + P]),
                                       [h[:, dc, tg * W:(tg + 1) * W] for h in (h2_hi, h2_lo)],
                                       dc == 0, dc == DC - 1)
                    last.then_inc((gate_done, up_done)[k], 1)

            def gates_up(step, m, par, tg, shared=False):
                if tg == 0:
                    pe.wait_ge(gd_split, m + 1)
                    if not shared:
                        pe.wait_ge(up_split, m - NSH + 2)
                for c in range(HC):
                    gate_chunk(step, par, tg, c, shared)

            def down(step, m, par, tg):
                pe.wait_ge(hid_lo_done, HC * step + HC)
                for k in range(TPG):
                    if isinstance(m, int) and m == 0 and k == (tg + 1) % TG:
                        pe.wait_ge(gateT_ready, tg + 2 if tg + 1 < TG else TG)
                    if isinstance(m, int) and m == 0 and tg == TG - 1 and k == 0:
                        pe.wait_ge(route_step, 1)
                    if isinstance(m, int) and m == 0 and tg == 0:
                        if k == 0:
                            pe.wait_ge(gateT_ready, 1)
                            pe.wait_ge(mod_read, 2 + 2 * B)
                    else:
                        pe.wait_ge(F_added, NT * m + TPG * (tg - 1) + k + 1)
                    for c in range(HC):
                        last = product(ps_d[k][:, :], [h[tg % 2][:, c, k * P:(k + 1) * P] for h in (hid_hi, hid_lo)],
                                       [w[:, 1, c * D:(c + 1) * D] for w in w_gd[par]],
                                       c == 0, c == HC - 1)
                    last.then_inc(down_done, 1)

            def normalised2_T(tg, chunks):
                def used(dc):
                    if tg == 0:
                        if dc == 0:
                            score_read(ATT - 1, QT - 1)
                    elif tg == 1 and dc < 2:
                        pe.wait_ge(ln_lo, DC * (TG + tg - 1) + 2 * dc + 2)
                    else:
                        pe.wait_ge(ln_lo, DC * (TG + tg) + dc - 1)
                layer_norm_transpose(TG + tg, xb[:, tg % 2], LN2_BANKS[min(tg, 1)], used, chunks)

            def router(tg):
                if tg == 0:
                    pe.wait_ge(wr_split, 1)
                    p_read(ATT - 1, NPG - 1)
                elif tg > 1:
                    pe.wait_ge(F_added, TPG * (tg - 2) + tg + 1)
                for dc in range(DC):
                    last = product(ps_d[tg][0:E, :], (wr_hi[:, dc], wr_lo[:, dc]),
                                   [h[:, dc, tg * W:(tg + 1) * W] for h in (h2_hi, h2_lo)], dc == 0, dc == DC - 1)
                last.then_inc(router_done, 1)

            normalised2_T(0, range(DC))
            out_read(ATT - 1, QT - 1)
            for b in range(B):
                mod_row(5, b, wmod2[:, 2], ps_g[b][:, :])
            pe.wait_ge(gd_split, 1)
            for tg in range(TG):
                for c in range(HC):
                    if tg + 1 < TG:
                        normalised2_T(tg + 1, range(DC // HC * c, DC // HC * (c + 1)))
                    if c == 0:
                        pe.wait_ge(ln_lo, DC * (TG + tg + 1))
                    gate_chunk(tg, 0, tg, c, shared=True, first=(tg == 0))
                if tg == 2:
                    pe.wait_ge(mod_read, 2 + 2 * B)
                router(tg)
                if tg > 0:
                    down(tg - 1, 0, 0, tg - 1)
            pe.wait_ge(gateT_ready, TG)
            pe.wait_ge(F_added, NT - 2 * TPG + 1)
            gate_T = gateT[:, :, :].rearrange("e g w -> e (g w)")
            for t in range(NT):
                last = nc.tensor.transpose(ps_d[0][:, t * E:(t + 1) * E], gate_T[:, t * P:(t + 1) * P],
                                           ident[0:E, 0:E])
            last.then_inc(gateT_back, 1)
            for step in range(TG, NSH * TG):
                gates_up(step, step // TG, step // TG % 2, step % TG, shared=True)
                if step == NSH * TG - 1:
                    pe.wait_ge(mix3_step, 3)
                    for tg in range(TG):
                        if tg >= 2:
                            pe.wait_ge(mixT_read, tg - 1)
                        for t in range(TPG):
                            last = nc.tensor.transpose(ps_gu[tg % 2][1][0:3 * NB, t * P:(t + 1) * P],
                                                       mix3[:, TPG * tg + t, :].bitcast(F32), ident[:, :])
                        last.then_inc(mixT_done, 1)
                down(step - 1, (step - 1) // TG, (step - 1) // TG % 2, (step - 1) % TG)
            w_T = wT[:, :, :].rearrange("e g w -> e (g w)")
            pe.wait_ge(bd_step, 3)
            pe.wait_ge(mixT_read, TG)
            for t in range(NT):
                if t < TPG:
                    pe.wait_ge(F_added, NT * (NSH - 1) + NT - 2 * TPG + t + 1)
                else:
                    pe.wait_ge(bias_added, t - TPG + 1)
                mm(ps_d[t % TPG][:, :], w_T[:, t * P:(t + 1) * P], bd[:, :], start=True, stop=True) \
                  .then_inc(bias_done, 1)
            pe.wait_ge(bias_added, NT)
            with pe.Fori(0, NR // 2) as it:
                for par in range(2):
                    m = NSH + 2 * it + par
                    for tg in range(TG):
                        gates_up(TG * m + tg, m, par, tg)
                        if tg == 0:
                            down(TG * m - 1, m - 1, 1 - par, TG - 1)
                        else:
                            down(TG * m + tg - 1, m, par, tg - 1)
            down(TG * NM - 1, NM - 1, (NM - 1) % 2, TG - 1)


def kernel(**inputs):
    import numpy as np
    import concourse.bacc as bacc
    from concourse.bass_utils import run_bass_kernel_spmd as run

    a = {k.replace("L0_", ""): np.asarray(v) for k, v in inputs.items()}
    H, Dh, D = a["attn_W_Q"].shape
    DC = D // P
    NR, _, HID = a["ffn_Wgate"].shape
    HC = HID // P
    NSH = a["ffn_Ws_up"].shape[1] // HID
    E = a["ffn_Wg"].shape[1]

    def head_major(w):
        return w.transpose(0, 2, 1).reshape(H, DC, P, Dh).transpose(0, 2, 1, 3).reshape(H, P, DC * Dh)

    def chunked(w):
        n, rows, cols = w.shape
        return w.reshape(n, rows // P, P, cols).transpose(0, 2, 1, 3).reshape(n, P, -1)

    arrays = {
        "x_in": a["attn_x"],
        "w_attn": np.concatenate([head_major(a["attn_W_Q"]), head_major(a["attn_W_K"]), head_major(a["attn_W_V"]),
                                  a["attn_W_O"].T.reshape(H, P, D)], axis=2),
        "w_mod": a["wmod"],
        "c_T": a["c"].T.reshape(DC, P, -1).transpose(1, 0, 2),
        "w_router": a["ffn_Wg"].reshape(DC, P, E).transpose(1, 0, 2),
        "b_router": a["ffn_bg"].reshape(E, 1),
        "w_routed": np.concatenate([chunked(a["ffn_Wgate"]), chunked(a["ffn_Wdown"]), chunked(a["ffn_Wup"]),
                                    np.stack([a["ffn_bgate"], a["ffn_bup"]], 1).reshape(NR, 2 * HC, P)
                                    .transpose(0, 2, 1)], axis=2),
        "w_shared_up": chunked(a["ffn_Ws_up"].reshape(D, NSH, HID).transpose(1, 0, 2)),
        "w_shared_down": chunked(a["ffn_Ws_down"].reshape(NSH, HID, D)),
        "b_shared_up": a["ffn_bs_up"].reshape(NSH, HC, P).transpose(2, 0, 1),
        "b_down": np.concatenate([a["ffn_bs_down"][None], a["ffn_bdown"]]),
    }
    arrays = {k: np.ascontiguousarray(v) for k, v in arrays.items()}
    nc = bacc.Bacc("TRN2", target_bir_lowering=False, num_devices=1)
    args = [nc.dram_tensor(k, v.shape, mybir.dt.from_np(v.dtype), kind="ExternalInput").ap()
            for k, v in arrays.items()]
    out = nc.dram_tensor("out", arrays["x_in"].shape, F32, kind="ExternalOutput").ap()
    block_kernel(nc, *args, out)
    return run(nc, [arrays], core_ids=[0]).results[0]["out"]
```

```python
from contextlib import ExitStack

import concourse.bass as bass
from concourse import mybir

F32 = mybir.dt.float32
F32R = mybir.dt.float32r
ACT = mybir.ActivationFunctionType
ALU = mybir.AluOpType
AX = mybir.AxisListType

P = 128
EPS = 1e-5
MASKED = -1e10


def block_kernel(nc, x_in, w_attn, w_mod, c_T, w_router, b_router, w_routed, w_shared_up, w_shared_down,
                 b_shared_up, b_down, out):
    B, S, D = x_in.shape
    H = w_attn.shape[0]
    DC = D // P
    QT = S // P
    NT = B * QT
    W = 512
    NG = S // W
    TG = B * NG
    TPG = W // P
    E = b_router.shape[0]
    NR = w_routed.shape[0]
    NSH = w_shared_down.shape[0]
    NM = NSH + NR
    HC = w_shared_down.shape[2] // D
    HID = HC * P
    SCALE = float(P) ** -0.5
    TOPK = NR

    y_dram = nc.dram_tensor("y_scratch", (B, S, D), F32, kind="Internal").ap()
    x2_dram = nc.dram_tensor("x2_scratch", (B, S, D), F32, kind="Internal").ap()

    def tiles(dram, group):
        b, g = divmod(group, NG)
        return dram[b, g * W:(g + 1) * W, :].rearrange("(t p) d -> p t d", p=P)

    P_GROUPS = [(i, j, min(4, i + 1 - j)) for i in range(QT) for j in range(0, i + 1, 4)]
    NPG = len(P_GROUPS)
    GROUPS_OF = [[k for k, g in enumerate(P_GROUPS) if g[0] == i] for i in range(QT)]

    with ExitStack() as ctx:
        def sb(name, shape, dt, c=ctx):
            return c.enter_context(nc.sbuf_tensor(name, shape, dt))

        def sem(name):
            return ctx.enter_context(nc.semaphore(name))

        ident = sb("ident", [P, P], F32)
        causal = sb("causal", [P, P], F32)
        ones = sb("ones", [P, 1, 1], F32)[:, :, :]
        tril = sb("tril", [P, E, E], F32)
        mod_cols = sb("mod_cols", [P, 4 * DC, B], F32)
        rest_rows = sb("rest_rows", [P, 1], F32)
        cT = sb("cT", [P, DC, B], F32)
        sc = sb("sc", [P, DC, B], F32)
        sc_wide = sb("sc_wide", [P, DC * B, P], F32)
        NLN = 2 * TG
        st = sb("st", [P, NLN, TPG, 6], F32)
        mv = sb("mv", [P, NLN, TPG, 2], F32)
        sd = sb("sd", [P, NLN, TPG], F32)
        rstd = sb("rstd", [P, NLN, TPG], F32)
        shift = sb("shift", [P, NLN, TPG], F32)

        w_gd = [None, None]
        with ExitStack() as y:
            acc = sb("acc", [P, QT, D], F32, y)
        w_gd[1] = [sb(f"w_gd_{part}1", [P, 2, HC * D], F32R) for part in ("hi", "lo")]

        attn = ExitStack()
        hT_hi = sb("hT_hi", [P, DC, S], F32R, attn)
        hT_lo = sb("hT_lo", [P, DC, S], F32R, attn)
        with ExitStack() as ln:
            x_sb = sb("x_sb", [P, NG, TPG, D], F32, ln)

        def qk(par):
            return [sb(f"{name}{par}", [P, S], F32R, attn) for name in ("q_hi", "q_lo", "k_hi", "k_lo")]

        def values_sb(par):
            return [sb(f"{name}{par}", [P, QT, P], F32R, attn) for name in ("v_hi", "v_lo")]

        qk_even = qk(0)
        vT = sb("vT", [P, NG, W], F32, attn)
        wqkv_raw = sb("wqkv_raw", [P, 2, 3, DC, P], F32, attn)
        wqkv_hi = sb("wqkv_hi", [P, 3, DC, P], F32R, attn)
        wqkv_lo = sb("wqkv_lo", [P, 3, DC, P], F32R, attn)
        v_even = values_sb(0)
        wo_raw = sb("wo_raw", [P, 2, D], F32, attn)
        q_hi, q_lo, k_hi, k_lo = zip(qk_even, qk(1))
        v_hi, v_lo = zip(v_even, values_sb(1))
        wo_hi = sb("wo_hi", [P, D], F32R, attn)
        wo_lo = sb("wo_lo", [P, D], F32R, attn)
        probs = sb("probs", [P, 2, S], F32, attn)
        z_hi = sb("z_hi", [P, S], F32R, attn)
        z_lo = sb("z_lo", [P, S], F32R, attn)
        with ExitStack() as mod:
            wmod = sb("wmod", [P, 3, DC, D], F32, mod)
            mod_rows = sb("mod_rows", [B, 2, D], F32, mod)
        pT_hi = [sb(f"pT_hi{g}", [P, 4 * (g + 1), W], F32R, attn) for g in range(NG)]
        pT_lo = [sb(f"pT_lo{g}", [P, 4 * (g + 1), W], F32R, attn) for g in range(NG)]
        ga_row = sb("ga_row", [P, B, D], F32, attn)
        nmax = sb("nmax", [P, QT], F32, attn)
        rsum = sb("rsum", [P, 2, QT], F32, attn)
        rinv = sb("rinv", [P, 2, QT], F32, attn)
        attn.close()

        F = sb("F", [P, NT, D], F32)
        wmod2 = F[:, 0:3 * DC].rearrange("p (v k) d -> p v k d", k=DC)
        yb = F[:, 3 * TPG:4 * TPG]
        y_of = [yb, None] + [acc[:, TPG * g:TPG * (g + 1)] for g in range(NG)]
        with ExitStack() as ln:
            xb = sb("xb", [P, 2, TPG, D], F32, ln)
        w_up = [[sb(f"w_up_{part}{par}", [P, 1, HC * D], F32R) for part in ("hi", "lo")] for par in range(2)]
        route_tmp = xb[:, 0].rearrange("p t d -> p (t d)")
        wf_land = sb("wf_land", [P, 3 * HC * D + 2 * HC], F32)
        wf_raw = wf_land[:, 0:3 * HC * D].rearrange("p (a f) -> p a f", a=3)
        bgu_raw = wf_land[:, 3 * HC * D:].rearrange("p (a c) -> p a c", a=2)
        wr_raw = sb("wr_raw", [P, DC, E], F32)
        wr_hi = sb("wr_hi", [P, DC, E], F32R)
        wr_lo = sb("wr_lo", [P, DC, E], F32R)
        br = sb("br", [E, 1], F32)
        bsu = sb("bsu", [P, NSH, HC], F32)
        with ExitStack() as end:
            x2b = sb("x2b", [P, 2, TPG, D], F32, end)
        w_gd[0] = [sb(f"w_gd_{part}0", [P, 2, HC * D], F32R) for part in ("hi", "lo")]
        with ExitStack() as y:
            y_of[1] = sb("y_b1", [P, TPG, D], F32, y)[:, :, :]
        hid_hi, hid_lo = [None, None], [None, None]
        hid_hi[1] = sb("hid_hi1", [P, HC, W], F32R)
        hid_lo[1] = sb("hid_lo1", [P, HC, W], F32R)
        h2_hi = sb("h2_hi", [P, DC, B * S], F32R)
        h2_lo = sb("h2_lo", [P, DC, B * S], F32R)
        hid_hi[0] = sb("hid_hi0", [P, HC, W], F32R)
        hid_lo[0] = sb("hid_lo0", [P, HC, W], F32R)
        hid = sb("hid", [P, HC, W], F32)
        bgu = [sb(f"bgu{par}", [P, 2, HC], F32) for par in range(2)]
        NB = 1 + NR
        with ExitStack() as gates:
            gateT = sb("gateT", [E, TG, W], F32, gates)
        wT = sb("wT", [3 * NB, TG, W], F32R)
        gb_row = sb("gb_row", [P, B, D], F32)
        bd_raw = sb("bd_raw", [3 * NB, D], F32)
        bd = sb("bd", [3 * NB, D], F32R)
        mix3 = sb("mix3", [P, NT, 3 * NB], F32R)
        mix = sb("mix", [P, NT, 1 + NR], F32)
        rank = sb("rank", [P, NT, E], F32)
        gs = sb("gs", [P, NT, E], F32)
        sel = sb("sel", [P, NT, E], F32)
        gm = sb("gm", [P, NT], F32)
        gsum = sb("gsum", [P, NT], F32)
        ginv = sb("ginv", [P, NT], F32)

        def ps(name, shape):
            return ctx.enter_context(nc.psum_tensor(name, shape, F32))

        ps_s = [ps(f"ps_s{k}", [P, 2, W]) for k in range(2)]
        ps_t = [ps(f"ps_t{k}", [P, W]) for k in range(2)]
        ps_g = [ps(f"ps_g{k}", [P, W]) for k in range(2)]
        S_BANKS = [ps_s[k // 2][:, k % 2, :] for k in range(4)]
        LN_BANKS = [S_BANKS, [ps_t[0][:, :], ps_t[1][:, :]] + S_BANKS[:2]]
        V_BANK = [ps_t[0][:, :], ps_g[1][:, :]]
        FIRST_ORDER = [0, 2, 4, 1, 3, 5]
        FIRST_PROJ = [ps_g[0][:, :], S_BANKS[3], ps_g[1][:, :], S_BANKS[0], S_BANKS[2], S_BANKS[1]]
        PROJ_BANK = [0, 0, 1, 0, 1, 1]
        PV_BANK = [0, 1]
        WO_BANK = [0, 0, 0, 1, 1, 0, 0, 1]
        P_BANK = [0, 1, 0, 1, 0, 1, 0, 1, 1, 0, 1, 0]

        def score_pieces(i):
            return (1, P * (i + 1)) if P * (i + 1) <= W else (2, P * (i + 1) // 2)

        def p_block(pT, i, j, n):
            return pT[i // 4][:, j:j + n, (i % 4) * P:(i % 4 + 1) * P]

        def p_bank(k, n):
            return ps_t[P_BANK[k]][:, 0:n * P].rearrange("p (j q) -> p j q", q=P)

        ps_gu = [[ps_s[c][:, k, :] for k in range(2)] for c in range(2)]
        ps_d = [ps_t[0], ps_t[1], ps_g[0], ps_g[1]]
        LN2_BANKS = [S_BANKS, [S_BANKS[1], S_BANKS[3]]]

        const_done = sem("const_done")
        ident_0 = sem("ident_0")
        cT_loaded = sem("cT_loaded")
        wmod_loaded = [sem(f"wmod_loaded{v}") for v in range(6)]
        acc_zeroed = sem("acc_zeroed")
        silu_step = sem("silu_step")
        silu_exp = sem("silu_exp")
        sc_ready = sem("sc_ready")
        mod_done = sem("mod_done")
        mod_read = sem("mod_read")
        gate_step = sem("gate_step")
        x_loaded = [sem(f"x_loaded{g}") for g in range(NG)]
        ln_stat = sem("ln_stat")
        ln_agg = sem("ln_agg")
        ln_var = sem("ln_var")
        ln_sd = sem("ln_sd")
        ln_rstd = sem("ln_rstd")
        ln_shift = sem("ln_shift")
        xn_ready = sem("xn_ready")
        lnT_done = sem("lnT_done")
        ln_affine = sem("ln_affine")
        ln_hi = sem("ln_hi")
        ln_hi_odd = sem("ln_hi_odd")
        rows_done = sem("rows_done")
        rows_copied = sem("rows_copied")
        ln_lo = sem("ln_lo")
        wqkv_loaded = [sem(f"wqkv_loaded{k}") for k in range(2)]
        wo_loaded = [sem(f"wo_loaded{k}") for k in range(2)]
        wqkv_rounded = sem("wqkv_rounded")
        wqkv_split = sem("wqkv_split")
        wo_rounded = sem("wo_rounded")
        wo_split = sem("wo_split")
        proj_done = sem("proj_done")
        qk_hi_done = sem("qk_hi_done")
        qk_lo_done = sem("qk_lo_done")
        vT_copied = sem("vT_copied")
        vtr_done = sem("vtr_done")
        v_hi_done = sem("v_hi_done")
        v_lo_done = sem("v_lo_done")
        score_done = sem("score_done")
        masked = sem("masked")
        rowmax = sem("rowmax")
        exp_done = sem("exp_done")
        pT_done = sem("pT_done")
        p_hi_done = sem("p_hi_done")
        p_lo_done = sem("p_lo_done")
        pv_done = sem("pv_done")
        z_hi_done = sem("z_hi_done")
        z_lo_done = sem("z_lo_done")
        rinv_ready = sem("rinv_ready")
        wo_done = sem("wo_done")
        acc_done = sem("acc_done")
        y_ready = sem("y_ready")
        y_stored = sem("y_stored")
        xb_loaded = [sem(f"xb_loaded{k}") for k in range(2)]
        yb_loaded = [sem(f"yb_loaded{k}") for k in range(NG)]
        small_loaded = sem("small_loaded")
        bd_loaded = sem("bd_loaded")
        x2b_loaded = [sem(f"x2b_loaded{k}") for k in range(2)]
        x2_ready = sem("x2_ready")
        x2_stored = [sem(f"x2_stored{tg}") for tg in range(TG)]
        wr_rounded = sem("wr_rounded")
        wr_split = sem("wr_split")
        wf_loaded = sem("wf_loaded")
        gd_rounded = sem("gd_rounded")
        gd_split = sem("gd_split")
        up_rounded = sem("up_rounded")
        up_split = sem("up_split")
        bd_step = sem("bd_step")
        mix3_step = sem("mix3_step")
        bgu_ready = sem("bgu_ready")
        router_done = sem("router_done")
        gateT_ready = sem("gateT_ready")
        gateT_back = sem("gateT_back")
        route_step = sem("route_step")
        route_shift = sem("route_shift")
        route_exp = sem("route_exp")
        mix_ready = sem("mix_ready")
        mixT_done = sem("mixT_done")
        mixT_read = sem("mixT_read")
        bias_done = sem("bias_done")
        bias_added = sem("bias_added")
        gate_done = sem("gate_done")
        up_done = sem("up_done")
        silu_done = sem("silu_done")
        hidden_ready = sem("hidden_ready")
        hid_hi_done = sem("hid_hi_done")
        hid_lo_done = sem("hid_lo_done")
        down_done = sem("down_done")
        F_added = sem("F_added")
        F_scaled = sem("F_scaled")
        out_ready = sem("out_ready")
        out_stored = sem("out_stored")

        block = ctx.enter_context(nc.Block())

        UNITS = H
        ATT = B * UNITS

        @block.sync
        def _(sp):
            sp.dma_start(cT[:, :, :], c_T).then_inc(cT_loaded, 16)
            mod_v = w_mod.rearrange("(k p) n -> p k n", p=P)

            def load_mod(v, dst):
                sp.dma_start(dst, mod_v[:, :, v * D:(v + 1) * D]).then_inc(wmod_loaded[v], 16)

            def load_x(b):
                for g in range(NG):
                    sp.dma_start(x_sb[:, g], tiles(x_in, NG * b + g)).then_inc(x_loaded[g], 16)

            def load_qkv(head, par):
                sp.dma_start(wqkv_raw[:, par].rearrange("p k c n -> p (k c n)"),
                             w_attn[bass.ds(head, 1), :, 0:3 * D].rearrange("o p n -> p (o n)")) \
                  .then_inc(wqkv_loaded[par], 16)

            def load_wo(head, par):
                sp.dma_start(wo_raw[:, par], w_attn[bass.ds(head, 1), :, 3 * D:4 * D].rearrange("o p n -> p (o n)")) \
                  .then_inc(wo_loaded[par], 16)

            def stream(U, head_qkv, head_wo, par):
                if head_qkv is not None:
                    sp.wait_ge(wqkv_split, 3 * U + 6)
                    load_qkv(head_qkv, 1 - par)
                if head_wo is not None:
                    sp.wait_ge(wo_split, U + 1)
                    load_wo(head_wo, par)

            load_mod(0, wmod[:, 0])
            sp.dma_start(x_sb[:, 0], tiles(x_in, 0)).then_inc(x_loaded[0], 16)
            load_mod(1, wmod[:, 1])
            for g in range(1, NG):
                sp.dma_start(x_sb[:, g], tiles(x_in, g)).then_inc(x_loaded[g], 16)
            for head in range(2):
                load_qkv(head, head)
                load_wo(head, head)
            load_mod(2, wmod[:, 2])
            sp.wait_ge(wqkv_split, 3)
            load_qkv(2, 0)
            for b in range(B):
                u0 = b * UNITS
                with sp.Fori(0, UNITS // 2 - 2) as it:
                    for par in range(2):
                        stream(u0 + 2 * it + par, 2 * it + par + 3, 2 * it + par + 2, par)
                more = b + 1 < B
                stream(u0 + UNITS - 4, UNITS - 1, UNITS - 2, 0)
                stream(u0 + UNITS - 3, 0 if more else None, UNITS - 1, 1)
                if more:
                    stream(u0 + UNITS - 2, 1, 0, 0)
                    sp.wait_ge(score_done, QT * (u0 + UNITS - 1))
                    load_x(b + 1)
                    stream(u0 + UNITS - 1, 2, 1, 1)
                else:
                    sp.wait_ge(proj_done, 6 * ATT)
                    sp.wait_ge(vtr_done, 2 * ATT)
                    sp.wait_ge(score_done, QT * (ATT - 1))
                    load_mod(3, wmod2[:, 0])
                    load_mod(4, wmod2[:, 1])
                    sp.dma_start(xb[:, 0], tiles(x_in, 0)).then_inc(xb_loaded[0], 16)
                    sp.dma_start(yb, tiles(y_dram, 0)).then_inc(yb_loaded[0], 16)
                    sp.dma_start(xb[:, 1], tiles(x_in, 1)).then_inc(xb_loaded[1], 16)
                    sp.wait_ge(pv_done, 2 * (ATT - 1))
                    sp.wait_ge(wo_split, ATT - 1)
                    sp.dma_start(y_of[1], tiles(y_dram, 1)).then_inc(yb_loaded[1], 16)
                if more:
                    for g in range(NG):
                        sp.wait_ge(y_ready, QT * b + TPG * (g + 1))
                        sp.dma_start(tiles(y_dram, NG * b + g), acc[:, TPG * g:TPG * (g + 1), :]) \
                          .then_inc(y_stored, 16)

            def load_shared(m):
                sp.dma_start(wf_raw[:, 0, :], w_shared_up[m]).then_inc(wf_loaded, 16)
                sp.dma_start(wf_raw[:, 1, :], w_shared_down[m]).then_inc(wf_loaded, 16)

            load_shared(0)
            sp.dma_start(wr_raw[:, :, :], w_router).then_inc(small_loaded, 16)
            sp.dma_start(br[:, :], b_router).then_inc(small_loaded, 16)
            sp.dma_start(bsu[:, :, :], b_shared_up).then_inc(small_loaded, 16)
            load_mod(5, wmod2[:, 2])
            for tg in range(TG):
                sp.wait_ge(x2_ready, tg + 1)
                sp.dma_start(tiles(x2_dram, tg), y_of[tg]).then_inc(x2_stored[tg], 16)
                if tg + 2 < TG:
                    sp.wait_ge(lnT_done, DC * (TG + tg + 1))
                    sp.dma_start(xb[:, tg % 2], tiles(x_in, tg + 2)).then_inc(xb_loaded[tg % 2], 16)
                if tg == 0:
                    sp.wait_ge(y_ready, NT)
                    for part in range(3):
                        sp.dma_start(bd_raw[part * NB:(part + 1) * NB, :], b_down).then_inc(bd_loaded, 16)
                if tg == 1:
                    sp.wait_ge(gd_split, 1)
                    load_shared(1)
            sp.wait_ge(gd_split, NSH)
            with sp.Fori(0, NR) as n:
                sp.wait_ge(up_split, n + 1)
                sp.dma_start(wf_land[:, :], w_routed[bass.ds(n, 1)].rearrange("o p f -> p (o f)")) \
                  .then_inc(wf_loaded, 32)
            for tg in range(TG):
                sp.wait_ge(x2_stored[tg], 16)
            sp.wait_ge(down_done, NT * (NM - 1))
            for tg in range(2):
                sp.dma_start(x2b[:, tg % 2], tiles(x2_dram, tg)).then_inc(x2b_loaded[tg % 2], 16)
            for tg in range(TG):
                halves = 2 if tg == TG - 1 else 1
                for half in range(halves):
                    n = TPG // halves
                    t = TPG * tg + n * half
                    sp.wait_ge(out_ready, t + n)
                    sp.dma_start(tiles(out, tg)[:, n * half:n * (half + 1), :], F[:, t:t + n, :]) \
                      .then_inc(out_stored, 16)
                if tg + 2 < TG:
                    sp.dma_start(x2b[:, tg % 2], tiles(x2_dram, tg + 2)).then_inc(x2b_loaded[tg % 2], 16)
            sp.wait_ge(out_stored, 16 * (TG + 1))

        @block.gpsimd
        def _(pool):
            nc.gpsimd.memset(ident[:, :], 0.0).then_inc(ident_0, 1)
            nc.gpsimd.memset(causal[:, :], 0.0).then_inc(ident_0, 1)
            nc.gpsimd.memset(tril[:, :, :], 1.0).then_inc(ident_0, 1)
            nc.gpsimd.memset(ones, 1.0).then_inc(ident_0, 1)
            pool.wait_ge(ident_0, 4)
            nc.gpsimd.affine_select(out=ident[:, :], in_=ident[:, :], compare_op=ALU.not_equal, fill=1.0, base=0,
                                    pattern=[[-1, P]], channel_multiplier=1).then_inc(const_done, 1)
            nc.gpsimd.affine_select(out=causal[:, :], in_=causal[:, :], compare_op=ALU.is_ge, fill=MASKED, base=0,
                                    pattern=[[-1, P]], channel_multiplier=1).then_inc(const_done, 1)
            nc.gpsimd.affine_select(out=tril[:, :, :], in_=tril[:, :, :], compare_op=ALU.is_gt, fill=0.0, base=0,
                                    pattern=[[1, E], [-1, E]], channel_multiplier=0).then_inc(const_done, 1)
            nc.gpsimd.memset(rest_rows[:, :], -1.0).then_inc(ident_0, 1)
            pool.wait_ge(ident_0, 5)
            nc.gpsimd.affine_select(out=rest_rows[:, :], in_=rest_rows[:, :], compare_op=ALU.is_ge, fill=0.0,
                                    base=-NB, pattern=[[-1, 1]], channel_multiplier=1).then_inc(const_done, 1)
            pool.wait_ge(const_done, 4)
            nc.gpsimd.affine_select(out=rest_rows[:, :], in_=rest_rows[:, :], compare_op=ALU.is_ge, fill=0.0,
                                    base=2 * NB - 1, pattern=[[-1, 1]], channel_multiplier=-1) \
              .then_inc(const_done, 1)

            def round_to(hi, raw):
                return nc.gpsimd.tensor_tensor(hi, raw, ones.to_broadcast(list(raw.shape)), ALU.mult)

            def split_qkv(unit, par, loads, first=False, after_all=False):
                for k in range(3):
                    if k == 0:
                        pool.wait_ge(wqkv_loaded[par], 16 * loads)
                    if after_all:
                        pool.wait_ge(proj_done, 6 * unit)
                    elif not first:
                        pool.wait_ge(proj_done, 6 * unit - 6 + 2 * k + 2)
                    round_to(wqkv_hi[:, k], wqkv_raw[:, par, k]).then_inc(wqkv_rounded, 1)
                    pool.wait_ge(wqkv_rounded, 3 * unit + k + 1)
                    nc.gpsimd.tensor_tensor(wqkv_lo[:, k], wqkv_raw[:, par, k], wqkv_hi[:, k].bitcast(F32),
                                            ALU.subtract).then_inc(wqkv_split, 1)

            def split_wo(unit, par, loads, first=False):
                pool.wait_ge(wo_loaded[par], 16 * loads)
                if not first:
                    pool.wait_ge(wo_done, QT * unit)
                round_to(wo_hi[:, None, :], wo_raw[:, par:par + 1]).then_inc(wo_rounded, 1)
                pool.wait_ge(wo_rounded, unit + 1)
                nc.gpsimd.tensor_tensor(wo_lo[:, :], wo_raw[:, par], wo_hi[:, :].bitcast(F32),
                                        ALU.subtract).then_inc(wo_split, 1)

            half = UNITS // 2
            for b in range(B):
                u0 = b * UNITS
                if b == 0:
                    split_qkv(0, 0, 1, first=True)
                else:
                    pool.wait_ge(y_stored, 16 * NG * b)
                nc.gpsimd.memset(acc[:, :, :], 0.0).then_inc(acc_zeroed, 1)
                split_qkv(u0 + 1, 1, b * half + 1, after_all=True)
                split_wo(u0, 0, b * half + 1, first=(b == 0))
                with pool.Fori(0, half - 1) as it:
                    split_qkv(u0 + 2 + 2 * it, 0, b * half + it + 2)
                    split_wo(u0 + 1 + 2 * it, 1, b * half + it + 1)
                    split_qkv(u0 + 3 + 2 * it, 1, b * half + it + 2)
                    split_wo(u0 + 2 + 2 * it, 0, b * half + it + 2)
                if b + 1 < B:
                    split_qkv(u0 + UNITS, 0, (b + 1) * half + 1)
                split_wo(u0 + UNITS - 1, 1, (b + 1) * half)

            def add_x(tg):
                pool.wait_ge(xb_loaded[tg % 2], 16 * (tg // 2 + 1))
                if tg < NG:
                    pool.wait_ge(yb_loaded[tg], 16)
                else:
                    pool.wait_ge(y_ready, TPG * (tg + 1))
                nc.gpsimd.tensor_tensor(y_of[tg], y_of[tg], xb[:, tg % 2], ALU.add).then_inc(x2_ready, 1)

            for tg in range(NG):
                add_x(tg)
            pool.wait_ge(small_loaded, 16 * 3)
            round_to(wr_hi[:, :, :], wr_raw[:, :, :]).then_inc(wr_rounded, 1)
            pool.wait_ge(wr_rounded, 1)
            nc.gpsimd.tensor_tensor(wr_lo[:, :, :], wr_raw[:, :, :], wr_hi[:, :, :].bitcast(F32),
                                    ALU.subtract).then_inc(wr_split, 1)

            def split_slice(m, par):
                pool.wait_ge(wf_loaded, 32 * m + 32)
                hi, lo = w_gd[par]
                round_to(hi[:, :, :], wf_raw[:, 0:2]).then_inc(gd_rounded, 1)
                pool.wait_ge(gd_rounded, m + 1)
                nc.gpsimd.tensor_tensor(lo[:, :, :], wf_raw[:, 0:2], hi[:, :, :].bitcast(F32), ALU.subtract) \
                  .then_inc(gd_split, 1)

            def split_up(n, par):
                hi, lo = w_up[par]
                round_to(hi[:, :, :], wf_raw[:, 2:3]).then_inc(up_rounded, 1)
                round_to(bgu[par][:, :, :], bgu_raw).then_inc(bgu_ready, 1)
                pool.wait_ge(up_rounded, n + 1)
                pool.wait_ge(gd_split, n + NSH + 1)
                nc.gpsimd.tensor_tensor(lo[:, :, :], wf_raw[:, 2:3], hi[:, :, :].bitcast(F32), ALU.subtract) \
                  .then_inc(up_split, 1)

            pool.wait_ge(pv_done, 2 * (ATT - 1))
            split_slice(0, 0)
            for tg in range(NG, TG):
                add_x(tg)
            for tg in range(NG, TG):
                pool.wait_ge(x2_stored[tg], 16)
            pool.wait_ge(xn_ready, NLN * TPG)
            split_slice(1, 1)
            nc.gpsimd.memset(ones, 1.0).then_inc(up_split, 1)
            pool.wait_ge(mix_ready, 2)
            with pool.Fori(0, NR // 2) as it:
                for par in range(2):
                    m = 2 * it + par + NSH
                    pool.wait_ge(down_done, NT * (m - 1))
                    split_slice(m, par)
                    split_up(2 * it + par, par)
            for t in range(NT):
                pool.wait_ge(F_scaled, t + 1)
                tg = t // TPG
                if t % TPG == 0:
                    pool.wait_ge(x2b_loaded[tg % 2], 16 * (tg // 2 + 1))
                nc.gpsimd.tensor_tensor(F[:, t], F[:, t], x2b[:, tg % 2, t % TPG], ALU.add).then_inc(out_ready, 1)

        @block.scalar
        def _(act):
            nc_act = nc.scalar
            act.wait_ge(cT_loaded, 16)
            nc_act.activation(sc[:, :, :], cT[:, :, :], ACT.Exp, scale=-1.0).then_inc(silu_exp, 1)

            def layer_norm_sd(G):
                act.wait_ge(ln_var, G + 1)
                nc_act.activation(sd[:, G], sd[:, G], ACT.Sqrt).then_inc(ln_sd, 1)

            def layer_norm_apply(G, src, dst):
                act.wait_ge(ln_shift, G + 1)
                for t in range(TPG):
                    nc_act.activation(dst[:, t], src[:, t], ACT.Identity, bias=shift[:, G, t:t + 1],
                                      scale=rstd[:, G, t:t + 1]).then_inc(xn_ready, 1)

            def layer_norm_out(G, dst_hi, col, banks, vec, b, chunks=range(DC)):
                for dc in chunks:
                    act.wait_ge(lnT_done, DC * G + dc + 1)
                    bank = banks[dc % len(banks)]
                    nc_act.activation(bank, bank, ACT.Identity, bias=mod_cols[:, vec * DC + dc, b:b + 1],
                                      scale=mod_cols[:, (vec + 1) * DC + dc, b:b + 1]).then_inc(ln_affine, 1)
                    if dc % 2 == 0:
                        act.wait_ge(ln_affine, DC * G + dc + 1)
                        nc_act.activation(dst_hi[:, dc, col:col + W], bank, ACT.Copy).then_inc(ln_hi, 1)

            def proj_hi(unit, par, k, banks=[ps_g[n][:, :] for n in PROJ_BANK], order=range(6)):
                act.wait_ge(proj_done, 6 * unit + order.index(k) + 1)
                g = k % NG
                bank = banks[k]
                if k < 4:
                    dst = (q_hi, k_hi)[k // 2][par]
                    nc_act.activation(dst[:, g * W:(g + 1) * W], bank, ACT.Copy,
                                      scale=SCALE if k < 2 else 1.0).then_inc(qk_hi_done, 1)
                else:
                    nc_act.activation(vT[:, g, :], bank, ACT.Copy).then_inc(vT_copied, 1)

            def v_round(unit, par, g, bank):
                act.wait_ge(vtr_done, 2 * unit + g + 1)
                nc_act.activation(v_hi[par][:, 4 * g:4 * g + 4, :], bank.rearrange("p (j h) -> p j h", h=P),
                                  ACT.Copy).then_inc(v_hi_done, 1)

            def softmax_exp(unit, par, i):
                act.wait_ge(rowmax, QT * unit + i + 1)
                pieces, n = score_pieces(i)
                nc_act.activation(probs[:, i % 2, 0:pieces * n].rearrange("p (a n) -> p a n", n=n),
                                  ps_s[i % 2][:, 0:pieces, 0:n], ACT.Exp, bias=nmax[:, i:i + 1],
                                  accum_out=rsum[:, par, i:i + 1]).then_inc(exp_done, 1)

            def p_round(unit, i, part=slice(None)):
                for k in GROUPS_OF[i][part]:
                    _, j, n = P_GROUPS[k]
                    act.wait_ge(pT_done, NPG * unit + k + 1)
                    nc_act.activation(p_block(pT_hi, i, j, n), p_bank(k, n), ACT.Copy).then_inc(p_hi_done, 1)

            def z_round(unit, g):
                act.wait_ge(pv_done, 2 * unit + g + 1)
                nc_act.activation(z_hi[:, g * W:(g + 1) * W], ps_g[PV_BANK[g]][:, :], ACT.Copy) \
                      .then_inc(z_hi_done, 1)

            def slot(U, par, has_prev=True, has_next=True, also=lambda: None):
                nxt = lambda k: proj_hi(U + 1, 1 - par, k) if has_next else None
                softmax_exp(U, par, 0)
                softmax_exp(U, par, 1)
                nxt(0)
                p_round(U, 0)
                softmax_exp(U, par, 2)
                if has_prev:
                    z_round(U - 1, 1)
                nxt(1)
                p_round(U, 1)
                softmax_exp(U, par, 3)
                nxt(2)
                p_round(U, 2)
                softmax_exp(U, par, 4)
                nxt(3)
                p_round(U, 3)
                softmax_exp(U, par, 5)
                nxt(4)
                p_round(U, 4)
                z_round(U, 0)
                p_round(U, 5)
                softmax_exp(U, par, 6)
                if has_next:
                    v_round(U + 1, 1 - par, 0, V_BANK[0])
                p_round(U, 6, slice(0, 1))
                softmax_exp(U, par, 7)
                nxt(5)
                p_round(U, 6, slice(1, 2))
                if has_next:
                    v_round(U + 1, 1 - par, 1, V_BANK[1])
                p_round(U, 7)
                also()

            def ahead(b):
                def also():
                    if b + 1 < B:
                        for g in range(NG):
                            layer_norm_sd(NG * (b + 1) + g)
                        for g in range(NG):
                            layer_norm_apply(NG * (b + 1) + g, x_sb[:, g], x_sb[:, g])
                return also

            for b in range(B):
                u0 = b * UNITS
                if b == 0:
                    layer_norm_sd(0)
                    for n in range(2):
                        act.wait_ge(rows_done, n + 1)
                        nc_act.activation(mod_rows[:, n, :], ps_g[n][0:B, :], ACT.Copy).then_inc(rows_copied, 1)
                    act.wait_ge(mod_read, 1)
                    layer_norm_sd(1)
                    layer_norm_out(0, hT_hi, 0, LN_BANKS[0], 0, 0)
                for g in range(1, NG):
                    layer_norm_out(NG * b + g, hT_hi, g * W, LN_BANKS[g], 0, b)
                for k in FIRST_ORDER:
                    proj_hi(u0, 0, k, FIRST_PROJ, FIRST_ORDER)
                for g in range(NG):
                    v_round(u0, 0, g, ps_t[g])
                slot(u0, 0, has_prev=False)
                with act.Fori(0, UNITS // 2 - 1) as it:
                    slot(u0 + 1 + 2 * it, 1)
                    slot(u0 + 2 + 2 * it, 0)
                slot(u0 + UNITS - 1, 1, has_next=False, also=ahead(b))
                if b + 1 == B:
                    layer_norm_sd(TG)
                    layer_norm_apply(TG, y_of[0], xb[:, 0])
                z_round(u0 + UNITS - 1, 1)
                if b + 1 < B:
                    layer_norm_out(NG * (b + 1), hT_hi, 0, LN_BANKS[0], 0, b + 1)

            def prepare(tg):
                layer_norm_sd(TG + tg)
                layer_norm_apply(TG + tg, y_of[tg], xb[:, tg % 2])

            def normalise(tg, chunks):
                layer_norm_out(TG + tg, h2_hi, tg * W, LN2_BANKS[min(tg, 1)], 2, tg // NG, chunks)

            def silu(step, c, bias, first=False):
                act.wait_ge(gate_done, HC * step + c + 1)
                if not first:
                    act.wait_ge(hid_lo_done, HC * step - HC + c + 1)
                nc_act.activation(hid[:, c, :], ps_gu[c][0], ACT.Silu, bias=bias(c)).then_inc(silu_done, 1)

            def hidden_hi(step, tg, shared=False):
                for c in range(HC):
                    if shared:
                        act.wait_ge(silu_done, HC * step + c + 1)
                    else:
                        act.wait_ge(hidden_ready, HC * step - HC * TG * NSH + c + 1)
                    nc_act.activation(hid_hi[tg % 2][:, c, :], hid[:, c, :], ACT.Copy).then_inc(hid_hi_done, 1)

            act.wait_ge(mod_read, 2 + B)
            act.wait_ge(acc_done, QT * ATT)
            normalise(0, range(2))
            layer_norm_sd(TG + 1)
            normalise(0, range(2, DC))
            layer_norm_apply(TG + 1, y_of[1], xb[:, 1])
            act.wait_ge(small_loaded, 16 * 3)
            act.wait_ge(y_ready, NT)
            for tg in range(TG):
                for c in range(HC):
                    if tg + 1 < TG:
                        normalise(tg + 1, range(DC // HC * c, DC // HC * (c + 1)))
                    silu(tg, c, lambda c: bsu[:, 0, c:c + 1], first=(tg == 0))
                if tg == 1:
                    act.wait_ge(x2_stored[1], 16)
                if tg == 0:
                    prepare(2)
                hidden_hi(tg, tg, shared=True)
                act.wait_ge(router_done, tg + 1)
                nc_act.activation(gateT[:, tg, :], ps_d[tg][0:E, :], ACT.Identity, bias=br[:, 0:1]) \
                      .then_inc(gateT_ready, 1)
                if 0 < tg and tg + 2 < TG:
                    prepare(tg + 2)
            def copy_mixT(tg):
                act.wait_ge(mixT_done, tg + 1)
                nc_act.activation(wT[:, tg, :], ps_gu[tg % 2][1][0:3 * NB, :], ACT.Copy).then_inc(mixT_read, 1)

            for m in range(1, NSH):
                for tg in range(TG):
                    if m == 1 and tg == 0:
                        act.wait_ge(route_shift, 1)
                        nc_act.activation(sel[:, :, :], gs[:, :, :], ACT.Exp).then_inc(route_exp, 1)
                    for c in range(HC):
                        silu(TG * m + tg, c, lambda c: bsu[:, m, c:c + 1])
                    if m == 1 and tg < 2:
                        copy_mixT(2 * tg)
                        copy_mixT(2 * tg + 1)
                    hidden_hi(TG * m + tg, tg, shared=True)
            with act.Fori(0, NR // 2) as it:
                for par in range(2):
                    n = 2 * it + par
                    act.wait_ge(bgu_ready, n + 1)
                    for tg in range(TG):
                        for c in range(HC):
                            silu(TG * NSH + TG * n + tg, c, lambda c: bgu[par][:, 0, c:c + 1])
                        hidden_hi(TG * NSH + TG * n + tg, tg)

        @block.vector
        def _(dve):
            v = nc.vector
            dve.wait_ge(silu_exp, 1)
            v.tensor_scalar_add(sc[:, :, :], sc[:, :, :], 1.0).then_inc(silu_step, 1)
            dve.wait_ge(silu_step, 1)
            v.reciprocal(sc[:, :, :], sc[:, :, :]).then_inc(silu_step, 1)
            dve.wait_ge(silu_step, 2)
            v.tensor_tensor(sc[:, :, :], sc[:, :, :], cT[:, :, :], ALU.mult).then_inc(silu_step, 1)
            dve.wait_ge(silu_step, 3)
            for k in range(DC):
                for b in range(B):
                    v.tensor_copy(sc_wide[:, k * B + b, :], sc[:, k, b:b + 1].to_broadcast([P, P])) \
                     .then_inc(sc_ready, 1)

            def layer_norm_tiles(G, src, ts):
                for t in ts:
                    v.bn_stats(st[:, G, t], src[:, t]).then_inc(ln_stat, 1)

            def layer_norm_stats(G, src):
                layer_norm_tiles(G, src, range(TPG))
                layer_norm_var(G)

            def layer_norm_var(G):
                for t in range(TPG):
                    dve.wait_ge(ln_stat, TPG * G + t + 1)
                    v.bn_aggr(mv[:, G, t], st[:, G, t]).then_inc(ln_agg, 1)
                dve.wait_ge(ln_agg, TPG * (G + 1))
                v.tensor_scalar_add(sd[:, G], mv[:, G, :, 1], EPS).then_inc(ln_var, 1)

            def layer_norm_rstd(G):
                dve.wait_ge(ln_sd, G + 1)
                v.reciprocal(rstd[:, G], sd[:, G]).then_inc(ln_rstd, 1)
                dve.wait_ge(ln_rstd, G + 1)
                v.scalar_tensor_tensor(out=shift[:, G], in0=mv[:, G, :, 0], scalar=-1.0, in1=rstd[:, G],
                                       op0=ALU.mult, op1=ALU.mult).then_inc(ln_shift, 1)

            def layer_norm_apply(G, src, dst):
                layer_norm_rstd(G)
                for t in range(TPG):
                    v.tensor_scalar(dst[:, t], src[:, t], mv[:, G, t, 0:1], rstd[:, G, t:t + 1],
                                    ALU.subtract, ALU.mult).then_inc(xn_ready, 1)

            def layer_norm_rest(G, dst_hi, dst_lo, col, banks, chunks=range(DC)):
                for dc in chunks:
                    if dc % 2 == 0:
                        dve.wait_ge(ln_hi, (DC * G + dc) // 2 + 1)
                    else:
                        dve.wait_ge(ln_affine, DC * G + dc + 1)
                        v.tensor_copy(dst_hi[:, dc, col:col + W], banks[dc % len(banks)]).then_inc(ln_hi_odd, 1)
                        dve.wait_ge(ln_hi_odd, (DC * G + dc) // 2 + 1)
                    v.tensor_tensor(dst_lo[:, dc, col:col + W], banks[dc % len(banks)],
                                    dst_hi[:, dc, col:col + W].bitcast(F32), ALU.subtract).then_inc(ln_lo, 1)

            def modulation_columns(vecs, count, bank):
                dve.wait_ge(mod_done, count)
                mod_ps = bank[:, 0:4 * DC * B].rearrange("p (v b) -> p v b", b=B)
                for vec in vecs:
                    rows = slice(vec * DC, (vec + 1) * DC)
                    last = v.tensor_scalar_add(mod_cols[:, rows], mod_ps[:, rows], float(vec % 2))
                last.then_inc(mod_read, 1)

            def gate_row(n, dst, bank, count):
                dve.wait_ge(mod_done, count)
                v.tensor_scalar(dst, bank, 0.0, 2.0, ALU.is_ge, ALU.mult).then_inc(gate_step, 1)
                dve.wait_ge(gate_step, 3 * n + 1)
                v.tensor_scalar_add(dst, dst, -1.0).then_inc(gate_step, 1)
                dve.wait_ge(gate_step, 3 * n + 2)
                v.tensor_tensor(bank, bank, dst, ALU.mult).then_inc(gate_step, 1)
                dve.wait_ge(gate_step, 3 * n + 3)
                v.scalar_tensor_tensor(out=dst, in0=bank, scalar=0.25, in1=dst, op0=ALU.max, op1=ALU.mult) \
                 .then_inc(mod_read, 1)

            def proj_lo(unit, par, k, banks=[ps_g[n][:, :] for n in PROJ_BANK], order=range(4)):
                if k >= 4:
                    return
                dve.wait_ge(qk_hi_done, 4 * unit + order.index(k) + 1)
                cols = slice((k % NG) * W, (k % NG + 1) * W)
                hi, lo = ((q_hi, q_lo), (k_hi, k_lo))[k // 2]
                v.scalar_tensor_tensor(out=lo[par][:, cols], in0=banks[k],
                                       scalar=SCALE if k < 2 else 1.0, in1=hi[par][:, cols].bitcast(F32),
                                       op0=ALU.mult, op1=ALU.subtract).then_inc(qk_lo_done, 1)

            def v_rest(unit, par, g, bank):
                dve.wait_ge(v_hi_done, 2 * unit + g + 1)
                rows = slice(4 * g, 4 * g + 4)
                v.tensor_tensor(v_lo[par][:, rows, :], bank.rearrange("p (j h) -> p j h", h=P),
                                v_hi[par][:, rows, :].bitcast(F32), ALU.subtract).then_inc(v_lo_done, 1)

            def row_max(unit, i):
                pieces, n = score_pieces(i)
                bank = ps_s[i % 2]
                at = P * i - (pieces - 1) * n
                dve.wait_ge(score_done, QT * unit + i + 1)
                diag = bank[:, pieces - 1, at:at + P]
                v.tensor_tensor(diag, diag, causal[:, :], ALU.add).then_inc(masked, 1)
                dve.wait_ge(masked, QT * unit + i + 1)
                v.tensor_reduce(nmax[:, i:i + 1], bank[:, 0:pieces, 0:n], AX.XY, ALU.max, negate=True) \
                 .then_inc(rowmax, 1)

            def p_rest(unit, i, part=slice(None)):
                for k in GROUPS_OF[i][part]:
                    _, j, n = P_GROUPS[k]
                    dve.wait_ge(p_hi_done, NPG * unit + k + 1)
                    v.tensor_tensor(p_block(pT_lo, i, j, n), p_bank(k, n), p_block(pT_hi, i, j, n).bitcast(F32),
                                    ALU.subtract).then_inc(p_lo_done, 1)

            def z_rest(unit, par, g):
                dve.wait_ge(z_hi_done, 2 * unit + g + 1)
                cols = slice(g * W, (g + 1) * W)
                v.tensor_tensor(z_lo[:, cols], ps_g[PV_BANK[g]][:, :], z_hi[:, cols].bitcast(F32),
                                ALU.subtract).then_inc(z_lo_done, 1)
                dve.wait_ge(exp_done, QT * unit + TPG * (g + 1))
                v.reciprocal(rinv[:, par, TPG * g:TPG * (g + 1)], rsum[:, par, TPG * g:TPG * (g + 1)]) \
                 .then_inc(rinv_ready, 1)

            def add_out(unit, par, t):
                dve.wait_ge(wo_done, QT * unit + t + 1)
                dve.wait_ge(rinv_ready, 2 * unit + t // TPG + 1)
                v.scalar_tensor_tensor(out=acc[:, t], in0=ps_g[WO_BANK[t]][:, :], scalar=rinv[:, par, t:t + 1],
                                       in1=acc[:, t], op0=ALU.mult, op1=ALU.add).then_inc(acc_done, 1)

            def slot(U, par, has_prev=True, has_next=True, also=lambda i: None):
                nxt = lambda k: proj_lo(U + 1, 1 - par, k) if has_next else None
                prev = lambda t: add_out(U - 1, 1 - par, t) if has_prev else None
                prev(3)
                row_max(U, 1)
                nxt(0)
                p_rest(U, 0)
                also(0)
                row_max(U, 2)
                if has_prev:
                    z_rest(U - 1, 1 - par, 1)
                nxt(1)
                if has_next:
                    prev(4)
                p_rest(U, 1)
                also(1)
                row_max(U, 3)
                if not has_next:
                    prev(4)
                prev(5)
                nxt(2)
                if has_next:
                    prev(6)
                p_rest(U, 2)
                also(2)
                row_max(U, 4)
                if not has_next:
                    prev(6)
                prev(7)
                nxt(3)
                p_rest(U, 3)
                also(3)
                row_max(U, 5)
                p_rest(U, 4)
                also(4)
                row_max(U, 6)
                z_rest(U, par, 0)
                p_rest(U, 5)
                if has_next:
                    row_max(U, 7)
                    v_rest(U + 1, 1 - par, 0, V_BANK[0])
                    add_out(U, par, 0)
                else:
                    add_out(U, par, 0)
                    row_max(U, 7)
                    also(5)
                p_rest(U, 6, slice(0, 1))
                add_out(U, par, 1)
                p_rest(U, 6, slice(1, 2))
                also(6)
                if has_next:
                    v_rest(U + 1, 1 - par, 1, V_BANK[1])
                add_out(U, par, 2)
                if has_next:
                    row_max(U + 1, 0)
                else:
                    add_out(U, par, 3)
                p_rest(U, 7)
                also(7)

            def scale_by_ga(b, ts):
                for t in ts:
                    dve.wait_ge(acc_done, QT * (UNITS * (b + 1) - 1) + t + 1)
                    v.tensor_tensor(acc[:, t], acc[:, t], ga_row[:, b], ALU.mult).then_inc(y_ready, 1)

            def stats_x2(tg):
                dve.wait_ge(x2_ready, tg + 1)
                layer_norm_stats(TG + tg, y_of[tg])

            def ahead(b):
                def also(i):
                    if b + 1 < B:
                        if 3 <= i < 3 + 2 * NG:
                            g, half = divmod(i - 3, 2)
                            if half == 0:
                                dve.wait_ge(x_loaded[g], 16 * (b + 2))
                            layer_norm_tiles(NG * (b + 1) + g, x_sb[:, g], range(2 * half, 2 * half + 2))
                        if i == 7:
                            for g in range(NG):
                                layer_norm_var(NG * (b + 1) + g)
                            for g in range(NG):
                                layer_norm_rstd(NG * (b + 1) + g)
                    else:
                        if i == 4:
                            modulation_columns((2, 3), 2 + B, ps_g[0][:, :])
                        if i == 7:
                            stats_x2(0)
                return also

            for b in range(B):
                u0 = b * UNITS
                if b == 0:
                    for g in range(NG):
                        dve.wait_ge(x_loaded[g], 16)
                        layer_norm_stats(g, x_sb[:, g])
                        if g == 0:
                            layer_norm_apply(g, x_sb[:, g], x_sb[:, g])
                    modulation_columns((0, 1), 1, ps_t[0][:, :])
                    for g in range(1, NG):
                        layer_norm_apply(g, x_sb[:, g], x_sb[:, g])
                    layer_norm_rest(0, hT_hi, hT_lo, 0, LN_BANKS[0])
                for g in range(1, NG):
                    layer_norm_rest(NG * b + g, hT_hi, hT_lo, g * W, LN_BANKS[g])
                if b > 0:
                    scale_by_ga(b - 1, range(TPG, QT))
                order = [k for k in FIRST_ORDER if k < 4]
                for k in order:
                    proj_lo(u0, 0, k, FIRST_PROJ, order)
                for g in range(NG):
                    v_rest(u0, 0, g, ps_t[g])
                if b == 0:
                    for n in range(B):
                        gate_row(n, ga_row[:, n], ps_g[n % 2][:, :], 2 + n)
                row_max(u0, 0)
                dve.wait_ge(acc_zeroed, b + 1)
                slot(u0, 0, has_prev=False)
                with dve.Fori(0, UNITS // 2 - 1) as it:
                    slot(u0 + 1 + 2 * it, 1)
                    slot(u0 + 2 + 2 * it, 0)
                slot(u0 + UNITS - 1, 1, has_next=False, also=ahead(b))
                if b + 1 == B:
                    layer_norm_rstd(TG)
                scale_by_ga(b, range(TPG))
                z_rest(u0 + UNITS - 1, 1, 1)
                for t in range(TPG, QT):
                    add_out(u0 + UNITS - 1, 1, t)
                    if b + 1 < B and t == TPG + 1:
                        layer_norm_rest(NG * (b + 1), hT_hi, hT_lo, 0, LN_BANKS[0], range(2))
                if b + 1 < B:
                    layer_norm_rest(NG * (b + 1), hT_hi, hT_lo, 0, LN_BANKS[0], range(2, DC))

            def normalise_rest(tg, chunks=range(DC)):
                layer_norm_rest(TG + tg, h2_hi, h2_lo, tg * W, LN2_BANKS[min(tg, 1)], chunks)

            def hidden(step, tg, par=None):
                if par is not None:
                    for c in range(HC):
                        dve.wait_ge(up_done, HC * step - HC * TG * NSH + c + 1)
                        dve.wait_ge(silu_done, HC * step + c + 1)
                        v.scalar_tensor_tensor(out=hid[:, c, :], in0=ps_gu[c][1],
                                               scalar=bgu[par][:, 1, c:c + 1],
                                               in1=hid[:, c, :], op0=ALU.add, op1=ALU.mult) \
                         .then_inc(hidden_ready, 1)
                for c in range(HC):
                    dve.wait_ge(hid_hi_done, HC * step + c + 1)
                    v.tensor_tensor(hid_lo[tg % 2][:, c, :], hid[:, c, :], hid_hi[tg % 2][:, c, :].bitcast(F32),
                                    ALU.subtract).then_inc(hid_lo_done, 1)

            def add_down(m, tg, col=None, ks=range(TPG)):
                for k in ks:
                    t = TPG * tg + k
                    dve.wait_ge(down_done, NT * m + t + 1)
                    if col is None:
                        if m == 0:
                            v.tensor_copy(F[:, t], ps_d[k][:, :]).then_inc(F_added, 1)
                        else:
                            dve.wait_ge(F_added, NT * (m - 1) + t + 1)
                            v.tensor_tensor(F[:, t], F[:, t], ps_d[k][:, :], ALU.add).then_inc(F_added, 1)
                    else:
                        dve.wait_ge(F_added, NT * m - NT + t + 1)
                        v.scalar_tensor_tensor(out=F[:, t], in0=ps_d[k][:, :],
                                               scalar=mix[:, t, bass.ds(col, 1)], in1=F[:, t],
                                               op0=ALU.mult, op1=ALU.add).then_inc(F_added, 1)

            def split_biases():
                dve.wait_ge(bd_loaded, 16 * 3)
                v.tensor_copy(bd[:, :], bd_raw[:, :]).then_inc(bd_step, 1)
                dve.wait_ge(bd_step, 1)
                dve.wait_ge(const_done, 5)
                v.scalar_tensor_tensor(out=bd_raw[:, :], in0=bd[:, :].bitcast(F32), scalar=rest_rows[0:3 * NB, :],
                                       in1=bd_raw[:, :], op0=ALU.mult, op1=ALU.add).then_inc(bd_step, 1)
                dve.wait_ge(bd_step, 2)
                v.tensor_copy(bd[:, :], bd_raw[:, :]).then_inc(bd_step, 1)

            def route():
                done = 1

                def after():
                    nonlocal done
                    dve.wait_ge(route_step, done)
                    done += 1

                gt, eq = (route_tmp[:, k * NT * E * E:(k + 1) * NT * E * E].rearrange("p (t i j) -> p t i j", i=E, j=E)
                          for k in range(2))
                g_j = gs[:, :, None, :].to_broadcast([P, NT, E, E])
                g_i = gs[:, :, :, None].to_broadcast([P, NT, E, E])
                after()
                v.tensor_tensor(eq, g_j, g_i, ALU.is_equal).then_inc(route_step, 1)
                after()
                v.tensor_tensor(eq, eq, tril[:, None, :, :].to_broadcast([P, NT, E, E]), ALU.mult) \
                 .then_inc(route_step, 1)
                after()
                v.tensor_tensor(gt, g_j, g_i, ALU.is_gt).then_inc(route_step, 1)
                after()
                v.tensor_tensor(gt, gt, eq, ALU.add).then_inc(route_step, 1)
                after()
                v.tensor_reduce(rank[:, :, :], gt, AX.X, ALU.add).then_inc(route_step, 1)
                after()
                v.tensor_reduce(gm[:, :], gs[:, :, :], AX.X, ALU.max).then_inc(route_step, 1)
                after()
                v.tensor_tensor(gs[:, :, :], gs[:, :, :], gm[:, :, None].to_broadcast([P, NT, E]), ALU.subtract) \
                 .then_inc(route_shift, 1)
                v.tensor_scalar(rank[:, :, :], rank[:, :, :], float(TOPK), None, ALU.is_lt).then_inc(route_step, 1)
                after()
                dve.wait_ge(route_exp, 1)
                v.tensor_tensor(rank[:, :, :], rank[:, :, :], sel[:, :, :], ALU.mult).then_inc(route_step, 1)
                after()
                v.tensor_reduce(gsum[:, :], rank[:, :, :], AX.X, ALU.add).then_inc(route_step, 1)
                after()
                v.reciprocal(ginv[:, :], gsum[:, :]).then_inc(route_step, 1)
                after()
                v.memset(mix[:, :, 0:1], 1.0).then_inc(mix_ready, 1)
                v.tensor_tensor(mix[:, :, 1:1 + NR], rank[:, :, 0:NR], ginv[:, :, None].to_broadcast([P, NT, NR]),
                                ALU.mult).then_inc(mix_ready, 1)
                dve.wait_ge(mix_ready, 2)
                for part in range(2):
                    v.tensor_copy(mix3[:, :, part * NB:(part + 1) * NB], mix[:, :, :]).then_inc(mix3_step, 1)
                dve.wait_ge(mix3_step, 2)
                v.tensor_tensor(mix3[:, :, 2 * NB:3 * NB], mix[:, :, :], mix3[:, :, 0:NB].bitcast(F32),
                                ALU.subtract).then_inc(mix3_step, 1)

            stats_x2(1)
            normalise_rest(0, range(2))
            layer_norm_rstd(TG + 1)
            normalise_rest(0, range(2, DC))
            scale_by_ga(B - 1, range(TPG, QT))
            for tg in range(TG):
                if tg + 1 < TG:
                    normalise_rest(tg + 1, range(2))
                if tg == 0:
                    stats_x2(2)
                if tg + 1 < TG:
                    normalise_rest(tg + 1, range(2, DC))
                if tg == 0:
                    layer_norm_rstd(TG + 2)
                if 0 < tg < B:
                    gate_row(B + tg, gb_row[:, tg], ps_g[tg][:, :], 3 + B + tg)
                hidden(tg, tg)
                if 0 < tg and tg + 2 < TG:
                    stats_x2(tg + 2)
                if tg == 0:
                    gate_row(B, gb_row[:, 0], ps_g[0][:, :], 3 + B)
                if 0 < tg and tg + 2 < TG:
                    layer_norm_rstd(TG + tg + 2)
                if tg > 0:
                    if tg == TG - 1:
                        split_biases()
                    add_down(0, tg - 1)
            dve.wait_ge(gateT_back, 1)
            v.tensor_copy(gs[:, :, :], ps_d[0][:, 0:NT * E].rearrange("p (t e) -> p t e", e=E)) \
             .then_inc(route_step, 1)
            route()
            dve.wait_ge(x2_stored[0], 16)
            for step in range(TG, NSH * TG):
                if step == NSH * TG - 1:
                    for k in range(TPG):
                        t = NT - TPG + k
                        dve.wait_ge(bias_done, k + 1)
                        dve.wait_ge(F_added, t + 1)
                        v.tensor_tensor(F[:, t], F[:, t], ps_d[k][:, :], ALU.add).then_inc(bias_added, 1)
                hidden(step, step % TG)
                add_down((step - 1) // TG, (step - 1) % TG)

            def scale_by_gb(t):
                dve.wait_ge(F_added, NT * (NM - 1) + t + 1)
                v.tensor_tensor(F[:, t], F[:, t], gb_row[:, t // QT], ALU.mult).then_inc(F_scaled, 1)

            def expert(n, m, par, last=False):
                for tg in range(TG):
                    hidden(TG * m + tg, tg, par)
                    if tg == 0:
                        add_down(m - 1, TG - 1, n)
                    else:
                        add_down(m, tg - 1, n + 1)
                        if last:
                            for t in range(TPG * (tg - 1), TPG * tg):
                                scale_by_gb(t)

            dve.wait_ge(bias_added, TPG)
            with dve.Fori(0, NR // 2 - 1) as it:
                for par in range(2):
                    n = 2 * it + par
                    dve.wait_ge(bgu_ready, n + 1)
                    expert(n, NSH + n, par)
            for par in range(2):
                n = NR - 2 + par
                dve.wait_ge(bgu_ready, n + 1)
                expert(n, NSH + n, par, last=(n == NR - 1))
            for k in range(TPG):
                add_down(NM - 1, TG - 1, NR, [k])
                scale_by_gb(NT - TPG + k)

        @block.tensor
        def _(pe):
            mm = nc.tensor.matmul

            def product(out, stat, mov, first, last):
                mm(out, stat[0], mov[0], start=first, stop=False)
                mm(out, stat[0], mov[1], start=False, stop=False)
                return mm(out, stat[1], mov[0], start=False, stop=last)

            pe.wait_ge(sc_ready, DC * B)
            pe.wait_ge(const_done, 3)
            order = [0, 1, 3, 4]

            def mod_columns(n, w, bank):
                mod_ps = bank[:, 0:4 * DC * B].rearrange("p (v b) -> p v b", b=B)
                pe.wait_ge(wmod_loaded[order[n]], 16)
                for dc in range(DC):
                    for k in range(DC):
                        last = mm(mod_ps[:, n * DC + dc, :], w[:, k, dc * P:(dc + 1) * P],
                                  sc[:, k, :], start=(k == 0), stop=(k == DC - 1))
                return last

            def mod_row(vec, b, w, bank):
                pe.wait_ge(wmod_loaded[vec], 16)
                for k in range(DC):
                    last = mm(bank, sc_wide[:, k * B + b, :], w[:, k, :], start=(k == 0), stop=(k == DC - 1))
                last.then_inc(mod_done, 1)

            def layer_norm_transpose(G, src, banks, used, chunks=range(DC)):
                for dc in chunks:
                    used(dc)
                    for t in range(TPG):
                        if dc == 0:
                            pe.wait_ge(xn_ready, TPG * G + t + 1)
                        last = nc.tensor.transpose(banks[dc % len(banks)][:, t * P:(t + 1) * P],
                                                   src[:, t, dc * P:(dc + 1) * P], ident[:, :])
                    last.then_inc(lnT_done, 1)

            def project(unit, par, k, banks=[ps_g[n][:, :] for n in PROJ_BANK]):
                g = k % NG
                pe.wait_ge(wqkv_split, 3 * unit + k // 2 + 1)
                for dc in range(DC):
                    last = product(banks[k], (wqkv_hi[:, k // 2, dc], wqkv_lo[:, k // 2, dc]),
                                   [h[:, dc, g * W:(g + 1) * W] for h in (hT_hi, hT_lo)], dc == 0, dc == DC - 1)
                last.then_inc(proj_done, 1)

            def v_transpose(unit, g, bank):
                pe.wait_ge(vT_copied, 2 * unit + g + 1)
                for j in range(4):
                    last = nc.tensor.transpose(bank[:, j * P:(j + 1) * P], vT[:, g, j * P:(j + 1) * P], ident[:, :])
                last.then_inc(vtr_done, 1)

            def scores(unit, par, i):
                if i == 0:
                    pe.wait_ge(qk_lo_done, 4 * unit + 4)
                pieces, n = score_pieces(i)
                cols = slice(i * P, (i + 1) * P)
                for piece, (s, m) in enumerate(((q_hi, k_hi), (q_hi, k_lo), (q_lo, k_hi))):
                    for a in range(pieces):
                        last = mm(ps_s[i % 2][:, a, 0:n], s[par][:, cols], m[par][:, a * n:(a + 1) * n],
                                  start=(piece == 0), stop=(piece == 2))
                last.then_inc(score_done, 1)

            def p_transpose(unit, i, used, part=slice(None)):
                pe.wait_ge(exp_done, QT * unit + i + 1)
                for k in GROUPS_OF[i][part]:
                    _, j0, n = P_GROUPS[k]
                    used(k)
                    for j in range(n):
                        last = nc.tensor.transpose(ps_t[P_BANK[k]][:, j * P:(j + 1) * P],
                                                   probs[:, i % 2, (j0 + j) * P:(j0 + j + 1) * P], ident[:, :])
                    last.then_inc(pT_done, 1)

            def values(unit, par, g):
                pe.wait_ge(p_lo_done, NPG * unit + GROUPS_OF[4 * g + 3][-1] + 1)
                if g == 0:
                    pe.wait_ge(v_lo_done, 2 * unit + 2)
                nj = 4 * (g + 1)
                for j in range(nj):
                    c0 = max(0, j - 4 * g) * P
                    last = product(ps_g[PV_BANK[g]][:, c0:W], (v_hi[par][:, j], v_lo[par][:, j]),
                                   (pT_hi[g][:, j, c0:W], pT_lo[g][:, j, c0:W]), j == 0, j == nj - 1)
                last.then_inc(pv_done, 1)

            def out_proj(unit, t):
                if t == 0:
                    pe.wait_ge(wo_split, unit + 1)
                if t % TPG == 0:
                    pe.wait_ge(z_lo_done, 2 * unit + t // TPG + 1)
                cols = slice(t * P, (t + 1) * P)
                product(ps_g[WO_BANK[t]][:, :], (z_hi[:, cols], z_lo[:, cols]), (wo_hi[:, :], wo_lo[:, :]),
                        True, True).then_inc(wo_done, 1)

            def proj_read(unit, k):
                if k < 4:
                    pe.wait_ge(qk_lo_done, 4 * unit + k + 1)
                else:
                    pe.wait_ge(vT_copied, 2 * unit + k - 3)

            def z_read(unit, g):
                pe.wait_ge(z_lo_done, 2 * unit + g + 1)

            def out_read(unit, t):
                pe.wait_ge(acc_done, QT * unit + t + 1)

            def p_read(unit, k):
                pe.wait_ge(p_lo_done, NPG * unit + k + 1)

            def v_read(unit, g):
                pe.wait_ge(v_lo_done, 2 * unit + g + 1)

            def score_read(unit, i):
                pe.wait_ge(exp_done, QT * unit + i + 1)

            def slot(U, par, has_prev=True, has_next=True, also=None):
                N, Q = U + 1, 1 - par

                def p_used(k):
                    if k < 2:
                        if has_prev:
                            p_read(U - 1, NPG - 1 - k)
                        else:
                            v_read(U, k)
                    elif k == 8:
                        p_read(U, 7)
                    elif k == 9:
                        v_read(N, 0) if has_next else p_read(U, 6)
                    else:
                        p_read(U, k - 2)

                if has_next:
                    if has_prev:
                        out_read(U - 1, 2)
                    else:
                        proj_read(U, 3)
                    project(N, Q, 0)
                p_transpose(U, 0, p_used)
                score_read(U, 0)
                scores(U, par, 2)
                if has_prev:
                    out_read(U - 1, 3)
                    values(U - 1, Q, 1)
                if has_next:
                    proj_read(N, 0)
                    project(N, Q, 1)
                if has_prev and has_next:
                    z_read(U - 1, 1)
                    out_proj(U - 1, 4)
                p_transpose(U, 1, p_used)
                score_read(U, 1)
                scores(U, par, 3)
                if not has_next:
                    z_read(U - 1, 1)
                    out_proj(U - 1, 4)
                if has_prev:
                    if has_next:
                        proj_read(N, 1)
                    else:
                        out_read(U - 1, 3)
                    out_proj(U - 1, 5)
                if has_next:
                    if has_prev:
                        out_read(U - 1, 4)
                    else:
                        proj_read(U, 5)
                    project(N, Q, 2)
                if has_prev and has_next:
                    out_read(U - 1, 5)
                    out_proj(U - 1, 6)
                p_transpose(U, 2, p_used)
                score_read(U, 2)
                scores(U, par, 4)
                if not has_next:
                    out_read(U - 1, 5)
                    out_proj(U - 1, 6)
                if has_prev:
                    if has_next:
                        proj_read(N, 2)
                    else:
                        out_read(U - 1, 4)
                    out_proj(U - 1, 7)
                if has_next:
                    if has_prev:
                        out_read(U - 1, 6)
                    else:
                        proj_read(N, 1)
                    project(N, Q, 3)
                elif also:
                    out_read(U - 1, 6)
                    also(0)
                p_transpose(U, 3, p_used)
                score_read(U, 3)
                scores(U, par, 5)
                if has_next:
                    if has_prev:
                        out_read(U - 1, 7)
                    else:
                        proj_read(N, 2)
                    project(N, Q, 4)
                elif also:
                    also(1)
                p_transpose(U, 4, p_used)
                score_read(U, 4)
                scores(U, par, 6)
                if has_next:
                    proj_read(N, 3)
                elif also:
                    pe.wait_ge(mod_read, 2 + B)
                else:
                    out_read(U - 1, 6)
                values(U, par, 0)
                p_transpose(U, 5, p_used)
                score_read(U, 5)
                scores(U, par, 7)
                z_read(U, 0)
                out_proj(U, 0)
                if has_next:
                    p_read(U, 6)
                    v_transpose(N, 0, V_BANK[0])
                p_transpose(U, 6, p_used, slice(0, 1))
                if has_next:
                    proj_read(N, 4)
                    project(N, Q, 5)
                out_read(U, 0)
                out_proj(U, 1)
                p_transpose(U, 6, p_used, slice(1, 2))
                if has_next:
                    v_transpose(N, 1, V_BANK[1])
                    score_read(U, 6)
                    scores(N, Q, 0)
                out_read(U, 1)
                out_proj(U, 2)
                if not has_next:
                    out_read(U - 1, 7)
                    out_proj(U, 3)
                p_transpose(U, 7, p_used)
                if has_next:
                    score_read(U, 7)
                    scores(N, Q, 1)
                    v_read(N, 1)
                    out_proj(U, 3)

            for n in range(2):
                pe.wait_ge(wmod_loaded[n], 16)
                for k in range(DC):
                    last = mm(ps_g[n][0:B, :], sc[:, k, :], wmod[:, n, k, :], start=(k == 0), stop=(k == DC - 1))
                last.then_inc(rows_done, 1)
            for n in range(2):
                pe.wait_ge(rows_copied, n + 1)
                for dc in range(DC):
                    at = (n * DC + dc) * B
                    last = nc.tensor.transpose(ps_t[0][:, at:at + B], mod_rows[:, n, dc * P:(dc + 1) * P],
                                               ident[0:B, 0:B])
            last.then_inc(mod_done, 1)

            def normalised_T(b, g, chunks=range(DC)):
                G = NG * b + g

                def used(dc):
                    if g == 0:
                        if b > 0 and dc == 0:
                            score_read(UNITS * b - 1, QT - 1)
                    elif dc == 0:
                        if b == 0:
                            pe.wait_ge(mod_read, 1)
                        else:
                            p_read(UNITS * b - 1, NPG - 1)
                    elif dc >= 2:
                        pe.wait_ge(ln_lo, DC * (G - 1) + dc - 1)
                layer_norm_transpose(G, x_sb[:, g], LN_BANKS[g], used, chunks)

            def normalised2_T(tg, chunks):
                def used(dc):
                    if tg == 0:
                        if dc == 0:
                            score_read(ATT - 1, QT - 1)
                    elif tg == 1 and dc < 2:
                        pe.wait_ge(ln_lo, DC * (TG + tg - 1) + 2 * dc + 2)
                    else:
                        pe.wait_ge(ln_lo, DC * (TG + tg) + dc - 1)
                layer_norm_transpose(TG + tg, xb[:, tg % 2], LN2_BANKS[min(tg, 1)], used, chunks)

            def experts_mod(n):
                last = mod_columns(2 + n, wmod2[:, n], ps_g[0][:, :])
                if n == 1:
                    last.then_inc(mod_done, 1)

            for b in range(B):
                u0 = b * UNITS
                if b == 0:
                    normalised_T(0, 0)
                    normalised_T(0, 1)
                else:
                    out_read(u0 - 1, QT - 1)
                for k in FIRST_ORDER:
                    pe.wait_ge(ln_lo, DC * (NG * b + k % NG + 1))
                    project(u0, 0, k, FIRST_PROJ)
                for g in range(NG):
                    v_transpose(u0, g, ps_t[g])
                scores(u0, 0, 0)
                scores(u0, 0, 1)
                if b == 0:
                    proj_read(u0, 3)
                    for n in range(B):
                        mod_row(2, n, wmod[:, 2], ps_g[n][:, :])
                    pe.wait_ge(mod_read, 1 + B)
                slot(u0, 0, has_prev=False)
                with pe.Fori(0, UNITS // 2 - 1) as it:
                    slot(u0 + 1 + 2 * it, 1)
                    slot(u0 + 2 + 2 * it, 0)
                last = u0 + UNITS - 1
                slot(last, 1, has_next=False, also=None if b + 1 < B else experts_mod)
                out_read(last, 3)
                values(last, 1, 1)
                if b + 1 < B:
                    normalised_T(b + 1, 0)
                else:
                    normalised2_T(0, range(DC))
                z_read(last, 1)
                out_proj(last, 4)
                out_proj(last, 5)
                if b + 1 < B:
                    normalised_T(b + 1, 1, range(2))
                out_read(last, 5)
                out_proj(last, 6)
                out_read(last, 4)
                out_proj(last, 7)
                if b + 1 < B:
                    normalised_T(b + 1, 1, range(2, DC))

            def gate_chunk(step, par, tg, c, shared=False, first=False):
                for k in range(1 if shared else 2):
                    if not first:
                        pe.wait_ge((silu_done, hid_lo_done)[k], HC * step - HC + c + 1)
                    hi, lo = (w_gd, w_up)[k][par]
                    for dc in range(DC):
                        at = dc * HID + c * P
                        last = product(ps_gu[c][k], (hi[:, 0, at:at + P], lo[:, 0, at:at + P]),
                                       [h[:, dc, tg * W:(tg + 1) * W] for h in (h2_hi, h2_lo)],
                                       dc == 0, dc == DC - 1)
                    last.then_inc((gate_done, up_done)[k], 1)

            def gates_up(step, m, par, tg, shared=False):
                if tg == 0:
                    pe.wait_ge(gd_split, m + 1)
                    if not shared:
                        pe.wait_ge(up_split, m - NSH + 2)
                for c in range(HC):
                    gate_chunk(step, par, tg, c, shared)

            def down(step, m, par, tg, biases=False):
                pe.wait_ge(hid_lo_done, HC * step + HC)
                for k in range(TPG):
                    if isinstance(m, int) and m == 0 and k == (tg + 1) % TG:
                        pe.wait_ge(gateT_ready, tg + 2 if tg + 1 < TG else TG)
                    if isinstance(m, int) and m == 0 and tg == TG - 1 and k == 0:
                        pe.wait_ge(route_step, 1)
                    if isinstance(m, int) and m == 0 and tg == 0:
                        if k == 0:
                            pe.wait_ge(gateT_ready, 1)
                            pe.wait_ge(mod_read, 2 + 2 * B)
                    else:
                        pe.wait_ge(F_added, NT * m + TPG * (tg - 1) + k + 1)
                    for c in range(HC):
                        last = product(ps_d[k][:, :], [h[tg % 2][:, c, k * P:(k + 1) * P] for h in (hid_hi, hid_lo)],
                                       [w[:, 1, c * D:(c + 1) * D] for w in w_gd[par]],
                                       c == 0, c == HC - 1 and not biases)
                    if biases:
                        last = mm(ps_d[k][:, :], wT[:, tg, k * P:(k + 1) * P], bd[:, :], start=False, stop=True)
                    last.then_inc(down_done, 1)

            def router(tg):
                if tg == 0:
                    pe.wait_ge(wr_split, 1)
                    p_read(ATT - 1, NPG - 1)
                elif tg > 1:
                    pe.wait_ge(F_added, TPG * (tg - 2) + tg + 1)
                for dc in range(DC):
                    last = product(ps_d[tg][0:E, :], (wr_hi[:, dc], wr_lo[:, dc]),
                                   [h[:, dc, tg * W:(tg + 1) * W] for h in (h2_hi, h2_lo)], dc == 0, dc == DC - 1)
                last.then_inc(router_done, 1)

            out_read(ATT - 1, QT - 1)
            for b in range(B):
                mod_row(5, b, wmod2[:, 2], ps_g[b][:, :])
            for tg in range(TG):
                for c in range(HC):
                    if tg + 1 < TG:
                        normalised2_T(tg + 1, range(DC // HC * c, DC // HC * (c + 1)))
                    if c == 0:
                        if tg == 0:
                            pe.wait_ge(gd_split, 1)
                        pe.wait_ge(ln_lo, DC * (TG + tg + 1))
                    gate_chunk(tg, 0, tg, c, shared=True, first=(tg == 0))
                if tg == 2:
                    pe.wait_ge(mod_read, 2 + 2 * B)
                router(tg)
                if tg > 0:
                    down(tg - 1, 0, 0, tg - 1)
            pe.wait_ge(gateT_ready, TG)
            pe.wait_ge(F_added, NT - 2 * TPG + 1)
            gate_T = gateT[:, :, :].rearrange("e g w -> e (g w)")
            for t in range(NT):
                last = nc.tensor.transpose(ps_d[0][:, t * E:(t + 1) * E], gate_T[:, t * P:(t + 1) * P],
                                           ident[0:E, 0:E])
            last.then_inc(gateT_back, 1)
            def mix_transpose(tg):
                for t in range(TPG):
                    last = nc.tensor.transpose(ps_gu[tg % 2][1][0:3 * NB, t * P:(t + 1) * P],
                                               mix3[:, TPG * tg + t, :].bitcast(F32), ident[:, :])
                last.then_inc(mixT_done, 1)

            for step in range(TG, NSH * TG):
                tg = step - TG
                if tg == TG - 1:
                    pe.wait_ge(mixT_read, TG)
                    for k in range(TPG):
                        pe.wait_ge(F_added, NT + TPG * (tg - 2) + k + 1)
                        mm(ps_d[k][:, :], wT[:, tg, k * P:(k + 1) * P], bd[:, :], start=True, stop=True) \
                          .then_inc(bias_done, 1)
                gates_up(step, step // TG, step // TG % 2, step % TG, shared=True)
                if tg == 0:
                    down(step - 1, 0, 0, TG - 1)
                    pe.wait_ge(mix3_step, 3)
                    mix_transpose(0)
                    mix_transpose(1)
                else:
                    if tg == 1:
                        pe.wait_ge(mixT_read, 2)
                        pe.wait_ge(bd_step, 3)
                        mix_transpose(2)
                        mix_transpose(3)
                    if tg == TG - 1:
                        pe.wait_ge(bias_added, TPG)
                    down(step - 1, 1, 1, tg - 1, biases=True)
            with pe.Fori(0, NR // 2) as it:
                for par in range(2):
                    m = NSH + 2 * it + par
                    for tg in range(TG):
                        gates_up(TG * m + tg, m, par, tg)
                        if tg == 0:
                            down(TG * m - 1, m - 1, 1 - par, TG - 1)
                        else:
                            down(TG * m + tg - 1, m, par, tg - 1)
            down(TG * NM - 1, NM - 1, (NM - 1) % 2, TG - 1)


def kernel(**inputs):
    import numpy as np
    import concourse.bacc as bacc
    from concourse.bass_utils import run_bass_kernel_spmd as run

    a = {k.replace("L0_", ""): np.asarray(v) for k, v in inputs.items()}
    H, Dh, D = a["attn_W_Q"].shape
    DC = D // P
    NR, _, HID = a["ffn_Wgate"].shape
    HC = HID // P
    NSH = a["ffn_Ws_up"].shape[1] // HID
    E = a["ffn_Wg"].shape[1]

    def head_major(w):
        return w.transpose(0, 2, 1).reshape(H, DC, P, Dh).transpose(0, 2, 1, 3).reshape(H, P, DC * Dh)

    def chunked(w):
        n, rows, cols = w.shape
        return w.reshape(n, rows // P, P, cols).transpose(0, 2, 1, 3).reshape(n, P, -1)

    arrays = {
        "x_in": a["attn_x"],
        "w_attn": np.concatenate([head_major(a["attn_W_Q"]), head_major(a["attn_W_K"]), head_major(a["attn_W_V"]),
                                  a["attn_W_O"].T.reshape(H, P, D)], axis=2),
        "w_mod": a["wmod"],
        "c_T": a["c"].T.reshape(DC, P, -1).transpose(1, 0, 2),
        "w_router": a["ffn_Wg"].reshape(DC, P, E).transpose(1, 0, 2),
        "b_router": a["ffn_bg"].reshape(E, 1),
        "w_routed": np.concatenate([chunked(a["ffn_Wgate"]), chunked(a["ffn_Wdown"]), chunked(a["ffn_Wup"]),
                                    np.stack([a["ffn_bgate"], a["ffn_bup"]], 1).reshape(NR, 2 * HC, P)
                                    .transpose(0, 2, 1)], axis=2),
        "w_shared_up": chunked(a["ffn_Ws_up"].reshape(D, NSH, HID).transpose(1, 0, 2)),
        "w_shared_down": chunked(a["ffn_Ws_down"].reshape(NSH, HID, D)),
        "b_shared_up": a["ffn_bs_up"].reshape(NSH, HC, P).transpose(2, 0, 1),
        "b_down": np.concatenate([a["ffn_bs_down"][None], a["ffn_bdown"]]),
    }
    arrays = {k: np.ascontiguousarray(v) for k, v in arrays.items()}
    nc = bacc.Bacc("TRN2", target_bir_lowering=False, num_devices=1)
    args = [nc.dram_tensor(k, v.shape, mybir.dt.from_np(v.dtype), kind="ExternalInput").ap()
            for k, v in arrays.items()]
    out = nc.dram_tensor("out", arrays["x_in"].shape, F32, kind="ExternalOutput").ap()
    block_kernel(nc, *args, out)
    return run(nc, [arrays], core_ids=[0]).results[0]["out"]
```
